# Optimizing a Trainium2 kernel written in Bass

```python
import numpy as np
import jax
import jax.numpy as jnp

def _softmax(x, axis=-1):
    return jax.nn.softmax(x, axis=axis)

def _gelu(x):
    return jax.nn.gelu(x, approximate=True)

def _silu(x):
    return jax.nn.silu(x)

def _sigmoid(x):
    return jax.nn.sigmoid(x)

def _layernorm(x, axis=-1, eps=1e-05):
    m = jnp.mean(x, axis=axis, keepdims=True)
    v = jnp.var(x, axis=axis, keepdims=True)
    return (x - m) / jnp.sqrt(v + eps)

def _scatter_add(tgt, idx, src, axis=0):
    return tgt.at[idx].add(src)

def _segment_sum(src, seg, n):
    return jax.ops.segment_sum(src, seg, n)
kernel_name = 'mk_hybrid_d4_jaxref_r8_7088c0'

def setup_inputs(seed: int=0):
    np.random.seed(seed)
    _w = jnp.asarray

    def _L0_attn_a_setup():
        import jax, jax.numpy as jnp
        import numpy as np
        N_HEAD = 16
        LATENT = 32

        def _rotate_half(x):
            xe = x[..., ::2]
            xo = x[..., 1::2]
            return jnp.stack((-xo, xe), axis=-1).reshape(x.shape)

        def _rope_tables(T, latent_dim, dtype):
            inv_freq = 1.0 / 10000.0 ** (jnp.arange(0, latent_dim, 2, dtype=jnp.float32) / latent_dim)
            t = jnp.arange(T, dtype=jnp.float32)
            freqs = jnp.outer(t, inv_freq)
            cos = jnp.repeat(jnp.cos(freqs), 2, axis=-1)[:, :latent_dim]
            sin = jnp.repeat(jnp.sin(freqs), 2, axis=-1)[:, :latent_dim]
            return (cos.astype(dtype), sin.astype(dtype))
        key = jax.random.key(seed)
        ks = jax.random.split(key, 14)
        C = 128
        hd = C // N_HEAD
        L = LATENT
        s = 0.02
        return {'x': jax.random.normal(ks[0], (4, 256, C), jnp.float32), 'c_attn_w': jax.random.normal(ks[1], (3 * C, C), jnp.float32) * s, 'c_attn_b': jnp.zeros((3 * C,), jnp.float32), 'q2l_w': jax.random.normal(ks[2], (L, hd), jnp.float32) * s, 'q2l_b': jnp.zeros((L,), jnp.float32), 'kv2l_w': jax.random.normal(ks[3], (L, hd), jnp.float32) * s, 'kv2l_b': jnp.zeros((L,), jnp.float32), 'l2o_w': jax.random.normal(ks[4], (hd, L), jnp.float32) * s, 'l2o_b': jnp.zeros((hd,), jnp.float32), 'wqk_w': jax.random.normal(ks[5], (L, L), jnp.float32) * s, 'wqk_b': jnp.zeros((L,), jnp.float32), 'cproj_w': jax.random.normal(ks[6], (C, C), jnp.float32) * s, 'cproj_b': jnp.zeros((C,), jnp.float32)}
    _L0_attn_a_in = _L0_attn_a_setup()

    def _L0_attn_b_setup():
        import jax, jax.numpy as jnp
        import numpy as np
        DIM = 128
        B, S = (8, 256)
        LN_EPS = 1e-05
        key = jax.random.key(seed)
        k1, k2, k3 = jax.random.split(key, 3)
        x = jax.random.normal(k1, (B, S, DIM), dtype=jnp.float32)
        w_qkv = jax.random.normal(k2, (3 * DIM, DIM), dtype=jnp.float32) * np.sqrt(2.0 / (DIM + 3 * DIM))
        w_fc = jax.random.normal(k3, (DIM, DIM), dtype=jnp.float32) * np.sqrt(2.0 / (DIM + DIM))
        b_fc = jnp.zeros((DIM,), dtype=jnp.float32)
        gamma = jnp.ones((DIM,), dtype=jnp.float32)
        beta = jnp.zeros((DIM,), dtype=jnp.float32)
        return {'x': x, 'w_qkv': w_qkv, 'w_fc': w_fc, 'b_fc': b_fc, 'gamma': gamma, 'beta': beta}
    _L0_attn_b_in = _L0_attn_b_setup()

    def _L0_ffn_setup():
        import jax, jax.numpy as jnp
        import numpy as np
        B, T, C = (4, 256, 128)
        E = 8
        K = 2
        H = 176
        HS = 176 * 2
        key = jax.random.key(seed)
        k = jax.random.split(key, 8)
        s = 0.02
        return {'x': jax.random.normal(k[0], (B, T, C), jnp.float32), 'Wg': jax.random.normal(k[1], (C, E), jnp.float32) * s, 'W1': jax.random.normal(k[2], (E, C, H), jnp.float32) * s, 'W2': jax.random.normal(k[3], (E, C, H), jnp.float32) * s, 'W3': jax.random.normal(k[4], (E, H, C), jnp.float32) * s, 'Ws1': jax.random.normal(k[5], (C, HS), jnp.float32) * s, 'Ws2': jax.random.normal(k[6], (C, HS), jnp.float32) * s, 'Ws3': jax.random.normal(k[7], (HS, C), jnp.float32) * s}
    _L0_ffn_in = _L0_ffn_setup()

    def _L1_attn_a_setup():
        import jax, jax.numpy as jnp
        import numpy as np
        EPS = 0.0001
        key = jax.random.key(seed)
        ks = jax.random.split(key, 6)
        B, T, DIM, H, S = (8, 256, 128, 16, 64)
        D = DIM // H
        tokens = jax.random.normal(ks[0], (B, T, DIM), dtype=jnp.float32)
        norm_w = jnp.ones((DIM,), dtype=jnp.float32)
        a = jnp.tile(jnp.eye(S, dtype=jnp.float32)[None], (H, 1, 1))
        b = jax.random.normal(ks[1], (H, D, S), dtype=jnp.float32) * 0.02
        c = jax.random.normal(ks[2], (H, S, D), dtype=jnp.float32) * 0.02
        skip = jnp.ones((H, D), dtype=jnp.float32)
        w_out = jax.random.normal(ks[3], (DIM, DIM), dtype=jnp.float32) * (1.0 / np.sqrt(DIM))
        b_out = jnp.zeros((DIM,), dtype=jnp.float32)
        return {'tokens': tokens, 'norm_w': norm_w, 'a': a, 'b': b, 'c': c, 'skip': skip, 'w_out': w_out, 'b_out': b_out}
    _L1_attn_a_in = _L1_attn_a_setup()

    def _L1_attn_b_setup():
        import jax, jax.numpy as jnp
        import numpy as np
        N_EMBD = 128
        N_HEAD = 16
        HEAD_SIZE = N_EMBD // N_HEAD
        B, T = (8, 512)
        EPS = 0.001
        key = jax.random.key(seed)
        k1, k2, k3 = jax.random.split(key, 3)
        x = jax.random.normal(k1, (B, T, N_EMBD), dtype=jnp.float32)
        Wqkv = jax.random.normal(k2, (3 * N_EMBD, N_EMBD), dtype=jnp.float32) * 0.02
        bqkv = jnp.zeros((3 * N_EMBD,), dtype=jnp.float32)
        Wproj = jax.random.normal(k3, (N_EMBD, N_EMBD), dtype=jnp.float32) * 0.02
        bproj = jnp.zeros((N_EMBD,), dtype=jnp.float32)
        scale = jnp.asarray(1.0 / np.sqrt(HEAD_SIZE), dtype=jnp.float32)
        return {'x': x, 'Wqkv': Wqkv, 'bqkv': bqkv, 'Wproj': Wproj, 'bproj': bproj, 'scale': scale}
    _L1_attn_b_in = _L1_attn_b_setup()

    def _L1_ffn_setup():
        import jax, jax.numpy as jnp
        import numpy as np
        B, S, H = (1, 256, 128)
        E, K = (16, 4)
        G, TG = (4, 2)
        I_MOE = 64
        N_SH = 2
        SCALE = 2.5

        def _mlp(x, gw, uw, dw):
            return jax.nn.silu(x @ gw.T) * (x @ uw.T) @ dw.T

        def _route(x2d, router_weight, e_bias):
            T = x2d.shape[0]
            scores = jax.nn.sigmoid(x2d @ router_weight.T)
            sc = scores + e_bias[None, :]
            group_scores = jnp.sum(jax.lax.top_k(sc.reshape(T, G, E // G), 2)[0], axis=-1)
            _, gidx = jax.lax.top_k(group_scores, TG)
            gmask = jnp.zeros((T, G), sc.dtype).at[jnp.arange(T)[:, None], gidx].set(1.0)
            smask = jnp.repeat(gmask, E // G, axis=1)
            masked = jnp.where(smask > 0, sc, 0.0)
            _, tidx = jax.lax.top_k(masked, K)
            tw = jnp.take_along_axis(scores, tidx, axis=1)
            tw = tw / (jnp.sum(tw, axis=-1, keepdims=True) + 1e-20)
            tw = tw * SCALE
            return (tidx, tw)

        def _moe_forward(hidden_states, router_weight, e_bias, gate_w, up_w, down_w, sh_gate_w, sh_up_w, sh_down_w):
            orig_shape = hidden_states.shape
            x = hidden_states.reshape(-1, H)
            T = x.shape[0]
            tidx, tw = _route(x, router_weight, e_bias)
            g = jnp.einsum('th,eih->tei', x, gate_w)
            u = jnp.einsum('th,eih->tei', x, up_w)
            h = jax.nn.silu(g) * u
            yo = jnp.einsum('tei,ehi->teh', h, down_w)
            combine = jnp.zeros((T, E), tw.dtype).at[jnp.arange(T)[:, None], tidx].add(tw)
            routed = jnp.einsum('te,teh->th', combine, yo)
            shared = _mlp(hidden_states.reshape(-1, H), sh_gate_w, sh_up_w, sh_down_w)
            return (routed + shared).reshape(orig_shape)
        key = jax.random.key(seed)
        ks = jax.random.split(key, 9)
        s = 0.02
        return {'hidden_states': jax.random.normal(ks[0], (B, S, H), jnp.float32), 'router_weight': jax.random.normal(ks[1], (E, H), jnp.float32) * s, 'e_bias': jnp.zeros((E,), jnp.float32), 'gate_w': jax.random.normal(ks[2], (E, I_MOE, H), jnp.float32) * s, 'up_w': jax.random.normal(ks[3], (E, I_MOE, H), jnp.float32) * s, 'down_w': jax.random.normal(ks[4], (E, H, I_MOE), jnp.float32) * s, 'sh_gate_w': jax.random.normal(ks[5], (N_SH * I_MOE, H), jnp.float32) * s, 'sh_up_w': jax.random.normal(ks[6], (N_SH * I_MOE, H), jnp.float32) * s, 'sh_down_w': jax.random.normal(ks[7], (H, N_SH * I_MOE), jnp.float32) * s}
    _L1_ffn_in = _L1_ffn_setup()

    def _L2_attn_a_setup():
        import jax, jax.numpy as jnp
        import numpy as np
        D_MODEL, D_INNER, D_STATE, D_CONV, DT_RANK = (128, 256, 16, 4, 64)
        BATCH, SEQLEN = (4, 256)

        def _silu(x):
            return x * jax.nn.sigmoid(x)

        def _mamba_forward(hidden_states, in_proj_w, conv_w, conv_b, x_proj_w, dt_proj_w, dt_proj_b, A_log, D, out_proj_w):
            B, L, _ = hidden_states.shape
            d_inner, d_conv = conv_w.shape
            d_state = A_log.shape[1]
            dt_rank = dt_proj_w.shape[1]
            xz = jnp.einsum('bld,ed->ble', hidden_states, in_proj_w)
            x, z = (xz[..., :d_inner], xz[..., d_inner:])
            x_pad = jnp.pad(x, ((0, 0), (d_conv - 1, 0), (0, 0)))
            x_conv = sum((x_pad[:, w:w + L, :] * conv_w[:, w] for w in range(d_conv))) + conv_b
            x_conv = _silu(x_conv)
            x_dbl = jnp.einsum('bld,ed->ble', x_conv, x_proj_w)
            dt_in = x_dbl[..., :dt_rank]
            Bv = x_dbl[..., dt_rank:dt_rank + d_state]
            Cv = x_dbl[..., dt_rank + d_state:]
            delta = jax.nn.softplus(jnp.einsum('blr,dr->bld', dt_in, dt_proj_w) + dt_proj_b)
            A = -jnp.exp(A_log)

            def step(h, inp):
                d_t, B_t, C_t, u_t = inp
                dA = jnp.exp(d_t[:, :, None] * A)
                h = h * dA + (d_t * u_t)[:, :, None] * B_t[:, None, :]
                y = jnp.einsum('bdn,bn->bd', h, C_t)
                return (h, y)
            h0 = jnp.zeros((B, d_inner, d_state), dtype=hidden_states.dtype)
            xs = (jnp.swapaxes(delta, 0, 1), jnp.swapaxes(Bv, 0, 1), jnp.swapaxes(Cv, 0, 1), jnp.swapaxes(x_conv, 0, 1))
            _, ys = jax.lax.scan(step, h0, xs)
            y = jnp.swapaxes(ys, 0, 1) + x_conv * D
            y = y * _silu(z)
            return jnp.einsum('bld,md->blm', y, out_proj_w)
        key = jax.random.key(seed)
        ks = jax.random.split(key, 10)

        def n(k, shape, scale=1.0):
            return jax.random.normal(k, shape, dtype=jnp.float32) * scale
        A_log = jnp.log(jax.random.uniform(ks[7], (D_INNER, D_STATE), dtype=jnp.float32, minval=0.5, maxval=float(D_STATE)))
        return {'hidden_states': n(ks[0], (BATCH, SEQLEN, D_MODEL)), 'in_proj_w': n(ks[1], (2 * D_INNER, D_MODEL), D_MODEL ** (-0.5)), 'conv_w': n(ks[2], (D_INNER, D_CONV), D_CONV ** (-0.5)), 'conv_b': n(ks[3], (D_INNER,), 0.1), 'x_proj_w': n(ks[4], (DT_RANK + 2 * D_STATE, D_INNER), D_INNER ** (-0.5)), 'dt_proj_w': n(ks[5], (D_INNER, DT_RANK), DT_RANK ** (-0.5)), 'dt_proj_b': n(ks[6], (D_INNER,), 0.5), 'A_log': A_log, 'D': jnp.ones((D_INNER,), dtype=jnp.float32), 'out_proj_w': n(ks[8], (D_MODEL, D_INNER), D_INNER ** (-0.5))}
    _L2_attn_a_in = _L2_attn_a_setup()

    def _L2_attn_b_setup():
        import jax, jax.numpy as jnp
        import numpy as np
        import math
        D_MODEL = 128
        EXPAND = 2
        D_INNER = EXPAND * D_MODEL
        D_STATE = 16
        D_CONV = 4
        DT_RANK = math.ceil(D_MODEL / 16)
        BATCH = 1
        SEQLEN = 256

        def _silu(x):
            return x * jax.nn.sigmoid(x)

        def _selective_scan(u, delta, A, B, C, D, z, delta_bias):
            delta = jax.nn.softplus(delta + delta_bias[None, :, None])
            dA = jnp.exp(jnp.einsum('bdl,dn->lbdn', delta, A))
            dBu = jnp.einsum('bdl,bnl->lbdn', delta * u, B)
            Ct = jnp.transpose(C, (2, 0, 1))

            def step(h, inp):
                dA_t, dBu_t, C_t = inp
                h = dA_t * h + dBu_t
                y = jnp.einsum('bdn,bn->bd', h, C_t)
                return (h, y)
            h0 = jnp.zeros((u.shape[0], u.shape[1], A.shape[1]), dtype=u.dtype)
            _, ys = jax.lax.scan(step, h0, (dA, dBu, Ct))
            y = jnp.transpose(ys, (1, 2, 0))
            y = y + D[:, None] * u
            return y * _silu(z)

        def _causal_conv1d(x, conv_w, conv_b):
            x_pad = jnp.pad(x, ((0, 0), (0, 0), (D_CONV - 1, 0)))
            kernel = conv_w[:, None, :]
            y = jax.lax.conv_general_dilated(x_pad, kernel, window_strides=(1,), padding='VALID', dimension_numbers=('NCH', 'OIH', 'NCH'), feature_group_count=D_INNER)
            return y + conv_b[None, :, None]
        key = jax.random.key(seed)
        ks = jax.random.split(key, 12)
        hidden_states = jax.random.normal(ks[0], (BATCH, SEQLEN, D_MODEL), dtype=jnp.float32)
        in_proj_w = jax.random.normal(ks[1], (2 * D_INNER, D_MODEL), dtype=jnp.float32) * D_MODEL ** (-0.5)
        conv_w = jax.random.normal(ks[2], (D_INNER, D_CONV), dtype=jnp.float32) * D_CONV ** (-0.5)
        conv_b = jnp.zeros((D_INNER,), dtype=jnp.float32)
        dt_std = DT_RANK ** (-0.5)

        def dt_bias(k):
            dt = jnp.exp(jax.random.uniform(k, (D_INNER,)) * (math.log(0.1) - math.log(0.001)) + math.log(0.001))
            dt = jnp.clip(dt, 0.0001, None)
            return dt + jnp.log(-jnp.expm1(-dt))
        A_log = jnp.log(jnp.broadcast_to(jnp.arange(1, D_STATE + 1, dtype=jnp.float32), (D_INNER, D_STATE)))
        x1_proj_w = jax.random.normal(ks[3], (DT_RANK + 2 * D_STATE, D_INNER), dtype=jnp.float32) * D_INNER ** (-0.5)
        dt1_proj_w = jax.random.uniform(ks[4], (D_INNER, DT_RANK), minval=-dt_std, maxval=dt_std)
        dt1_proj_b = dt_bias(ks[5])
        x2_proj_w = jax.random.normal(ks[6], (DT_RANK + 2 * D_STATE, D_INNER), dtype=jnp.float32) * D_INNER ** (-0.5)
        dt2_proj_w = jax.random.uniform(ks[7], (D_INNER, DT_RANK), minval=-dt_std, maxval=dt_std)
        dt2_proj_b = dt_bias(ks[8])
        out_proj_w = jax.random.normal(ks[9], (D_MODEL, D_INNER), dtype=jnp.float32) * D_INNER ** (-0.5)
        return {'hidden_states': hidden_states, 'in_proj_w': in_proj_w, 'conv_w': conv_w, 'conv_b': conv_b, 'x1_proj_w': x1_proj_w, 'dt1_proj_w': dt1_proj_w, 'dt1_proj_b': dt1_proj_b, 'A1_log': A_log, 'D1': jnp.ones((D_INNER,), dtype=jnp.float32), 'x2_proj_w': x2_proj_w, 'dt2_proj_w': dt2_proj_w, 'dt2_proj_b': dt2_proj_b, 'A2_log': A_log, 'D2': jnp.ones((D_INNER,), dtype=jnp.float32), 'out_proj_w': out_proj_w}
    _L2_attn_b_in = _L2_attn_b_setup()

    def _L2_ffn_setup():
        import jax, jax.numpy as jnp
        import numpy as np
        D_IN, D_HID = (128, 512)

        def _ternary(key, shape):
            return jax.random.randint(key, shape, -1, 2).astype(jnp.float32)

        def _tlin(x, w, s):
            return jnp.einsum('bsi,oi->bso', x, w) * s
        key = jax.random.key(seed)
        ks = jax.random.split(key, 12)
        inv = lambda fan: 1.0 / np.sqrt(fan).astype(np.float32)
        return {'x': jax.random.normal(ks[0], (4, 256, D_IN), dtype=jnp.float32), 'w1_w': _ternary(ks[1], (D_HID, D_IN)), 'w1_s': jax.random.uniform(ks[2], (D_HID,), dtype=jnp.float32) * inv(D_IN), 'w2_w': _ternary(ks[3], (D_HID, D_IN)), 'w2_s': jax.random.uniform(ks[4], (D_HID,), dtype=jnp.float32) * inv(D_IN), 'h1_w': _ternary(ks[5], (D_HID, D_HID)), 'h1_s': jax.random.uniform(ks[6], (D_HID,), dtype=jnp.float32) * inv(D_HID), 'h2_w': _ternary(ks[7], (D_HID, D_HID)), 'h2_s': jax.random.uniform(ks[8], (D_HID,), dtype=jnp.float32) * inv(D_HID), 'w3_w': _ternary(ks[9], (D_IN, D_HID)), 'w3_s': jax.random.uniform(ks[10], (D_IN,), dtype=jnp.float32) * inv(D_HID)}
    _L2_ffn_in = _L2_ffn_setup()

    def _L3_attn_a_setup():
        import jax, jax.numpy as jnp
        import numpy as np
        from jax import lax
        B, T, D = (4, 512, 128)
        H, d = (4, 64)
        EPS = 1e-06

        def pos_unit(x):
            p = jax.nn.elu(x) + 1.0
            return p / (jnp.linalg.norm(p, axis=-1, keepdims=True) + EPS)

        def _reference_tuple_inner(x, Wq, Wk, Wv, Wo):
            Bx, Tx, Dx = x.shape
            q = (x @ Wq.T).reshape(Bx, Tx, H, d)
            k = (x @ Wk.T).reshape(Bx, Tx, H, d)
            v = (x @ Wv.T).reshape(Bx, Tx, H, d)
            q = pos_unit(q)
            k = pos_unit(k)
            qT = jnp.transpose(q, (1, 0, 2, 3))
            kT = jnp.transpose(k, (1, 0, 2, 3))
            vT = jnp.transpose(v, (1, 0, 2, 3))
            kv0 = jnp.zeros((Bx, H, d, d), dtype=x.dtype)
            kc0 = jnp.zeros((Bx, H, d), dtype=x.dtype)

            def step(carry, inp):
                kv_cum, k_cum = carry
                qt, kt, vt = inp
                kv_cum = kv_cum + jnp.einsum('bhd,bhj->bhjd', kt, vt)
                k_cum = k_cum + kt
                num = jnp.einsum('bhd,bhjd->bhj', qt, kv_cum)
                den = jnp.einsum('bhd,bhd->bh', qt, k_cum)[..., None] + EPS
                return ((kv_cum, k_cum), num / den)
            (kv_f, kc_f), yT = lax.scan(step, (kv0, kc0), (qT, kT, vT))
            y = jnp.transpose(yT, (1, 0, 2, 3)).reshape(Bx, Tx, H * d)
            y = y @ Wo.T
            return (y, kv_f, kc_f)
        key = jax.random.key(seed)
        ks = jax.random.split(key, 5)
        s_in = 1.0 / np.sqrt(D)
        s_hd = 1.0 / np.sqrt(H * d)
        return {'x': jax.random.normal(ks[0], (B, T, D), dtype=jnp.float32), 'Wq': jax.random.normal(ks[1], (H * d, D), dtype=jnp.float32) * s_in, 'Wk': jax.random.normal(ks[2], (H * d, D), dtype=jnp.float32) * s_in, 'Wv': jax.random.normal(ks[3], (H * d, D), dtype=jnp.float32) * s_in, 'Wo': jax.random.normal(ks[4], (D, H * d), dtype=jnp.float32) * s_hd}
    _L3_attn_a_in = _L3_attn_a_setup()

    def _L3_attn_b_setup():
        import jax, jax.numpy as jnp
        import numpy as np
        DIM = 128
        B, S = (4, 512)
        key = jax.random.key(seed)
        ks = jax.random.split(key, 8)
        scale = 1.0 / np.sqrt(DIM)
        x = jax.random.normal(ks[0], (B, S, DIM), dtype=jnp.float32)
        Wk = jax.random.normal(ks[1], (DIM, DIM), dtype=jnp.float32) * scale
        Wv = jax.random.normal(ks[2], (DIM, DIM), dtype=jnp.float32) * scale
        Wr = jax.random.normal(ks[3], (DIM, DIM), dtype=jnp.float32) * scale
        Wo = jax.random.normal(ks[4], (DIM, DIM), dtype=jnp.float32) * scale
        time_decay = jax.random.normal(ks[5], (DIM,), dtype=jnp.float32) * 0.01 - 5.0
        time_first = jax.random.normal(ks[6], (DIM,), dtype=jnp.float32) * 0.01
        return {'x': x, 'Wk': Wk, 'Wv': Wv, 'Wr': Wr, 'Wo': Wo, 'time_decay': time_decay, 'time_first': time_first}
    _L3_attn_b_in = _L3_attn_b_setup()

    def _L3_ffn_setup():
        import jax, jax.numpy as jnp
        import numpy as np
        T, Z, D_DIM = (8, 256, 128)
        N_EXP, P_SLOT, H = (64, 32, 128)
        LN_EPS = 1e-05
        key = jax.random.key(seed)
        k = jax.random.split(key, 5)
        s = 0.02
        return {'x': jax.random.normal(k[0], (T, Z, D_DIM), dtype=jnp.float32), 'phi_w': jax.random.normal(k[1], (N_EXP * P_SLOT, D_DIM), dtype=jnp.float32) * s, 'phi_b': jax.random.normal(k[2], (N_EXP * P_SLOT,), dtype=jnp.float32) * s, 'expert_w': jax.random.normal(k[3], (N_EXP, D_DIM, H), dtype=jnp.float32) * s, 'expert_b': jax.random.normal(k[4], (N_EXP, H), dtype=jnp.float32) * s}
    _L3_ffn_in = _L3_ffn_setup()
    _d = {'L0_attn_a_x': _L0_attn_a_in['x'], 'L0_attn_a_c_attn_w': _L0_attn_a_in['c_attn_w'], 'L0_attn_a_c_attn_b': _L0_attn_a_in['c_attn_b'], 'L0_attn_a_q2l_w': _L0_attn_a_in['q2l_w'], 'L0_attn_a_q2l_b': _L0_attn_a_in['q2l_b'], 'L0_attn_a_kv2l_w': _L0_attn_a_in['kv2l_w'], 'L0_attn_a_kv2l_b': _L0_attn_a_in['kv2l_b'], 'L0_attn_a_l2o_w': _L0_attn_a_in['l2o_w'], 'L0_attn_a_l2o_b': _L0_attn_a_in['l2o_b'], 'L0_attn_a_wqk_w': _L0_attn_a_in['wqk_w'], 'L0_attn_a_wqk_b': _L0_attn_a_in['wqk_b'], 'L0_attn_a_cproj_w': _L0_attn_a_in['cproj_w'], 'L0_attn_a_cproj_b': _L0_attn_a_in['cproj_b'], 'L0_attn_b_w_qkv': _L0_attn_b_in['w_qkv'], 'L0_attn_b_w_fc': _L0_attn_b_in['w_fc'], 'L0_attn_b_b_fc': _L0_attn_b_in['b_fc'], 'L0_attn_b_gamma': _L0_attn_b_in['gamma'], 'L0_attn_b_beta': _L0_attn_b_in['beta'], 'L0_ffn_Wg': _L0_ffn_in['Wg'], 'L0_ffn_W1': _L0_ffn_in['W1'], 'L0_ffn_W2': _L0_ffn_in['W2'], 'L0_ffn_W3': _L0_ffn_in['W3'], 'L0_ffn_Ws1': _L0_ffn_in['Ws1'], 'L0_ffn_Ws2': _L0_ffn_in['Ws2'], 'L0_ffn_Ws3': _L0_ffn_in['Ws3'], 'L1_attn_a_norm_w': _L1_attn_a_in['norm_w'], 'L1_attn_a_a': _L1_attn_a_in['a'], 'L1_attn_a_b': _L1_attn_a_in['b'], 'L1_attn_a_c': _L1_attn_a_in['c'], 'L1_attn_a_skip': _L1_attn_a_in['skip'], 'L1_attn_a_w_out': _L1_attn_a_in['w_out'], 'L1_attn_a_b_out': _L1_attn_a_in['b_out'], 'L1_attn_b_Wqkv': _L1_attn_b_in['Wqkv'], 'L1_attn_b_bqkv': _L1_attn_b_in['bqkv'], 'L1_attn_b_Wproj': _L1_attn_b_in['Wproj'], 'L1_attn_b_bproj': _L1_attn_b_in['bproj'], 'L1_attn_b_scale': _L1_attn_b_in['scale'], 'L1_ffn_router_weight': _L1_ffn_in['router_weight'], 'L1_ffn_e_bias': _L1_ffn_in['e_bias'], 'L1_ffn_gate_w': _L1_ffn_in['gate_w'], 'L1_ffn_up_w': _L1_ffn_in['up_w'], 'L1_ffn_down_w': _L1_ffn_in['down_w'], 'L1_ffn_sh_gate_w': _L1_ffn_in['sh_gate_w'], 'L1_ffn_sh_up_w': _L1_ffn_in['sh_up_w'], 'L1_ffn_sh_down_w': _L1_ffn_in['sh_down_w'], 'L2_attn_a_in_proj_w': _L2_attn_a_in['in_proj_w'], 'L2_attn_a_conv_w': _L2_attn_a_in['conv_w'], 'L2_attn_a_conv_b': _L2_attn_a_in['conv_b'], 'L2_attn_a_x_proj_w': _L2_attn_a_in['x_proj_w'], 'L2_attn_a_dt_proj_w': _L2_attn_a_in['dt_proj_w'], 'L2_attn_a_dt_proj_b': _L2_attn_a_in['dt_proj_b'], 'L2_attn_a_A_log': _L2_attn_a_in['A_log'], 'L2_attn_a_D': _L2_attn_a_in['D'], 'L2_attn_a_out_proj_w': _L2_attn_a_in['out_proj_w'], 'L2_attn_b_in_proj_w': _L2_attn_b_in['in_proj_w'], 'L2_attn_b_conv_w': _L2_attn_b_in['conv_w'], 'L2_attn_b_conv_b': _L2_attn_b_in['conv_b'], 'L2_attn_b_x1_proj_w': _L2_attn_b_in['x1_proj_w'], 'L2_attn_b_dt1_proj_w': _L2_attn_b_in['dt1_proj_w'], 'L2_attn_b_dt1_proj_b': _L2_attn_b_in['dt1_proj_b'], 'L2_attn_b_A1_log': _L2_attn_b_in['A1_log'], 'L2_attn_b_D1': _L2_attn_b_in['D1'], 'L2_attn_b_x2_proj_w': _L2_attn_b_in['x2_proj_w'], 'L2_attn_b_dt2_proj_w': _L2_attn_b_in['dt2_proj_w'], 'L2_attn_b_dt2_proj_b': _L2_attn_b_in['dt2_proj_b'], 'L2_attn_b_A2_log': _L2_attn_b_in['A2_log'], 'L2_attn_b_D2': _L2_attn_b_in['D2'], 'L2_attn_b_out_proj_w': _L2_attn_b_in['out_proj_w'], 'L2_ffn_w1_w': _L2_ffn_in['w1_w'], 'L2_ffn_w1_s': _L2_ffn_in['w1_s'], 'L2_ffn_w2_w': _L2_ffn_in['w2_w'], 'L2_ffn_w2_s': _L2_ffn_in['w2_s'], 'L2_ffn_h1_w': _L2_ffn_in['h1_w'], 'L2_ffn_h1_s': _L2_ffn_in['h1_s'], 'L2_ffn_h2_w': _L2_ffn_in['h2_w'], 'L2_ffn_h2_s': _L2_ffn_in['h2_s'], 'L2_ffn_w3_w': _L2_ffn_in['w3_w'], 'L2_ffn_w3_s': _L2_ffn_in['w3_s'], 'L3_attn_a_Wq': _L3_attn_a_in['Wq'], 'L3_attn_a_Wk': _L3_attn_a_in['Wk'], 'L3_attn_a_Wv': _L3_attn_a_in['Wv'], 'L3_attn_a_Wo': _L3_attn_a_in['Wo'], 'L3_attn_b_Wk': _L3_attn_b_in['Wk'], 'L3_attn_b_Wv': _L3_attn_b_in['Wv'], 'L3_attn_b_Wr': _L3_attn_b_in['Wr'], 'L3_attn_b_Wo': _L3_attn_b_in['Wo'], 'L3_attn_b_time_decay': _L3_attn_b_in['time_decay'], 'L3_attn_b_time_first': _L3_attn_b_in['time_first'], 'L3_ffn_phi_w': _L3_ffn_in['phi_w'], 'L3_ffn_phi_b': _L3_ffn_in['phi_b'], 'L3_ffn_expert_w': _L3_ffn_in['expert_w'], 'L3_ffn_expert_b': _L3_ffn_in['expert_b']}
    _x0 = _d['L0_attn_a_x']
    _d['L0_attn_a_x'] = jax.random.normal(jax.random.fold_in(jax.random.key(seed), 1), (4, 512, 128), dtype=_x0.dtype)
    del _x0
    return _d

def reference(L0_attn_a_x, L0_attn_a_c_attn_w, L0_attn_a_c_attn_b, L0_attn_a_q2l_w, L0_attn_a_q2l_b, L0_attn_a_kv2l_w, L0_attn_a_kv2l_b, L0_attn_a_l2o_w, L0_attn_a_l2o_b, L0_attn_a_wqk_w, L0_attn_a_wqk_b, L0_attn_a_cproj_w, L0_attn_a_cproj_b, L0_attn_b_w_qkv, L0_attn_b_w_fc, L0_attn_b_b_fc, L0_attn_b_gamma, L0_attn_b_beta, L0_ffn_Wg, L0_ffn_W1, L0_ffn_W2, L0_ffn_W3, L0_ffn_Ws1, L0_ffn_Ws2, L0_ffn_Ws3, L1_attn_a_norm_w, L1_attn_a_a, L1_attn_a_b, L1_attn_a_c, L1_attn_a_skip, L1_attn_a_w_out, L1_attn_a_b_out, L1_attn_b_Wqkv, L1_attn_b_bqkv, L1_attn_b_Wproj, L1_attn_b_bproj, L1_attn_b_scale, L1_ffn_router_weight, L1_ffn_e_bias, L1_ffn_gate_w, L1_ffn_up_w, L1_ffn_down_w, L1_ffn_sh_gate_w, L1_ffn_sh_up_w, L1_ffn_sh_down_w, L2_attn_a_in_proj_w, L2_attn_a_conv_w, L2_attn_a_conv_b, L2_attn_a_x_proj_w, L2_attn_a_dt_proj_w, L2_attn_a_dt_proj_b, L2_attn_a_A_log, L2_attn_a_D, L2_attn_a_out_proj_w, L2_attn_b_in_proj_w, L2_attn_b_conv_w, L2_attn_b_conv_b, L2_attn_b_x1_proj_w, L2_attn_b_dt1_proj_w, L2_attn_b_dt1_proj_b, L2_attn_b_A1_log, L2_attn_b_D1, L2_attn_b_x2_proj_w, L2_attn_b_dt2_proj_w, L2_attn_b_dt2_proj_b, L2_attn_b_A2_log, L2_attn_b_D2, L2_attn_b_out_proj_w, L2_ffn_w1_w, L2_ffn_w1_s, L2_ffn_w2_w, L2_ffn_w2_s, L2_ffn_h1_w, L2_ffn_h1_s, L2_ffn_h2_w, L2_ffn_h2_s, L2_ffn_w3_w, L2_ffn_w3_s, L3_attn_a_Wq, L3_attn_a_Wk, L3_attn_a_Wv, L3_attn_a_Wo, L3_attn_b_Wk, L3_attn_b_Wv, L3_attn_b_Wr, L3_attn_b_Wo, L3_attn_b_time_decay, L3_attn_b_time_first, L3_ffn_phi_w, L3_ffn_phi_b, L3_ffn_expert_w, L3_ffn_expert_b):

    def _L0_attn_a_ref(x, c_attn_w, c_attn_b, q2l_w, q2l_b, kv2l_w, kv2l_b, l2o_w, l2o_b, wqk_w, wqk_b, cproj_w, cproj_b):
        import jax, jax.numpy as jnp
        import numpy as np
        N_HEAD = 16
        LATENT = 32

        def _rotate_half(x):
            xe = x[..., ::2]
            xo = x[..., 1::2]
            return jnp.stack((-xo, xe), axis=-1).reshape(x.shape)

        def _rope_tables(T, latent_dim, dtype):
            inv_freq = 1.0 / 10000.0 ** (jnp.arange(0, latent_dim, 2, dtype=jnp.float32) / latent_dim)
            t = jnp.arange(T, dtype=jnp.float32)
            freqs = jnp.outer(t, inv_freq)
            cos = jnp.repeat(jnp.cos(freqs), 2, axis=-1)[:, :latent_dim]
            sin = jnp.repeat(jnp.sin(freqs), 2, axis=-1)[:, :latent_dim]
            return (cos.astype(dtype), sin.astype(dtype))
        B, T, C = x.shape
        H = N_HEAD
        hd = C // H
        L = q2l_w.shape[0]
        qkv = x @ c_attn_w.T + c_attn_b
        q, k, v = jnp.split(qkv, 3, axis=2)

        def heads(t):
            return t.reshape(B, T, H, hd).transpose(0, 2, 1, 3)
        q, k, v = (heads(q), heads(k), heads(v))
        q_lat = q @ q2l_w.T + q2l_b
        k_lat = k @ kv2l_w.T + kv2l_b
        v_lat = v @ kv2l_w.T + kv2l_b
        cos, sin = _rope_tables(T, L, x.dtype)
        cos = cos[None, None]
        sin = sin[None, None]
        q_lat = q_lat * cos + _rotate_half(q_lat) * sin
        k_lat = k_lat * cos + _rotate_half(k_lat) * sin
        q_for_k = q_lat @ wqk_w.T + wqk_b
        att = jnp.einsum('bhql,bhkl->bhqk', q_for_k, k_lat) * L ** (-0.5)
        causal = jnp.tril(jnp.ones((T, T), dtype=bool))
        att = jnp.where(causal[None, None], att, -jnp.inf)
        att = jax.nn.softmax(att, axis=-1)
        y_lat = jnp.einsum('bhqk,bhkl->bhql', att, v_lat)
        y = y_lat @ l2o_w.T + l2o_b
        y = y.transpose(0, 2, 1, 3).reshape(B, T, C)
        return y @ cproj_w.T + cproj_b

    def _L0_attn_b_ref(x, w_qkv, w_fc, b_fc, gamma, beta):
        import jax, jax.numpy as jnp
        import numpy as np
        DIM = 128
        B, S = (8, 256)
        LN_EPS = 1e-05
        scaling = DIM ** (-0.5)
        qkv = jnp.einsum('bsd,ed->bse', x, w_qkv)
        q, k, v = jnp.split(qkv, 3, axis=-1)
        att = jax.nn.softmax(jnp.einsum('bqd,bkd->bqk', q, k) * scaling, axis=-1)
        y = jnp.einsum('bqk,bvd->bqd', att, v)
        y = jnp.einsum('bqd,ed->bqe', y, w_fc) + b_fc
        h = x + y
        mu = jnp.mean(h, axis=-1, keepdims=True)
        var = jnp.var(h, axis=-1, keepdims=True)
        return (h - mu) * jax.lax.rsqrt(var + LN_EPS) * gamma + beta

    def _L0_ffn_ref(x, Wg, W1, W2, W3, Ws1, Ws2, Ws3):
        import jax, jax.numpy as jnp
        import numpy as np
        B, T, C = (4, 256, 128)
        E = 8
        K = 2
        H = 176
        HS = 176 * 2
        b, t, c = x.shape
        xf = x.reshape(-1, c)
        n = xf.shape[0]
        router = xf @ Wg
        top_logits, idx = jax.lax.top_k(router, K)
        probs = jax.nn.softmax(top_logits.astype(jnp.float32), axis=-1).astype(x.dtype)
        w = jnp.zeros((n, E), x.dtype).at[jnp.arange(n)[:, None], idx].add(probs)
        h = jax.nn.silu(jnp.einsum('tc,ech->eth', xf, W1)) * jnp.einsum('tc,ech->eth', xf, W2)
        y = jnp.einsum('eth,ehc,te->tc', h, W3, w)
        y = y.reshape(b, t, c)
        hs = jax.nn.silu(xf @ Ws1) * (xf @ Ws2)
        y = y + (hs @ Ws3).reshape(b, t, c)
        return y

    def _L1_attn_a_ref(tokens, norm_w, a, b, c, skip, w_out, b_out):
        import jax, jax.numpy as jnp
        import numpy as np
        EPS = 0.0001
        B, T, DIM = tokens.shape
        H, D, S = b.shape
        ms = jnp.mean(jnp.square(tokens), axis=-1, keepdims=True)
        x = tokens * jax.lax.rsqrt(ms + EPS) * norm_w
        x = x.reshape(B, T, H, D)
        a_t = jnp.tanh(a)
        state0 = jnp.zeros((B, H, S), dtype=tokens.dtype)

        def step(state, x_t):
            state = jnp.tanh(jnp.einsum('bhs,hst->bht', state, a_t) + jnp.einsum('bhd,hds->bhs', x_t, b))
            mixed = jnp.einsum('bhs,hsd->bhd', state, c) + skip[None] * x_t
            return (state, mixed)
        xs = jnp.moveaxis(x, 1, 0)
        _, outs = jax.lax.scan(step, state0, xs)
        outs = jnp.moveaxis(outs, 0, 1).reshape(B, T, DIM)
        return tokens + outs @ w_out.T + b_out

    def _L1_attn_b_ref(x, Wqkv, bqkv, Wproj, bproj, scale):
        import jax, jax.numpy as jnp
        import numpy as np
        N_EMBD = 128
        N_HEAD = 16
        HEAD_SIZE = N_EMBD // N_HEAD
        B, T = (8, 512)
        EPS = 0.001
        Bsz, Tlen, C = x.shape
        H, D = (N_HEAD, HEAD_SIZE)
        qkv = jnp.einsum('btc,ec->bte', x, Wqkv) + bqkv
        q, k, v = jnp.split(qkv, 3, axis=-1)
        q = q.reshape(Bsz, Tlen, H, D) * scale
        k = k.reshape(Bsz, Tlen, H, D) * scale
        v = v.reshape(Bsz, Tlen, H, D)
        q = jax.nn.elu(q) + 1.0
        k = jax.nn.elu(k) + 1.0
        kv = k * v
        k_cumsum = jnp.cumsum(k, axis=1)
        kv_cumsum = jnp.cumsum(kv, axis=1)
        denom = jnp.einsum('bthd,bthd->bth', q, k_cumsum)
        denom = jnp.clip(denom, EPS, None)[..., None]
        y = q * kv_cumsum / denom
        y = y.reshape(Bsz, Tlen, C)
        return jnp.einsum('btc,ec->bte', y, Wproj) + bproj

    def _L1_ffn_ref(hidden_states, router_weight, e_bias, gate_w, up_w, down_w, sh_gate_w, sh_up_w, sh_down_w):
        import jax, jax.numpy as jnp
        import numpy as np
        B, S, H = (1, 256, 128)
        E, K = (16, 4)
        G, TG = (4, 2)
        I_MOE = 64
        N_SH = 2
        SCALE = 2.5

        def _mlp(x, gw, uw, dw):
            return jax.nn.silu(x @ gw.T) * (x @ uw.T) @ dw.T

        def _route(x2d, router_weight, e_bias):
            T = x2d.shape[0]
            scores = jax.nn.sigmoid(x2d @ router_weight.T)
            sc = scores + e_bias[None, :]
            group_scores = jnp.sum(jax.lax.top_k(sc.reshape(T, G, E // G), 2)[0], axis=-1)
            _, gidx = jax.lax.top_k(group_scores, TG)
            gmask = jnp.zeros((T, G), sc.dtype).at[jnp.arange(T)[:, None], gidx].set(1.0)
            smask = jnp.repeat(gmask, E // G, axis=1)
            masked = jnp.where(smask > 0, sc, 0.0)
            _, tidx = jax.lax.top_k(masked, K)
            tw = jnp.take_along_axis(scores, tidx, axis=1)
            tw = tw / (jnp.sum(tw, axis=-1, keepdims=True) + 1e-20)
            tw = tw * SCALE
            return (tidx, tw)

        def _moe_forward(hidden_states, router_weight, e_bias, gate_w, up_w, down_w, sh_gate_w, sh_up_w, sh_down_w):
            orig_shape = hidden_states.shape
            x = hidden_states.reshape(-1, H)
            T = x.shape[0]
            tidx, tw = _route(x, router_weight, e_bias)
            g = jnp.einsum('th,eih->tei', x, gate_w)
            u = jnp.einsum('th,eih->tei', x, up_w)
            h = jax.nn.silu(g) * u
            yo = jnp.einsum('tei,ehi->teh', h, down_w)
            combine = jnp.zeros((T, E), tw.dtype).at[jnp.arange(T)[:, None], tidx].add(tw)
            routed = jnp.einsum('te,teh->th', combine, yo)
            shared = _mlp(hidden_states.reshape(-1, H), sh_gate_w, sh_up_w, sh_down_w)
            return (routed + shared).reshape(orig_shape)
        return _moe_forward(hidden_states, router_weight, e_bias, gate_w, up_w, down_w, sh_gate_w, sh_up_w, sh_down_w)

    def _L2_attn_a_ref(hidden_states, in_proj_w, conv_w, conv_b, x_proj_w, dt_proj_w, dt_proj_b, A_log, D, out_proj_w):
        import jax, jax.numpy as jnp
        import numpy as np
        D_MODEL, D_INNER, D_STATE, D_CONV, DT_RANK = (128, 256, 16, 4, 64)
        BATCH, SEQLEN = (4, 256)

        def _silu(x):
            return x * jax.nn.sigmoid(x)

        def _mamba_forward(hidden_states, in_proj_w, conv_w, conv_b, x_proj_w, dt_proj_w, dt_proj_b, A_log, D, out_proj_w):
            B, L, _ = hidden_states.shape
            d_inner, d_conv = conv_w.shape
            d_state = A_log.shape[1]
            dt_rank = dt_proj_w.shape[1]
            xz = jnp.einsum('bld,ed->ble', hidden_states, in_proj_w)
            x, z = (xz[..., :d_inner], xz[..., d_inner:])
            x_pad = jnp.pad(x, ((0, 0), (d_conv - 1, 0), (0, 0)))
            x_conv = sum((x_pad[:, w:w + L, :] * conv_w[:, w] for w in range(d_conv))) + conv_b
            x_conv = _silu(x_conv)
            x_dbl = jnp.einsum('bld,ed->ble', x_conv, x_proj_w)
            dt_in = x_dbl[..., :dt_rank]
            Bv = x_dbl[..., dt_rank:dt_rank + d_state]
            Cv = x_dbl[..., dt_rank + d_state:]
            delta = jax.nn.softplus(jnp.einsum('blr,dr->bld', dt_in, dt_proj_w) + dt_proj_b)
            A = -jnp.exp(A_log)

            def step(h, inp):
                d_t, B_t, C_t, u_t = inp
                dA = jnp.exp(d_t[:, :, None] * A)
                h = h * dA + (d_t * u_t)[:, :, None] * B_t[:, None, :]
                y = jnp.einsum('bdn,bn->bd', h, C_t)
                return (h, y)
            h0 = jnp.zeros((B, d_inner, d_state), dtype=hidden_states.dtype)
            xs = (jnp.swapaxes(delta, 0, 1), jnp.swapaxes(Bv, 0, 1), jnp.swapaxes(Cv, 0, 1), jnp.swapaxes(x_conv, 0, 1))
            _, ys = jax.lax.scan(step, h0, xs)
            y = jnp.swapaxes(ys, 0, 1) + x_conv * D
            y = y * _silu(z)
            return jnp.einsum('bld,md->blm', y, out_proj_w)
        return _mamba_forward(hidden_states, in_proj_w, conv_w, conv_b, x_proj_w, dt_proj_w, dt_proj_b, A_log, D, out_proj_w)

    def _L2_attn_b_ref(hidden_states, in_proj_w, conv_w, conv_b, x1_proj_w, dt1_proj_w, dt1_proj_b, A1_log, D1, x2_proj_w, dt2_proj_w, dt2_proj_b, A2_log, D2, out_proj_w):
        import jax, jax.numpy as jnp
        import numpy as np
        import math
        D_MODEL = 128
        EXPAND = 2
        D_INNER = EXPAND * D_MODEL
        D_STATE = 16
        D_CONV = 4
        DT_RANK = math.ceil(D_MODEL / 16)
        BATCH = 1
        SEQLEN = 256

        def _silu(x):
            return x * jax.nn.sigmoid(x)

        def _selective_scan(u, delta, A, B, C, D, z, delta_bias):
            delta = jax.nn.softplus(delta + delta_bias[None, :, None])
            dA = jnp.exp(jnp.einsum('bdl,dn->lbdn', delta, A))
            dBu = jnp.einsum('bdl,bnl->lbdn', delta * u, B)
            Ct = jnp.transpose(C, (2, 0, 1))

            def step(h, inp):
                dA_t, dBu_t, C_t = inp
                h = dA_t * h + dBu_t
                y = jnp.einsum('bdn,bn->bd', h, C_t)
                return (h, y)
            h0 = jnp.zeros((u.shape[0], u.shape[1], A.shape[1]), dtype=u.dtype)
            _, ys = jax.lax.scan(step, h0, (dA, dBu, Ct))
            y = jnp.transpose(ys, (1, 2, 0))
            y = y + D[:, None] * u
            return y * _silu(z)

        def _causal_conv1d(x, conv_w, conv_b):
            x_pad = jnp.pad(x, ((0, 0), (0, 0), (D_CONV - 1, 0)))
            kernel = conv_w[:, None, :]
            y = jax.lax.conv_general_dilated(x_pad, kernel, window_strides=(1,), padding='VALID', dimension_numbers=('NCH', 'OIH', 'NCH'), feature_group_count=D_INNER)
            return y + conv_b[None, :, None]
        xz = jnp.einsum('bld,ed->bel', hidden_states, in_proj_w)
        x, z = jnp.split(xz, 2, axis=1)
        A1 = -jnp.exp(A1_log.astype(jnp.float32))
        A2 = -jnp.exp(A2_log.astype(jnp.float32))
        x = _silu(_causal_conv1d(x, conv_w, conv_b))

        def branch_params(xp_w, dtp_w):
            dbl = jnp.einsum('bdl,kd->bkl', x, xp_w)
            dt, Bm, Cm = jnp.split(dbl, [DT_RANK, DT_RANK + D_STATE], axis=1)
            dt = jnp.einsum('brl,dr->bdl', dt, dtp_w)
            return (dt, Bm, Cm)
        dt1, B1, C1 = branch_params(x1_proj_w, dt1_proj_w)
        dt2, B2, C2 = branch_params(x2_proj_w, dt2_proj_w)
        y1 = _selective_scan(x, dt1, A1, B1, C1, D1.astype(jnp.float32), z, dt1_proj_b.astype(jnp.float32))
        y2 = _selective_scan(x, dt2, A2, B2, C2, D2.astype(jnp.float32), z, dt2_proj_b.astype(jnp.float32))
        y = y1 - y2
        out = jnp.einsum('bdl,od->blo', y, out_proj_w)
        return out

    def _L2_ffn_ref(x, w1_w, w1_s, w2_w, w2_s, h1_w, h1_s, h2_w, h2_s, w3_w, w3_s):
        import jax, jax.numpy as jnp
        import numpy as np
        D_IN, D_HID = (128, 512)

        def _ternary(key, shape):
            return jax.random.randint(key, shape, -1, 2).astype(jnp.float32)

        def _tlin(x, w, s):
            return jnp.einsum('bsi,oi->bso', x, w) * s
        h = jax.nn.silu(_tlin(x, w1_w, w1_s)) * _tlin(x, w2_w, w2_s)
        h = jax.nn.gelu(_tlin(h, h1_w, h1_s), approximate=False)
        h = jax.nn.gelu(_tlin(h, h2_w, h2_s), approximate=False)
        return _tlin(h, w3_w, w3_s)

    def _L3_attn_a_ref(x, Wq, Wk, Wv, Wo):
        import jax, jax.numpy as jnp
        import numpy as np
        from jax import lax
        B, T, D = (4, 512, 128)
        H, d = (4, 64)
        EPS = 1e-06

        def pos_unit(x):
            p = jax.nn.elu(x) + 1.0
            return p / (jnp.linalg.norm(p, axis=-1, keepdims=True) + EPS)

        def _reference_tuple_inner(x, Wq, Wk, Wv, Wo):
            Bx, Tx, Dx = x.shape
            q = (x @ Wq.T).reshape(Bx, Tx, H, d)
            k = (x @ Wk.T).reshape(Bx, Tx, H, d)
            v = (x @ Wv.T).reshape(Bx, Tx, H, d)
            q = pos_unit(q)
            k = pos_unit(k)
            qT = jnp.transpose(q, (1, 0, 2, 3))
            kT = jnp.transpose(k, (1, 0, 2, 3))
            vT = jnp.transpose(v, (1, 0, 2, 3))
            kv0 = jnp.zeros((Bx, H, d, d), dtype=x.dtype)
            kc0 = jnp.zeros((Bx, H, d), dtype=x.dtype)

            def step(carry, inp):
                kv_cum, k_cum = carry
                qt, kt, vt = inp
                kv_cum = kv_cum + jnp.einsum('bhd,bhj->bhjd', kt, vt)
                k_cum = k_cum + kt
                num = jnp.einsum('bhd,bhjd->bhj', qt, kv_cum)
                den = jnp.einsum('bhd,bhd->bh', qt, k_cum)[..., None] + EPS
                return ((kv_cum, k_cum), num / den)
            (kv_f, kc_f), yT = lax.scan(step, (kv0, kc0), (qT, kT, vT))
            y = jnp.transpose(yT, (1, 0, 2, 3)).reshape(Bx, Tx, H * d)
            y = y @ Wo.T
            return (y, kv_f, kc_f)
        return _reference_tuple_inner(x, Wq, Wk, Wv, Wo)[0]

    def _L3_attn_b_ref(x, Wk, Wv, Wr, Wo, time_decay, time_first):
        import jax, jax.numpy as jnp
        import numpy as np
        DIM = 128
        B, S = (4, 512)
        k = jnp.einsum('bsd,ed->bse', x, Wk)
        v = jnp.einsum('bsd,ed->bse', x, Wv)
        r = jax.nn.sigmoid(jnp.einsum('bsd,ed->bse', x, Wr))
        w = -jnp.exp(time_decay)
        decay = jnp.exp(w)
        eu = jnp.exp(time_first)
        kv = k * v

        def step(state, kv_t):
            wkv = state + eu * kv_t
            new_state = decay * state + kv_t
            return (new_state, wkv)
        state0 = jnp.zeros((x.shape[0], x.shape[2]), dtype=x.dtype)
        _, wkv_seq = jax.lax.scan(step, state0, jnp.swapaxes(kv, 0, 1))
        out = r * jnp.swapaxes(wkv_seq, 0, 1)
        return jnp.einsum('bsd,ed->bse', out, Wo)

    def _L3_ffn_ref(x, phi_w, phi_b, expert_w, expert_b):
        import jax, jax.numpy as jnp
        import numpy as np
        T, Z, D_DIM = (8, 256, 128)
        N_EXP, P_SLOT, H = (64, 32, 128)
        LN_EPS = 1e-05
        t, z, d = x.shape
        n = expert_w.shape[0]
        p = phi_w.shape[0] // n
        logits = (jnp.einsum('tzd,ed->tze', x, phi_w) + phi_b).reshape(t, z, n, p)
        D = jax.nn.softmax(logits, axis=3)
        C = jax.nn.softmax(logits, axis=2)
        X_tilde = jnp.einsum('tznp,tzd->npd', D, x)
        X_tilde = jnp.clip(X_tilde, -33000.0, 65000.0)
        mu = jnp.mean(X_tilde, axis=-1, keepdims=True)
        var = jnp.mean(jnp.square(X_tilde - mu), axis=-1, keepdims=True)
        X_tilde = (X_tilde - mu) * jax.lax.rsqrt(var + LN_EPS)
        X_tilde = jnp.tanh(X_tilde)
        Y_tilde = jnp.einsum('npd,ndH->npH', X_tilde, expert_w) + expert_b[:, None, :]
        Y = jnp.einsum('tznp,npH->tzH', C, Y_tilde)
        return Y
    x = L0_attn_a_x
    x = x + _L0_attn_a_ref(_layernorm(x, axis=-1), L0_attn_a_c_attn_w, L0_attn_a_c_attn_b, L0_attn_a_q2l_w, L0_attn_a_q2l_b, L0_attn_a_kv2l_w, L0_attn_a_kv2l_b, L0_attn_a_l2o_w, L0_attn_a_l2o_b, L0_attn_a_wqk_w, L0_attn_a_wqk_b, L0_attn_a_cproj_w, L0_attn_a_cproj_b)
    x = x + _L0_ffn_ref(_layernorm(x, axis=-1), L0_ffn_Wg, L0_ffn_W1, L0_ffn_W2, L0_ffn_W3, L0_ffn_Ws1, L0_ffn_Ws2, L0_ffn_Ws3)
    x = x + _L0_attn_b_ref(_layernorm(x, axis=-1), L0_attn_b_w_qkv, L0_attn_b_w_fc, L0_attn_b_b_fc, L0_attn_b_gamma, L0_attn_b_beta)
    x = x + _L0_ffn_ref(_layernorm(x, axis=-1), L0_ffn_Wg, L0_ffn_W1, L0_ffn_W2, L0_ffn_W3, L0_ffn_Ws1, L0_ffn_Ws2, L0_ffn_Ws3)
    x = x + _L1_attn_a_ref(_layernorm(x, axis=-1), L1_attn_a_norm_w, L1_attn_a_a, L1_attn_a_b, L1_attn_a_c, L1_attn_a_skip, L1_attn_a_w_out, L1_attn_a_b_out)
    x = x + _L1_ffn_ref(_layernorm(x, axis=-1), L1_ffn_router_weight, L1_ffn_e_bias, L1_ffn_gate_w, L1_ffn_up_w, L1_ffn_down_w, L1_ffn_sh_gate_w, L1_ffn_sh_up_w, L1_ffn_sh_down_w)
    x = x + _L1_attn_b_ref(_layernorm(x, axis=-1), L1_attn_b_Wqkv, L1_attn_b_bqkv, L1_attn_b_Wproj, L1_attn_b_bproj, L1_attn_b_scale)
    x = x + _L1_ffn_ref(_layernorm(x, axis=-1), L1_ffn_router_weight, L1_ffn_e_bias, L1_ffn_gate_w, L1_ffn_up_w, L1_ffn_down_w, L1_ffn_sh_gate_w, L1_ffn_sh_up_w, L1_ffn_sh_down_w)
    x = x + _L2_attn_a_ref(_layernorm(x, axis=-1), L2_attn_a_in_proj_w, L2_attn_a_conv_w, L2_attn_a_conv_b, L2_attn_a_x_proj_w, L2_attn_a_dt_proj_w, L2_attn_a_dt_proj_b, L2_attn_a_A_log, L2_attn_a_D, L2_attn_a_out_proj_w)
    x = x + _L2_ffn_ref(_layernorm(x, axis=-1), L2_ffn_w1_w, L2_ffn_w1_s, L2_ffn_w2_w, L2_ffn_w2_s, L2_ffn_h1_w, L2_ffn_h1_s, L2_ffn_h2_w, L2_ffn_h2_s, L2_ffn_w3_w, L2_ffn_w3_s)
    x = x + _L2_attn_b_ref(_layernorm(x, axis=-1), L2_attn_b_in_proj_w, L2_attn_b_conv_w, L2_attn_b_conv_b, L2_attn_b_x1_proj_w, L2_attn_b_dt1_proj_w, L2_attn_b_dt1_proj_b, L2_attn_b_A1_log, L2_attn_b_D1, L2_attn_b_x2_proj_w, L2_attn_b_dt2_proj_w, L2_attn_b_dt2_proj_b, L2_attn_b_A2_log, L2_attn_b_D2, L2_attn_b_out_proj_w)
    x = x + _L2_ffn_ref(_layernorm(x, axis=-1), L2_ffn_w1_w, L2_ffn_w1_s, L2_ffn_w2_w, L2_ffn_w2_s, L2_ffn_h1_w, L2_ffn_h1_s, L2_ffn_h2_w, L2_ffn_h2_s, L2_ffn_w3_w, L2_ffn_w3_s)
    x = x + _L3_attn_a_ref(_layernorm(x, axis=-1), L3_attn_a_Wq, L3_attn_a_Wk, L3_attn_a_Wv, L3_attn_a_Wo)
    x = x + _L3_ffn_ref(_layernorm(x, axis=-1), L3_ffn_phi_w, L3_ffn_phi_b, L3_ffn_expert_w, L3_ffn_expert_b)
    x = x + _L3_attn_b_ref(_layernorm(x, axis=-1), L3_attn_b_Wk, L3_attn_b_Wv, L3_attn_b_Wr, L3_attn_b_Wo, L3_attn_b_time_decay, L3_attn_b_time_first)
    x = x + _L3_ffn_ref(_layernorm(x, axis=-1), L3_ffn_phi_w, L3_ffn_phi_b, L3_ffn_expert_w, L3_ffn_expert_b)
    return x

_drawn_inputs = setup_inputs


def setup_inputs(seed=0):
    import zlib

    import numpy as np

    out = dict(_drawn_inputs(seed))
    spreads = {'L0_attn_a_c_attn_b': (0.0, 0.1),
     'L0_attn_a_q2l_b': (0.0, 0.1),
     'L0_attn_a_kv2l_b': (0.0, 0.1),
     'L0_attn_a_l2o_b': (0.0, 0.1),
     'L0_attn_a_wqk_b': (0.0, 0.1),
     'L0_attn_a_cproj_b': (0.0, 0.1),
     'L0_attn_b_b_fc': (0.0, 0.1),
     'L0_attn_b_gamma': (1.0, 0.2),
     'L0_attn_b_beta': (0.0, 0.1),
     'L1_attn_a_norm_w': (1.0, 0.2),
     'L1_attn_a_skip': (1.0, 0.2),
     'L1_attn_a_b_out': (0.0, 0.1),
     'L1_attn_b_bqkv': (0.0, 0.1),
     'L1_attn_b_bproj': (0.0, 0.1),
     'L1_ffn_e_bias': (0.0, 0.1),
     'L2_attn_a_D': (1.0, 0.2),
     'L2_attn_b_conv_b': (0.0, 0.1),
     'L2_attn_b_D1': (1.0, 0.2),
     'L2_attn_b_D2': (1.0, 0.2)}
    factors = {}
    for name, (base, spread) in spreads.items():
        noise = np.random.default_rng([zlib.crc32(name.encode()), seed]).standard_normal(out[name].shape)
        drawn = base * np.exp(spread * noise) if base else spread * noise
        out[name] = jnp.asarray(drawn.astype(out[name].dtype))
    for name, factor in factors.items():
        out[name] = (out[name] * factor).astype(out[name].dtype)
    return out
```

```python
from contextlib import ExitStack, contextmanager

import numpy as np

import concourse.bass as bass
from concourse import mybir

F32 = mybir.dt.float32
BF16 = mybir.dt.bfloat16
U32 = mybir.dt.uint32
ALU = mybir.AluOpType
ACT = mybir.ActivationFunctionType
AX = mybir.AxisListType

P = 128
BATCH, TIME = 4, 512
TOKENS = BATCH * TIME
CHUNK = 512
CHUNKS = TOKENS // CHUNK
TILES = TOKENS // P
QT = CHUNK // P
MASKED = -1e30
LOWEST = -3e38


class Core:

    def __init__(self, nc):
        self.nc = nc
        self.count = 0


@contextmanager
def stage(g, semaphores):
    nc = g.nc
    g.count += 1
    n = g.count
    with ExitStack() as ctx:
        def sb(name, shape, dtype=F32):
            return ctx.enter_context(nc.sbuf_tensor(f"{name}_{n}", shape, dtype))

        sems = [nc.alloc_semaphore(f"{name}_{n}") for name in semaphores.split()]
        yield sb, sems
        nc.clear_and_free_semaphores(sems)
        nc.all_engine_barrier()


def chunk(tensor, b):
    return tensor[:, bass.ds(b * CHUNK, CHUNK)]


def fixed(tensor, j):
    return tensor[:, j * CHUNK:(j + 1) * CHUNK]


def layernorm(g):
    nc, bank, x, y = g.nc, g.bank, g.resid, g.normed
    with stage(g, "mean_ready centred squared var_ready logged rstd_ready normed_ready") as (sb, sems):
        mean_ready, centred, squared, var_ready, logged, rstd_ready, normed_ready = sems
        sq = sb("ln_sq", [P, TOKENS])
        rstd = sb("ln_rstd", [P, TOKENS])
        with nc.Block() as block:
            @block.tensor
            def _(pe):
                for j in range(CHUNKS):
                    nc.tensor.matmul(bank[j][:, :], g.mean_of, fixed(x, j), start=True, stop=True).then_inc(mean_ready, 1)
                for j in range(CHUNKS):
                    pe.wait_ge(squared, j + 1)
                    nc.tensor.matmul(bank[4 + j][:, :], g.mean_of, fixed(sq, j), start=True, stop=True).then_inc(var_ready, 1)

            @block.vector
            def _(dve):
                for j in range(CHUNKS):
                    dve.wait_ge(mean_ready, j + 1)
                    nc.vector.tensor_tensor(fixed(y, j), fixed(x, j), bank[j][:, :], ALU.subtract).then_inc(centred, 1)
                for j in range(CHUNKS):
                    dve.wait_ge(rstd_ready, j + 1)
                    dve.wait_ge(centred, j + 1)
                    nc.vector.tensor_tensor(fixed(y, j), fixed(y, j), fixed(rstd, j), ALU.mult).then_inc(normed_ready, 1)

            @block.scalar
            def _(act):
                for j in range(CHUNKS):
                    act.wait_ge(centred, j + 1)
                    nc.scalar.activation(fixed(sq, j), fixed(y, j), ACT.Square).then_inc(squared, 1)
                for j in range(CHUNKS):
                    act.wait_ge(var_ready, j + 1)
                    nc.scalar.activation(fixed(rstd, j), bank[4 + j][:, :], ACT.Ln, bias=g.eps5).then_inc(logged, 1)
                    act.wait_ge(logged, j + 1)
                    nc.scalar.activation(fixed(rstd, j), fixed(rstd, j), ACT.Exp, scale=-0.5).then_inc(rstd_ready, 1)


def latent_attention(g):
    nc, bank, w = g.nc, g.bank, g.w["l0a"]
    HEADS, HD, LAT, GROUPS = 16, 8, 32, 4
    SCALE = LAT ** -0.5
    HALF = HEADS // 2
    with stage(g, "proj_ready proj_kept lat_ready lat_kept rot_ready cos_done sin_done roped qk_ready qk_kept "
                  "vlat_ready vlat_kept v2_ready v2_kept cleared ones_set score_ready max_ready maxt_ready hi_kept "
                  "rest1 mid_kept mid_moved rest2 lo_kept st_ready exp_ready pv_ready recip_done "
                  "y_half y_ready out_ready resid_done") as (sb, sems):
        (proj_ready, proj_kept, lat_ready, lat_kept, rot_ready, cos_done, sin_done, roped, qk_ready, qk_kept,
         vlat_ready, vlat_kept, v2_ready, v2_kept, cleared, ones_set, score_ready, max_ready, maxt_ready, hi_kept,
         rest1, mid_kept, mid_moved, rest2, lo_kept, st_ready, exp_ready, pv_ready, recip_done,
         y_half, y_ready, out_ready, resid_done) = sems
        qkv = sb("a_qkv", [P, 3, CHUNK])
        lat = sb("a_lat", [P, 2, CHUNK])
        rc = sb("a_rc", [P, 2, CHUNK])
        rs = sb("a_rs", [P, 2, CHUNK])
        qr = sb("a_qr", [P, 2, CHUNK])
        kr = sb("a_kr", [P, GROUPS, CHUNK])
        qk = sb("a_qk", [P, GROUPS, CHUNK])
        vl = sb("a_vl", [P, 2, CHUNK])
        wide = sb("a_wide", [P, QT, 2, HALF * (P + HD)])
        mx = sb("a_mx", [P, QT, HEADS])
        mt = sb("a_mt", [P, CHUNK], BF16)
        mid = sb("a_mid", [HEADS, CHUNK], BF16)
        r1 = sb("a_r1", [HEADS, CHUNK])
        r2 = sb("a_r2", [HEADS, CHUNK])
        pt = sb("a_pt", [P, 4, CHUNK])
        rd = sb("a_rd", [64, 2, CHUNK])
        y = sb("a_y", [P, CHUNK])

        def values(kt, half):
            return wide[:, kt, half, :].rearrange("p (j e) -> p j e", e=P + HD)[:, :, 0:HD]

        def denominators(kt, half):
            return wide[:, kt, half, :].rearrange("p (j e) -> p j e", e=P + HD)[:, :, 64:64 + HD]

        items = [(h, kt) for h in range(HEADS) for kt in range(QT)]
        LOOK = 3
        with nc.Block() as block:
            @block.tensor
            def _(pe):
                pe.wait_ge(g.loaded["l0a"], 16)
                pe.wait_ge(ones_set, 1)
                with pe.Fori(0, CHUNKS) as b:
                    pe.wait_ge(resid_done, b + 1)
                    for i in range(3):
                        nc.tensor.matmul(bank[i][:, :], w["wqkv"][:, i * P:(i + 1) * P], chunk(g.normed, b),
                                         start=True, stop=True).then_inc(proj_ready, 1)
                    for n in range(2 * GROUPS):
                        i, s = n // GROUPS, n % 2
                        src = "q2l" if i == 0 else "kv2l"
                        pe.wait_ge(proj_kept, b * 3 + i + 1)
                        nc.tensor.matmul(bank[3][:, :], w[src][:, (n % GROUPS) * P:(n % GROUPS + 1) * P], qkv[:, i, :],
                                         start=True, stop=True).then_inc(lat_ready, 1)
                        pe.wait_ge(lat_kept, b * 8 + n + 1)
                        if n >= 1:
                            pe.wait_ge(sin_done, b * 8 + n)
                        nc.tensor.matmul(bank[4][:, :], w["rot"], lat[:, s, :], start=True, stop=True).then_inc(rot_ready, 1)
                        if i == 0:
                            pe.wait_ge(roped, b * 8 + n + 1)
                            if n >= 1:
                                pe.wait_ge(qk_kept, b * 4 + n)
                            nc.tensor.matmul(bank[5][:, :], w["wqk"], qr[:, s, :], start=True, stop=True).then_inc(qk_ready, 1)
                    for n in range(GROUPS):
                        pe.wait_ge(proj_kept, b * 3 + 3)
                        nc.tensor.matmul(bank[6 + n % 2][:, :], w["kv2l"][:, n * P:(n + 1) * P], qkv[:, 2, :],
                                         start=True, stop=True).then_inc(vlat_ready, 1)
                        pe.wait_ge(vlat_kept, b * 4 + n + 1)
                        for kt in range(QT):
                            mm = nc.tensor.matmul(bank[0][:, kt * P + n * 32:kt * P + n * 32 + 32],
                                                  vl[:, n % 2, kt * P:(kt + 1) * P], w["l2o"], start=True, stop=True)
                    mm.then_inc(v2_ready, 1)
                    pe.wait_ge(sin_done, b * 8 + 8)
                    pe.wait_ge(qk_kept, b * 4 + 4)
                    pe.wait_ge(roped, b * 8 + 8)
                    pe.wait_ge(v2_kept, b * 2 + 2)
                    for n in range(GROUPS * QT):
                        grp, qt = n // QT, n % QT
                        if n >= 2:
                            pe.wait_ge(max_ready, b * 16 + n - 1)
                        for j in range(4):
                            s = bank[4 * (n % 2) + j]
                            nc.tensor.matmul(s[:, 0:(qt + 1) * P], qk[32 * j:32 * j + 32, grp, qt * P:(qt + 1) * P],
                                             kr[32 * j:32 * j + 32, grp, 0:(qt + 1) * P], start=True, stop=False)
                            mm = nc.tensor.matmul(s[:, qt * P:(qt + 1) * P], g.ident_bf, g.mask_qk, start=False, stop=True)
                        mm.then_inc(score_ready, 1)
                    pe.wait_ge(max_ready, b * 16 + 16)
                    for qt in range(QT):
                        mm = nc.tensor.transpose(bank[0][0:HEADS, qt * P:(qt + 1) * P], mx[:, qt, :], g.ident)
                    mm.then_inc(maxt_ready, 1)
                    pe.wait_ge(hi_kept, b + 1)
                    pe.wait_ge(rest1, b + 1)
                    pe.wait_ge(mid_moved, b + 1)
                    pe.wait_ge(lo_kept, b + 1)
                    for n in range(len(items) + LOOK):
                        if n < len(items):
                            h, kt = items[n]
                            grp, j = h // 4, h % 4
                            if n >= 4:
                                pe.wait_ge(exp_ready, b * 64 + n - 3)
                            s = bank[n % 4][:, kt * P:CHUNK]
                            nc.tensor.matmul(s, kr[32 * j:32 * j + 32, grp, kt * P:(kt + 1) * P],
                                             qk[32 * j:32 * j + 32, grp, kt * P:CHUNK], start=True, stop=False)
                            nc.tensor.matmul(bank[n % 4][:, kt * P:(kt + 1) * P], g.ident_bf, g.mask_kq, start=False, stop=False)
                            nc.tensor.matmul(s, g.pick_b[0:96, h, :], mt[0:96, kt * P:CHUNK],
                                             start=False, stop=True).then_inc(st_ready, 1)
                        if n >= LOOK:
                            h, kt = items[n - LOOK]
                            half, j = h // HALF, h % HALF
                            pe.wait_ge(exp_ready, b * 64 + n - LOOK + 1)
                            mm = nc.tensor.matmul(bank[6 + half][:, kt * P:CHUNK], wide[:, kt, half, j * P:(j + 1) * P],
                                                  pt[:, (n - LOOK) % 4, kt * P:CHUNK],
                                                  start=(j == 0 and kt == 0), stop=(j == HALF - 1 and kt == QT - 1))
                            mm.then_inc(pv_ready, 1)
                    pe.wait_ge(y_ready, b + 1)
                    nc.tensor.matmul(bank[5][:, :], w["cproj"], y[:, :], start=True, stop=True).then_inc(out_ready, 1)

            @block.scalar
            def _(act):
                act.wait_ge(g.loaded["l0a"], 16)
                with act.Fori(0, CHUNKS) as b:
                    for i in range(3):
                        act.wait_ge(proj_ready, b * 3 + i + 1)
                        nc.scalar.activation(qkv[:, i, :], bank[i][:, :], ACT.Identity,
                                             bias=w["bqkv"][:, i:i + 1]).then_inc(proj_kept, 1)
                    for n in range(2 * GROUPS):
                        i, s = n // GROUPS, n % 2
                        act.wait_ge(lat_ready, b * 8 + n + 1)
                        if n >= 2:
                            act.wait_ge(cos_done, b * 8 + n - 1)
                            act.wait_ge(rot_ready, b * 8 + n - 1)
                        nc.scalar.activation(lat[:, s, :], bank[3][:, :], ACT.Identity,
                                             bias=w["q2l_b" if i == 0 else "kv2l_b"]).then_inc(lat_kept, 1)
                        if i == 0:
                            act.wait_ge(qk_ready, b * 4 + n + 1)
                            nc.scalar.activation(qk[:, n, :], bank[5][:, :], ACT.Identity, bias=w["wqk_b"]).then_inc(qk_kept, 1)
                    for n in range(GROUPS):
                        act.wait_ge(vlat_ready, b * 4 + n + 1)
                        nc.scalar.activation(vl[:, n % 2, :], bank[6 + n % 2][:, :], ACT.Identity,
                                             bias=w["kv2l_b"]).then_inc(vlat_kept, 1)
                    act.wait_ge(maxt_ready, b + 1)
                    nc.scalar.activation(mt[0:HEADS, :], bank[0][0:HEADS, :], ACT.Copy, scale=-1.0).then_inc(hi_kept, 1)
                    for n, (h, kt) in enumerate(items):
                        act.wait_ge(st_ready, b * 64 + n + 1)
                        if n >= 4:
                            act.wait_ge(pv_ready, b * 64 + n - 3)
                        nc.scalar.activation(pt[:, n % 4, kt * P:CHUNK], bank[n % 4][:, kt * P:CHUNK], ACT.Exp,
                                             scale=SCALE).then_inc(exp_ready, 1)

            @block.gpsimd
            def _(pool):
                nc.gpsimd.memset(wide[:], 0.0).then_inc(cleared, 1)
                nc.gpsimd.memset(mt[:], 0.0).then_inc(cleared, 1)
                pool.wait_ge(cleared, 1)
                for kt in range(QT):
                    for half in range(2):
                        ms = nc.gpsimd.memset(denominators(kt, half), 1.0)
                pool.wait_ge(cleared, 2)
                ms.then_inc(ones_set, 1)

            @block.vector
            def _(dve):
                dve.wait_ge(g.loaded["l0a"], 16)
                dve.wait_ge(ones_set, 1)
                nc.vector.memset(g.mark, 0.0).then_inc(resid_done, 1)
                with dve.Fori(0, CHUNKS) as b:
                    for n in range(2 * GROUPS):
                        i, s = n // GROUPS, n % 2
                        dve.wait_ge(lat_kept, b * 8 + n + 1)
                        nc.vector.tensor_tensor(rc[:, s, :], lat[:, s, :], w["cos"], ALU.mult).then_inc(cos_done, 1)
                        dve.wait_ge(rot_ready, b * 8 + n + 1)
                        nc.vector.tensor_tensor(rs[:, s, :], bank[4][:, :], w["sin"], ALU.mult).then_inc(sin_done, 1)
                        dve.wait_ge(cos_done, b * 8 + n + 1)
                        dve.wait_ge(sin_done, b * 8 + n + 1)
                        if i == 0 and n >= 2:
                            dve.wait_ge(qk_ready, b * 4 + n - 1)
                        turned = qr[:, s, :] if i == 0 else kr[:, n - GROUPS, :]
                        nc.vector.tensor_tensor(turned, rc[:, s, :], rs[:, s, :], ALU.add).then_inc(roped, 1)
                    dve.wait_ge(v2_ready, b + 1)
                    for half in range(2):
                        for kt in range(QT):
                            cp = nc.vector.tensor_copy(
                                values(kt, half), bank[0][:, kt * P + 64 * half:kt * P + 64 * half + 64].rearrange(
                                    "p (j d) -> p j d", d=HD))
                        cp.then_inc(v2_kept, 1)
                    for n in range(GROUPS * QT):
                        grp, qt = n // QT, n % QT
                        dve.wait_ge(score_ready, b * 16 + n + 1)
                        nc.vector.tensor_reduce(mx[:, qt, 4 * grp:4 * grp + 4], g.banks[4 * (n % 2):4 * (n % 2) + 4, 0:(qt + 1) * P],
                                                AX.X, ALU.max).then_inc(max_ready, 1)
                    dve.wait_ge(hi_kept, b + 1)
                    nc.vector.scalar_tensor_tensor(out=r1[:, :], in0=bank[0][0:HEADS, :], scalar=-1.0, in1=mt[0:HEADS, :],
                                                   op0=ALU.mult, op1=ALU.subtract).then_inc(rest1, 1)
                    dve.wait_ge(rest1, b + 1)
                    nc.vector.tensor_copy(mid[:, :], r1[:, :]).then_inc(mid_kept, 1)
                    dve.wait_ge(mid_kept, b + 1)
                    nc.vector.tensor_copy(mt[32:32 + HEADS, :], mid[:, :]).then_inc(mid_moved, 1)
                    nc.vector.tensor_tensor(r2[:, :], r1[:, :], mid[:, :], ALU.subtract).then_inc(rest2, 1)
                    dve.wait_ge(rest2, b + 1)
                    nc.vector.tensor_copy(mt[64:64 + HEADS, :], r2[:, :]).then_inc(lo_kept, 1)
                    for half in range(2):
                        dve.wait_ge(pv_ready, b * 64 + 32 * (half + 1))
                        nc.vector.reciprocal(rd[:, half, :], bank[6 + half][64:P, :]).then_inc(recip_done, 1)
                        dve.wait_ge(recip_done, b * 2 + half + 1)
                        nc.vector.tensor_tensor(y[64 * half:64 * half + 64, :], bank[6 + half][0:64, :], rd[:, half, :],
                                                ALU.mult).then_inc(y_half, 1)
                    dve.wait_ge(y_half, b * 2 + 2)
                    nc.vector.tensor_scalar(y[:, :], y[:, :], w["l2o_b"], None, ALU.add).then_inc(y_ready, 1)
                    dve.wait_ge(out_ready, b + 1)
                    nc.vector.scalar_tensor_tensor(out=chunk(g.resid, b), in0=bank[5][:, :], scalar=w["cproj_b"],
                                                   in1=chunk(g.resid, b), op0=ALU.add, op1=ALU.add).then_inc(resid_done, 1)


def spread_weights(g, router, experts):
    nc, bank = g.nc, g.bank
    with stage(g, "logit_ready score_kept step weight_ready turned cleared hi_kept rest1 mid_kept mid_moved rest2 "
                  "lo_kept") as (sb, sems):
        (logit_ready, score_kept, step, weight_ready, turned, cleared, hi_kept, rest1, mid_kept, mid_moved, rest2,
         lo_kept) = sems
        scores = sb("r_scores", [P, TILES, experts])
        weights = sb("r_weights", [P, TILES, experts])
        mid = sb("r_mid", [experts, TOKENS], BF16)
        r1 = sb("r_r1", [experts, TOKENS])
        spread = g.banks[4:8, 0:CHUNK][0:experts].rearrange("e a c -> e (a c)")
        with nc.Block() as block:
            @block.tensor
            def _(pe):
                pe.wait_ge(g.loaded[router.pack], 16)
                for t in range(TILES):
                    mm = nc.tensor.matmul(bank[0][:, t * experts:(t + 1) * experts], g.normed[:, t * P:(t + 1) * P],
                                          g.w[router.pack]["router"], start=True, stop=True)
                mm.then_inc(logit_ready, 1)
                pe.wait_ge(weight_ready, 1)
                for t in range(TILES):
                    mm = nc.tensor.transpose(bank[4 + t // QT][0:experts, t % QT * P:(t % QT + 1) * P], weights[:, t, :], g.ident)
                mm.then_inc(turned, 1)

            @block.scalar
            def _(act):
                act.wait_ge(logit_ready, 1)
                nc.scalar.activation(scores[:], bank[0][:, 0:TILES * experts].rearrange("p (t e) -> p t e", e=experts),
                                     router.squash).then_inc(score_kept, 1)
                router.scalar(nc, act, step)
                act.wait_ge(turned, 1)
                act.wait_ge(cleared, 2)
                nc.scalar.copy(g.rows[0:experts, :], spread).then_inc(hi_kept, 1)

            @block.gpsimd
            def _(pool):
                nc.gpsimd.memset(g.rows[:, :], 0.0).then_inc(cleared, 1)
                pool.wait_ge(cleared, 1)
                nc.gpsimd.memset(g.rows[96:97, :], 1.0).then_inc(cleared, 1)

            @block.vector
            def _(dve):
                dve.wait_ge(score_kept, 1)
                router.vector(nc, dve, step, sb, scores, weights).then_inc(weight_ready, 1)
                dve.wait_ge(hi_kept, 1)
                nc.vector.tensor_tensor(r1[:, :], spread, g.rows[0:experts, :], ALU.subtract).then_inc(rest1, 1)
                dve.wait_ge(rest1, 1)
                nc.vector.tensor_copy(mid[:, :], r1[:, :]).then_inc(mid_kept, 1)
                dve.wait_ge(mid_kept, 1)
                nc.vector.tensor_copy(g.rows[32:32 + experts, :], mid[:, :]).then_inc(mid_moved, 1)
                nc.vector.tensor_tensor(r1[:, :], r1[:, :], mid[:, :], ALU.subtract).then_inc(rest2, 1)
                dve.wait_ge(rest2, 1)
                nc.vector.tensor_copy(g.rows[64:64 + experts, :], r1[:, :]).then_inc(lo_kept, 1)


def chosen(nc, link, sb, g, name, values, pick, width):
    top = sb(f"{name}_top", [P, TILES, 8])
    at = sb(f"{name}_at", [P, TILES, 8], U32)
    atf = sb(f"{name}_atf", [P, TILES, 8])
    hot = [sb(f"{name}_hot{k}", [P, TILES, width]) for k in range(pick)]
    for t in range(TILES):
        last = nc.vector.max(top[:, t, :], values[:, t, :])
    link(last)
    for t in range(TILES):
        last = nc.vector.max_index(at[:, t, :], top[:, t, :], values[:, t, :])
    link(last)
    link(nc.vector.tensor_copy(atf[:], at[:]))
    for k in range(pick):
        last = nc.vector.tensor_tensor(hot[k][:], g.iota[:, 0:width].unsqueeze(1).broadcast_to([P, TILES, width]),
                                       atf[:, :, k:k + 1].broadcast_to([P, TILES, width]), ALU.is_equal)
    link(last)
    return top, hot


def linked(dve, step):
    count = [0]

    def link(ins):
        count[0] += 1
        ins.then_inc(step, 1)
        dve.wait_ge(step, count[0])
    return link


class TopTwoRouter:
    pack, squash, experts = "l0f", ACT.Copy, 8

    def __init__(self, g):
        self.g = g

    def scalar(self, nc, act, step):
        act.wait_ge(step, 5)
        nc.scalar.activation(self.e[:], self.e[:], ACT.Exp).then_inc(step, 1)

    def vector(self, nc, dve, step, sb, scores, weights):
        link = linked(dve, step)
        top, (first, second) = chosen(nc, link, sb, self.g, "r_e", scores, 2, 8)
        den = sb("r_den", [P, TILES])
        wide = [P, TILES, 8]
        link(nc.vector.tensor_tensor(self.e[:], top[:, :, 1], top[:, :, 0], ALU.subtract))
        dve.wait_ge(step, 6)
        nc.vector.tensor_scalar(den[:], self.e[:], 1.0, None, ALU.add).then_inc(step, 1)
        dve.wait_ge(step, 7)
        nc.vector.reciprocal(den[:], den[:]).then_inc(step, 1)
        dve.wait_ge(step, 8)
        nc.vector.tensor_tensor(self.e[:], self.e[:], den[:], ALU.mult).then_inc(step, 1)
        nc.vector.tensor_tensor(first[:], first[:], den[:].unsqueeze(2).broadcast_to(wide), ALU.mult).then_inc(step, 1)
        dve.wait_ge(step, 10)
        nc.vector.tensor_tensor(second[:], second[:], self.e[:].unsqueeze(2).broadcast_to(wide), ALU.mult).then_inc(step, 1)
        dve.wait_ge(step, 11)
        return nc.vector.tensor_tensor(weights[:], first[:], second[:], ALU.add)


class GroupedRouter:
    pack, squash, experts = "l1f", ACT.Sigmoid, 16
    SCALE, TINY = 2.5, 1e-20

    def __init__(self, g):
        self.g = g

    def scalar(self, nc, act, step):
        pass

    def vector(self, nc, dve, step, sb, scores, weights):
        link = linked(dve, step)
        wide = [P, TILES, 16]
        biased = sb("r_biased", wide)
        hi = sb("r_hi", [P, TILES, 4, 2])
        lo = sb("r_lo", [P, TILES, 4, 2])
        best = sb("r_best", [P, TILES, 4])
        next1 = sb("r_next1", [P, TILES, 4])
        next2 = sb("r_next2", [P, TILES, 4])
        group = sb("r_group", [P, TILES, 8])
        total = sb("r_total", [P, TILES])
        tt = nc.vector.tensor_tensor
        link(nc.vector.memset(group[:], LOWEST))
        link(tt(biased[:], scores[:], self.g.w["l1f"]["e_bias"].unsqueeze(1).broadcast_to(wide), ALU.add))
        pairs = biased[:].rearrange("p t (q a) -> p t q a", a=2)
        pair = lambda x: x[:].rearrange("p t q a -> p t (q a)")
        link(tt(pair(hi), pairs[:, :, :, 0], pairs[:, :, :, 1], ALU.max))
        link(tt(pair(lo), pairs[:, :, :, 0], pairs[:, :, :, 1], ALU.min))
        link(tt(best[:], hi[:, :, :, 0], hi[:, :, :, 1], ALU.max))
        link(tt(next1[:], hi[:, :, :, 0], hi[:, :, :, 1], ALU.min))
        link(tt(next2[:], lo[:, :, :, 0], lo[:, :, :, 1], ALU.max))
        link(tt(next1[:], next1[:], next2[:], ALU.max))
        link(tt(group[:, :, 0:4], best[:], next1[:], ALU.add))
        _, (g1, g2) = chosen(nc, link, sb, self.g, "r_g", group, 2, 4)
        link(tt(g1[:], g1[:], g2[:], ALU.add))
        quads = lambda x: x[:].rearrange("p t (q a) -> p (t q) a", a=4)
        link(tt(quads(biased), quads(biased), g1[:].rearrange("p t q -> p (t q)").unsqueeze(2).broadcast_to([P, TILES * 4, 4]),
                ALU.mult))
        _, hot = chosen(nc, link, sb, self.g, "r_e", biased, 4, 16)
        for other in hot[1:]:
            link(tt(hot[0][:], hot[0][:], other[:], ALU.add))
        link(tt(weights[:], scores[:], hot[0][:], ALU.mult))
        link(nc.vector.tensor_reduce(total[:], weights[:], AX.X, ALU.add))
        link(nc.vector.tensor_scalar(total[:], total[:], self.TINY, None, ALU.add))
        link(nc.vector.reciprocal(total[:], total[:]))
        link(nc.vector.tensor_scalar(total[:], total[:], self.SCALE, None, ALU.mult))
        return tt(weights[:], weights[:], total[:].unsqueeze(2).broadcast_to(wide), ALU.mult)


def gated_experts(g, router, pick, tiles):
    nc, bank, w = g.nc, g.bank, g.w[router.pack]
    with ExitStack() as ctx:
        g.count += 1
        g.rows = ctx.enter_context(nc.sbuf_tensor(f"rows_{g.count}", [P, TOKENS], BF16))
        router.e = ctx.enter_context(nc.sbuf_tensor(f"router_e_{g.count}", [P, TILES], F32))
        spread_weights(g, router, router.experts)
        with stage(g, "gate_ready up_ready weight_ready gated product_done hidden_ready down_done out_free") as (sb, sems):
            gate_ready, up_ready, weight_ready, gated, product_done, hidden_ready, down_done, out_free = sems
            gate = sb("f_gate", [P, 2, CHUNK])
            prod = sb("f_prod", [P, 2, CHUNK])
            hid = sb("f_hid", [P, 3, CHUNK])
            with nc.Block() as block:
                @block.tensor
                def _(pe):
                    with pe.Fori(0, CHUNKS) as b:
                        x = chunk(g.normed, b)
                        for m in range(tiles + 1):
                            if m < tiles:
                                if m >= 2:
                                    pe.wait_ge(gated, b * tiles + m - 1)
                                nc.tensor.matmul(bank[m % 2][:, :], w["gate"][:, m * P:(m + 1) * P], x,
                                                 start=True, stop=True).then_inc(gate_ready, 1)
                                if m >= 2:
                                    pe.wait_ge(product_done, b * tiles + m - 1)
                                nc.tensor.matmul(bank[2 + m % 2][:, :], w["up"][:, m * P:(m + 1) * P], x,
                                                 start=True, stop=True).then_inc(up_ready, 1)
                                if m >= 2:
                                    pe.wait_ge(hidden_ready, b * tiles + m - 1)
                                nc.tensor.matmul(bank[4 + m % 2][:, :], pick[0:97, m, :], chunk(g.rows, b)[0:97],
                                                 start=True, stop=True).then_inc(weight_ready, 1)
                            if m >= 1:
                                if m == 1:
                                    pe.wait_ge(out_free, b + 1)
                                pe.wait_ge(hidden_ready, b * tiles + m)
                                nc.tensor.matmul(bank[6][:, :], w["down"][:, (m - 1) * P:m * P], hid[:, (m - 1) % 3, :],
                                                      start=(m == 1), stop=(m == tiles)).then_inc(down_done, 1)

                @block.scalar
                def _(act):
                    with act.Fori(0, CHUNKS) as b:
                        for m in range(tiles):
                            act.wait_ge(gate_ready, b * tiles + m + 1)
                            if m >= 2:
                                act.wait_ge(product_done, b * tiles + m - 1)
                            nc.scalar.activation(gate[:, m % 2, :], bank[m % 2][:, :], ACT.Silu).then_inc(gated, 1)

                @block.vector
                def _(dve):
                    nc.vector.memset(g.mark, 0.0).then_inc(out_free, 1)
                    with dve.Fori(0, CHUNKS) as b:
                        for m in range(tiles):
                            dve.wait_ge(up_ready, b * tiles + m + 1)
                            dve.wait_ge(gated, b * tiles + m + 1)
                            nc.vector.tensor_tensor(prod[:, m % 2, :], gate[:, m % 2, :], bank[2 + m % 2][:, :],
                                                    ALU.mult).then_inc(product_done, 1)
                            dve.wait_ge(product_done, b * tiles + m + 1)
                            dve.wait_ge(weight_ready, b * tiles + m + 1)
                            if m >= 3:
                                dve.wait_ge(down_done, b * tiles + m - 2)
                            nc.vector.tensor_tensor(hid[:, m % 3, :], prod[:, m % 2, :], bank[4 + m % 2][:, :],
                                                    ALU.mult).then_inc(hidden_ready, 1)
                        dve.wait_ge(down_done, b * tiles + tiles)
                        nc.vector.tensor_tensor(chunk(g.resid, b), chunk(g.resid, b), bank[6][:, :], ALU.add).then_inc(out_free, 1)


def top_two_experts(g):
    gated_experts(g, TopTwoRouter(g), g.route0, 14)


def grouped_experts(g):
    gated_experts(g, GroupedRouter(g), g.route1, 9)


def plain_attention(g):
    nc, bank, w = g.nc, g.bank, g.w["l0b"]
    SCALE = P ** -0.5
    with stage(g, "proj_ready proj_kept vsum_ready score_ready max_ready negated exp_ready sum_inv row_ready diag_ready "
                  "spread_ready fc_ready fc_kept scaled h_ready mean_ready centred squared var_ready logged rstd_ready "
                  "normed affine resid_done") as (sb, sems):
        (proj_ready, proj_kept, vsum_ready, score_ready, max_ready, negated, exp_ready, sum_inv, row_ready, diag_ready,
         spread_ready, fc_ready, fc_kept, scaled, h_ready, mean_ready, centred, squared, var_ready, logged, rstd_ready,
         normed, affine, resid_done) = sems
        qk = sb("p_qk", [P, 2, CHUNK])
        vsum = sb("p_vsum", [P, 1])
        mx = sb("p_mx", [P, QT])
        exp = sb("p_exp", [P, CHUNK])
        total = sb("p_total", [P, QT])
        inv = sb("p_inv", [P, QT])
        diag = sb("p_diag", [P, QT, P])
        fc = sb("p_fc", [P, 1])
        h = sb("p_h", [P, CHUNK])
        sq = sb("p_sq", [P, CHUNK])
        rstd = sb("p_rstd", [P, CHUNK])
        with nc.Block() as block:
            @block.tensor
            def _(pe):
                pe.wait_ge(g.loaded["l0b"], 16)
                with pe.Fori(0, CHUNKS) as b:
                    pe.wait_ge(resid_done, b + 1)
                    for i in range(3):
                        nc.tensor.matmul(bank[i][:, :], w["wqkv"][:, i * P:(i + 1) * P], chunk(g.normed, b),
                                         start=True, stop=True).then_inc(proj_ready, 1)
                    pe.wait_ge(proj_kept, b * 2 + 2)
                    for qt in range(QT):
                        mm = nc.tensor.matmul(bank[4 + qt][:, :], qk[:, 0, qt * P:(qt + 1) * P], qk[:, 1, :], start=True, stop=True)
                    mm.then_inc(score_ready, 1)
                    pe.wait_ge(vsum_ready, b + 1)
                    nc.tensor.matmul(bank[3][:, 0:1], w["wfc"], vsum[:, :], start=True, stop=True).then_inc(fc_ready, 1)
                    pe.wait_ge(diag_ready, b * QT + QT)
                    for qt in range(QT):
                        mm = nc.tensor.matmul(bank[0][:, qt * P:(qt + 1) * P], g.ones, diag[:, qt, :], start=True, stop=True)
                    mm.then_inc(spread_ready, 1)
                    pe.wait_ge(h_ready, b + 1)
                    nc.tensor.matmul(bank[1][:, :], g.mean_of, h[:, :], start=True, stop=True).then_inc(mean_ready, 1)
                    pe.wait_ge(squared, b + 1)
                    nc.tensor.matmul(bank[2][:, :], g.mean_of, sq[:, :], start=True, stop=True).then_inc(var_ready, 1)

            @block.scalar
            def _(act):
                with act.Fori(0, CHUNKS) as b:
                    for i in range(2):
                        act.wait_ge(proj_ready, b * 3 + i + 1)
                        nc.scalar.copy(qk[:, i, :], bank[i][:, :]).then_inc(proj_kept, 1)
                    act.wait_ge(negated, b + 1)
                    for qt in range(QT):
                        if qt >= 1:
                            act.wait_ge(exp_ready, b * QT + qt)
                        nc.scalar.activation(exp[:, :], bank[4 + qt][:, :], ACT.Exp, bias=mx[:, qt:qt + 1], scale=SCALE,
                                             accum_out=total[:, qt:qt + 1]).then_inc(exp_ready, 1)
                    act.wait_ge(fc_ready, b + 1)
                    nc.scalar.copy(fc[:, :], bank[3][:, 0:1]).then_inc(fc_kept, 1)
                    act.wait_ge(centred, b + 1)
                    nc.scalar.activation(sq[:, :], h[:, :], ACT.Square).then_inc(squared, 1)
                    act.wait_ge(var_ready, b + 1)
                    nc.scalar.activation(rstd[:, :], bank[2][:, :], ACT.Ln, bias=g.eps5).then_inc(logged, 1)
                    act.wait_ge(logged, b + 1)
                    nc.scalar.activation(rstd[:, :], rstd[:, :], ACT.Exp, scale=-0.5).then_inc(rstd_ready, 1)

            @block.vector
            def _(dve):
                nc.vector.memset(g.mark, 0.0).then_inc(resid_done, 1)
                with dve.Fori(0, CHUNKS) as b:
                    dve.wait_ge(proj_ready, b * 3 + 3)
                    nc.vector.tensor_reduce(vsum[:, :], bank[2][:, :], AX.X, ALU.add).then_inc(vsum_ready, 1)
                    dve.wait_ge(score_ready, b + 1)
                    nc.vector.tensor_reduce(mx[:, :], g.banks[4:8, 0:CHUNK], AX.X, ALU.max).then_inc(max_ready, 1)
                    dve.wait_ge(max_ready, b + 1)
                    nc.vector.tensor_scalar(mx[:, :], mx[:, :], -SCALE, None, ALU.mult).then_inc(negated, 1)
                    dve.wait_ge(exp_ready, b * QT + QT)
                    nc.vector.reciprocal(inv[:, :], total[:, :]).then_inc(sum_inv, 1)
                    dve.wait_ge(sum_inv, b + 1)
                    nc.vector.tensor_tensor(inv[:, :], inv[:, :], total[:, :], ALU.mult).then_inc(row_ready, 1)
                    dve.wait_ge(row_ready, b + 1)
                    for qt in range(QT):
                        nc.vector.tensor_scalar(diag[:, qt, :], g.ident, inv[:, qt:qt + 1], None, ALU.mult).then_inc(diag_ready, 1)
                    dve.wait_ge(spread_ready, b + 1)
                    dve.wait_ge(fc_kept, b + 1)
                    nc.vector.tensor_scalar(h[:, :], bank[0][:, :], fc[:, :], w["b_fc"], ALU.mult, ALU.add).then_inc(scaled, 1)
                    dve.wait_ge(scaled, b + 1)
                    nc.vector.tensor_tensor(h[:, :], h[:, :], chunk(g.normed, b), ALU.add).then_inc(h_ready, 1)
                    dve.wait_ge(mean_ready, b + 1)
                    nc.vector.tensor_tensor(h[:, :], h[:, :], bank[1][:, :], ALU.subtract).then_inc(centred, 1)
                    dve.wait_ge(rstd_ready, b + 1)
                    dve.wait_ge(centred, b + 1)
                    nc.vector.tensor_tensor(h[:, :], h[:, :], rstd[:, :], ALU.mult).then_inc(normed, 1)
                    dve.wait_ge(normed, b + 1)
                    nc.vector.tensor_scalar(h[:, :], h[:, :], w["gamma"], w["beta"], ALU.mult, ALU.add).then_inc(affine, 1)
                    dve.wait_ge(affine, b + 1)
                    nc.vector.tensor_tensor(chunk(g.resid, b), chunk(g.resid, b), h[:, :], ALU.add).then_inc(resid_done, 1)


def recurrent_heads(g):
    nc, bank, w = g.nc, g.bank, g.w["l1a"]
    PAIRS, S, SPAN, BLOCK = 8, 64, 128, 8
    SPANS, TURNS = TIME // SPAN, SPAN // (2 * BLOCK)
    with stage(g, "weights_bounded squared ms_ready logged rms_ready scaled x_ready cleared0 cleared1 laid_free laid "
                  "drive0 drive1 state0 state1 carried mix_ready mix_kept out_ready biased resid_done") as (sb, sems):
        (weights_bounded, squared, ms_ready, logged, rms_ready, scaled, x_ready, cleared0, cleared1, laid_free, laid,
         drive0, drive1, state0, state1, carried, mix_ready, mix_kept, out_ready, biased, resid_done) = sems
        drive, state = (drive0, drive1), (state0, state1)
        at = sb("h_at", [P, PAIRS, S])
        sq = sb("h_sq", [P, TOKENS])
        rms = sb("h_rms", [P, TOKENS])
        xt = sb("h_xt", [P, TIME, BATCH])
        lay = sb("h_lay", [P, 2, 2, BLOCK, 32])
        hist = sb("h_hist", [P, SPAN + 1, PAIRS, 8])
        mix = sb("h_mix", [P, BATCH, TIME])

        with nc.Block() as block:
            @block.tensor
            def _(pe):
                pe.wait_ge(g.loaded["l1a"], 16)
                for j in range(CHUNKS):
                    pe.wait_ge(squared, j + 1)
                    nc.tensor.matmul(bank[j][:, :], g.mean_of, fixed(sq, j), start=True, stop=True).then_inc(ms_ready, 1)
                pe.wait_ge(weights_bounded, 1)
                pe.wait_ge(cleared0, 1)
                pe.wait_ge(cleared1, 1)
                pe.wait_ge(rms_ready, CHUNKS)
                with pe.Fori(0, SPANS) as c:
                    with pe.Fori(0, TURNS) as i:
                        turn = c * TURNS + i

                        def lay_inputs(blk):
                            pe.wait_ge(laid, turn * 2 + blk + 1)
                            for grp in range(2):
                                mm = nc.tensor.matmul(bank[2 * blk + grp][0:S, 0:BLOCK * 32], w["b"],
                                                      lay[:, blk, grp, :, :].rearrange("p s c -> p (s c)"), start=True, stop=True)
                            mm.then_inc(laid_free, 1)

                        lay_inputs(0)
                        pe.wait_ge(carried, c + 1)
                        for s in range(2 * BLOCK):
                            if s == 2:
                                lay_inputs(1)
                            for grp in range(2):
                                pe.wait_ge(state[grp], turn * 2 * BLOCK + s + 1)
                                out = bank[2 * (s // BLOCK) + grp]
                                for p in range(4):
                                    col = s % BLOCK * 32 + 8 * p
                                    mm = nc.tensor.matmul(
                                        out[0:S, col:col + 8], at[:, 4 * grp + p, :],
                                        hist[:, bass.ds(i * 2 * BLOCK + s, 1), 4 * grp + p, :].rearrange("p o e -> p (o e)"),
                                        start=False, stop=True, skip_group_check=True)
                                mm.then_inc(drive[grp], 1)
                    pe.wait_ge(state0, c * SPAN + SPAN + 1)
                    pe.wait_ge(state1, c * SPAN + SPAN + 1)
                    pe.wait_ge(mix_kept, c + 1)
                    for n in range(2 * PAIRS):
                        p, side = n // 2, n % 2
                        mm = nc.tensor.matmul(bank[4][:, :], w["c"][:, p * P:(p + 1) * P],
                                              hist[:, 1:SPAN + 1, p, 4 * side:4 * side + 4],
                                              start=(n == 0), stop=(n == 2 * PAIRS - 1))
                    mm.then_inc(mix_ready, 1)
                pe.wait_ge(mix_kept, SPANS + 1)
                for j in range(CHUNKS):
                    nc.tensor.matmul(bank[j][:, :], w["out"], mix[:, j, :], start=True, stop=True).then_inc(out_ready, 1)

            @block.scalar
            def _(act):
                act.wait_ge(g.loaded["l1a"], 16)
                for j in range(CHUNKS):
                    nc.scalar.activation(fixed(sq, j), fixed(g.normed, j), ACT.Square).then_inc(squared, 1)
                for j in range(CHUNKS):
                    act.wait_ge(ms_ready, j + 1)
                    nc.scalar.activation(fixed(rms, j), bank[j][:, :], ACT.Ln, bias=g.eps4).then_inc(logged, 1)
                    act.wait_ge(logged, j + 1)
                    nc.scalar.activation(fixed(rms, j), fixed(rms, j), ACT.Exp, scale=-0.5).then_inc(rms_ready, 1)
                nc.scalar.activation(at[:].rearrange("p a t -> p (a t)"), w["a"], ACT.Tanh).then_inc(weights_bounded, 1)
                with act.Fori(0, SPANS) as c:
                    with act.Fori(0, TURNS) as i:
                        for s in range(2 * BLOCK):
                            step = (c * TURNS + i) * 2 * BLOCK + s
                            for grp in range(2):
                                act.wait_ge(drive[grp], step + 1)
                                v = bank[2 * (s // BLOCK) + grp][0:S, s % BLOCK * 32:s % BLOCK * 32 + 32].rearrange(
                                    "s (p h b) -> s p h b", h=2, b=BATCH)
                                slot = bass.ds(i * 2 * BLOCK + s + 1, 1)
                                pairs = slice(4 * grp, 4 * grp + 4)
                                nc.scalar.activation(hist[0:S, slot, pairs, 0:4].rearrange("s o p b -> s (o p) b"),
                                                     v[:, :, 0, :], ACT.Tanh)
                                nc.scalar.activation(hist[S:P, slot, pairs, 4:8].rearrange("s o p b -> s (o p) b"),
                                                     v[:, :, 1, :], ACT.Tanh).then_inc(state[grp], 1)
                    act.wait_ge(state0, c * SPAN + SPAN + 1)
                    act.wait_ge(state1, c * SPAN + SPAN + 1)
                    nc.scalar.copy(hist[:, 0, :, :], hist[:, SPAN, :, :]).then_inc(carried, 1)

            @block.gpsimd
            def _(pool):
                nc.gpsimd.memset(hist[:, 0:SPAN // 2, :, :], 0.0).then_inc(cleared0, 1)
                pool.wait_ge(cleared0, 1)
                for n in range(2):
                    nc.gpsimd.memset(g.mark2[:, n:n + 1], 0.0).then_inc(laid_free, 1)
                pool.wait_ge(x_ready, CHUNKS)
                with pool.Fori(0, TIME // (2 * BLOCK)) as i:
                    for blk in range(2):
                        pool.wait_ge(laid_free, i * 2 + blk + 1)
                        x = xt[:, bass.ds(i * 2 * BLOCK + blk * BLOCK, BLOCK), :]
                        for grp in range(2):
                            own = g.head_of[:, 8 * grp:8 * grp + 8]
                            put = nc.gpsimd.tensor_tensor(
                                lay[:, blk, grp, :, :].rearrange("p s (h b) -> p s h b", b=BATCH),
                                own.unsqueeze(1).unsqueeze(3).broadcast_to([P, BLOCK, 8, BATCH]),
                                x.unsqueeze(2).broadcast_to([P, BLOCK, 8, BATCH]), ALU.mult)
                        put.then_inc(laid, 1)

            @block.vector
            def _(dve):
                nc.vector.memset(hist[:, SPAN // 2:SPAN + 1, :, :], 0.0).then_inc(cleared1, 1)
                nc.vector.memset(g.mark, 0.0).then_inc(state0, 1)
                dve.wait_ge(state0, 1)
                nc.vector.memset(g.mark, 0.0).then_inc(state1, 1)
                dve.wait_ge(state1, 1)
                nc.vector.memset(g.mark, 0.0).then_inc(carried, 1)
                dve.wait_ge(carried, 1)
                nc.vector.memset(g.mark, 0.0).then_inc(mix_kept, 1)
                dve.wait_ge(g.loaded["l1a"], 16)
                for j in range(CHUNKS):
                    dve.wait_ge(rms_ready, j + 1)
                    nc.vector.scalar_tensor_tensor(out=xt[:, :, j], in0=fixed(g.normed, j), scalar=w["norm_w"],
                                                   in1=fixed(rms, j), op0=ALU.mult, op1=ALU.mult).then_inc(x_ready, 1)
                dve.wait_ge(x_ready, CHUNKS)
                with dve.Fori(0, SPANS) as c:
                    dve.wait_ge(mix_ready, c + 1)
                    nc.vector.scalar_tensor_tensor(
                        out=mix[:, :, bass.ds(c * SPAN, SPAN)].rearrange("p b t -> p t b"),
                        in0=xt[:, bass.ds(c * SPAN, SPAN), :], scalar=w["skip"],
                        in1=bank[4][:, :].rearrange("p (t b) -> p t b", b=BATCH), op0=ALU.mult, op1=ALU.add).then_inc(mix_kept, 1)
                for j in range(CHUNKS):
                    nc.vector.tensor_tensor(fixed(g.resid, j), fixed(g.resid, j), fixed(g.normed, j), ALU.add).then_inc(biased, 1)
                for j in range(CHUNKS):
                    dve.wait_ge(out_ready, j + 1)
                    dve.wait_ge(biased, j + 1)
                    nc.vector.scalar_tensor_tensor(out=fixed(g.resid, j), in0=bank[j][:, :], scalar=w["b_out"],
                                                   in1=fixed(g.resid, j), op0=ALU.add, op1=ALU.add).then_inc(resid_done, 1)


def cumulative_attention(g):
    nc, bank, w = g.nc, g.bank, g.w["l1b"]
    EPS = 1e-3
    with stage(g, "proj_ready shifted lowered exp_ready v_kept raised kv_done ksum kvsum weighed den_ready clipped inverted "
                  "numer y_ready out_ready resid_done ones_set") as (sb, sems):
        (proj_ready, shifted, lowered, exp_ready, v_kept, raised, kv_done, ksum, kvsum, weighed, den_ready, clipped, inverted,
         numer, y_ready, out_ready, resid_done, ones_set) = sems
        one = sb("c_one", [P, CHUNK])
        t = sb("c_t", [P, 2, CHUNK])
        e = sb("c_e", [P, 2, CHUNK])
        qk = sb("c_qk", [P, 2, CHUNK])
        v = sb("c_v", [P, CHUNK])
        kc = sb("c_kc", [P, CHUNK])
        kvc = sb("c_kvc", [P, CHUNK])
        r = sb("c_r", [P, CHUNK])
        with nc.Block() as block:
            @block.tensor
            def _(pe):
                pe.wait_ge(g.loaded["l1b"], 16)
                with pe.Fori(0, CHUNKS) as b:
                    pe.wait_ge(resid_done, b + 1)
                    for i in range(3):
                        nc.tensor.matmul(bank[i][:, :], w["wqkv"][:, i * P:(i + 1) * P], chunk(g.normed, b),
                                         start=True, stop=True).then_inc(proj_ready, 1)
                    pe.wait_ge(weighed, b + 1)
                    nc.tensor.matmul(bank[3][:, :], g.same8, r[:, :], start=True, stop=True).then_inc(den_ready, 1)
                    pe.wait_ge(y_ready, b + 1)
                    nc.tensor.matmul(bank[4][:, :], w["wproj"], v[:, :], start=True, stop=True).then_inc(out_ready, 1)

            @block.scalar
            def _(act):
                act.wait_ge(g.loaded["l1b"], 16)
                with act.Fori(0, CHUNKS) as b:
                    for i in range(2):
                        act.wait_ge(lowered, b * 2 + i + 1)
                        nc.scalar.activation(e[:, i, :], e[:, i, :], ACT.Exp).then_inc(exp_ready, 1)
                    act.wait_ge(proj_ready, b * 3 + 3)
                    nc.scalar.activation(v[:, :], bank[2][:, :], ACT.Identity, bias=w["bqkv"][:, 2:3]).then_inc(v_kept, 1)

            @block.vector
            def _(dve):
                dve.wait_ge(g.loaded["l1b"], 16)
                nc.vector.memset(one[:, :], 1.0).then_inc(ones_set, 1)
                nc.vector.memset(g.mark, 0.0).then_inc(resid_done, 1)
                dve.wait_ge(ones_set, 1)
                with dve.Fori(0, CHUNKS) as b:
                    for i in range(2):
                        dve.wait_ge(proj_ready, b * 3 + i + 1)
                        nc.vector.tensor_scalar(t[:, i, :], bank[i][:, :], w["bqkv"][:, i:i + 1], w["scale"], ALU.add,
                                                ALU.mult).then_inc(shifted, 1)
                        dve.wait_ge(shifted, b * 2 + i + 1)
                        nc.vector.tensor_scalar(e[:, i, :], t[:, i, :], 0.0, None, ALU.min).then_inc(lowered, 1)
                    for i in range(2):
                        dve.wait_ge(exp_ready, b * 2 + i + 1)
                        nc.vector.scalar_tensor_tensor(out=qk[:, i, :], in0=t[:, i, :], scalar=0.0, in1=e[:, i, :],
                                                       op0=ALU.max, op1=ALU.add).then_inc(raised, 1)
                    dve.wait_ge(raised, b * 2 + 2)
                    nc.vector.tensor_tensor_scan(kc[:, :], one[:, :], qk[:, 1, :], 0.0, ALU.mult, ALU.add).then_inc(ksum, 1)
                    dve.wait_ge(v_kept, b + 1)
                    nc.vector.tensor_tensor(t[:, 0, :], qk[:, 1, :], v[:, :], ALU.mult).then_inc(kv_done, 1)
                    dve.wait_ge(ksum, b + 1)
                    nc.vector.tensor_tensor(r[:, :], qk[:, 0, :], kc[:, :], ALU.mult).then_inc(weighed, 1)
                    dve.wait_ge(kv_done, b + 1)
                    nc.vector.tensor_tensor_scan(kvc[:, :], one[:, :], t[:, 0, :], 0.0, ALU.mult, ALU.add).then_inc(kvsum, 1)
                    dve.wait_ge(den_ready, b + 1)
                    nc.vector.tensor_scalar(r[:, :], bank[3][:, :], EPS, None, ALU.max).then_inc(clipped, 1)
                    dve.wait_ge(clipped, b + 1)
                    nc.vector.reciprocal(r[:, :], r[:, :]).then_inc(inverted, 1)
                    dve.wait_ge(kvsum, b + 1)
                    nc.vector.tensor_tensor(kvc[:, :], kvc[:, :], qk[:, 0, :], ALU.mult).then_inc(numer, 1)
                    dve.wait_ge(numer, b + 1)
                    dve.wait_ge(inverted, b + 1)
                    nc.vector.tensor_tensor(v[:, :], kvc[:, :], r[:, :], ALU.mult).then_inc(y_ready, 1)
                    dve.wait_ge(out_ready, b + 1)
                    nc.vector.scalar_tensor_tensor(out=chunk(g.resid, b), in0=bank[4][:, :], scalar=w["bproj"],
                                                   in1=chunk(g.resid, b), op0=ALU.add, op1=ALU.add).then_inc(resid_done, 1)


def dense_ffn(g):
    nc, bank, w = g.nc, g.bank, g.w["l2f"]
    HID = 4
    with stage(g, "gate_ready gated up_ready h_ready act_ready act_done out_ready resid_done") as (sb, sems):
        gate_ready, gated, up_ready, h_ready, act_ready, act_done, out_ready, resid_done = sems
        gate = sb("d_gate", [P, 2, CHUNK])
        h = sb("d_h", [P, 3, HID, CHUNK])
        with nc.Block() as block:
            @block.tensor
            def _(pe):
                pe.wait_ge(g.loaded["l2f"], 16)
                with pe.Fori(0, CHUNKS) as b:
                    for m in range(HID):
                        if m >= 2:
                            pe.wait_ge(gated, b * HID + m - 1)
                        nc.tensor.matmul(bank[m % 2][:, :], w["w1"][:, m * P:(m + 1) * P], chunk(g.normed, b),
                                         start=True, stop=True).then_inc(gate_ready, 1)
                        if m >= 2:
                            pe.wait_ge(h_ready, b * HID + m - 1)
                        nc.tensor.matmul(bank[2 + m % 2][:, :], w["w2"][:, m * P:(m + 1) * P], chunk(g.normed, b),
                                         start=True, stop=True).then_inc(up_ready, 1)
                    for layer, name in ((0, "h1"), (1, "h2")):
                        for m in range(HID):
                            n = layer * HID + m
                            if n >= 3:
                                pe.wait_ge(act_done, b * 2 * HID + n - 2)
                            for k in range(HID):
                                if layer == 0:
                                    pe.wait_ge(h_ready, b * HID + k + 1)
                                else:
                                    pe.wait_ge(act_done, b * 2 * HID + k + 1)
                                mm = nc.tensor.matmul(bank[4 + n % 3][:, :], w[name][:, k * CHUNK + m * P:k * CHUNK + (m + 1) * P],
                                                      h[:, layer, k, :], start=(k == 0), stop=(k == HID - 1))
                            mm.then_inc(act_ready, 1)
                    pe.wait_ge(resid_done, b + 1)
                    for k in range(HID):
                        pe.wait_ge(act_done, b * 2 * HID + HID + k + 1)
                        mm = nc.tensor.matmul(bank[7][:, :], w["w3"][:, k * P:(k + 1) * P], h[:, 2, k, :],
                                              start=(k == 0), stop=(k == HID - 1))
                    mm.then_inc(out_ready, 1)

            @block.scalar
            def _(act):
                act.wait_ge(g.loaded["l2f"], 16)
                with act.Fori(0, CHUNKS) as b:
                    for m in range(HID):
                        act.wait_ge(gate_ready, b * HID + m + 1)
                        if m >= 2:
                            act.wait_ge(h_ready, b * HID + m - 1)
                        nc.scalar.activation(gate[:, m % 2, :], bank[m % 2][:, :], ACT.Silu,
                                             scale=w["s1"][:, m:m + 1]).then_inc(gated, 1)
                    for n in range(2 * HID):
                        act.wait_ge(act_ready, b * 2 * HID + n + 1)
                        scale = w["sh1" if n < HID else "sh2"][:, n % HID:n % HID + 1]
                        nc.scalar.activation(h[:, 1 + n // HID, n % HID, :], bank[4 + n % 3][:, :], ACT.Gelu,
                                             scale=scale).then_inc(act_done, 1)

            @block.vector
            def _(dve):
                dve.wait_ge(g.loaded["l2f"], 16)
                nc.vector.memset(g.mark, 0.0).then_inc(resid_done, 1)
                with dve.Fori(0, CHUNKS) as b:
                    for m in range(HID):
                        dve.wait_ge(up_ready, b * HID + m + 1)
                        dve.wait_ge(gated, b * HID + m + 1)
                        nc.vector.scalar_tensor_tensor(out=h[:, 0, m, :], in0=bank[2 + m % 2][:, :], scalar=w["s2"][:, m:m + 1],
                                                       in1=gate[:, m % 2, :], op0=ALU.mult, op1=ALU.mult).then_inc(h_ready, 1)
                    dve.wait_ge(out_ready, b + 1)
                    nc.vector.scalar_tensor_tensor(out=chunk(g.resid, b), in0=bank[7][:, :], scalar=w["s3"],
                                                   in1=chunk(g.resid, b), op0=ALU.mult, op1=ALU.add).then_inc(resid_done, 1)


def selective_scan(g, pack, ranks):
    nc, bank, w = g.nc, g.bank, g.w[pack]
    N, TAPS, BR = 16, 4, len(ranks)
    ITEMS = 2 * N
    with stage(g, "decay_ready negated skip_ready cleared in_ready x_kept z_ready tap_done conv_done u_ready dt_ready bc_ready dt_kept "
                  "hi_kept rest1 mid_kept mid_moved rest2 lo_kept delta_ready abs_done pos_done exp_done grown log_done inv_done "
                  "lost lost_part delta_sum delta_done du_done y_zeroed b_spread c_spread b_kept da_ready dbu_ready scan_done "
                  "term_ready y_added skipped gated out_ready resid_done") as (sb, sems):
        (decay_ready, negated, skip_ready, cleared, in_ready, x_kept, z_ready, tap_done, conv_done, u_ready, dt_ready, bc_ready, dt_kept,
         hi_kept, rest1, mid_kept, mid_moved, rest2, lo_kept, delta_ready, abs_done, pos_done, exp_done, grown, log_done, inv_done,
         lost, lost_part, delta_sum, delta_done, du_done, y_zeroed, b_spread, c_spread, b_kept, da_ready, dbu_ready, scan_done,
         term_ready, y_added, skipped, gated, out_ready, resid_done) = sems
        decay = sb("s_decay", [P, BR, 2 * N])
        skip = sb("s_skip", [P, 2])
        xp = sb("s_xp", [P, 2, TAPS - 1 + CHUNK])
        conv = sb("s_conv", [P, 2, 2, CHUNK])
        u = sb("s_u", [P, 2, CHUNK])
        z = sb("s_z", [P, 2, CHUNK])
        dt = sb("s_dt", [64, CHUNK])
        bc = sb("s_bc", [96, CHUNK], BF16)
        mid = sb("s_mid", [32, CHUNK], BF16)
        r1 = sb("s_r1", [32, CHUNK])
        mag = sb("s_mag", [P, 2, CHUNK])
        grow = sb("s_grow", [P, 2, CHUNK])
        delta = sb("s_delta", [P, 2, CHUNK])
        du = sb("s_du", [P, 2, CHUNK])
        zero = sb("s_zero", [P, CHUNK], BF16)
        bb = sb("s_bb", [P, 3, CHUNK])
        da = sb("s_da", [P, 4, CHUNK])
        dbu = sb("s_dbu", [P, 4, CHUNK])
        hh = sb("s_hh", [P, 2, CHUNK])
        term = sb("s_term", [P, 4, CHUNK])
        y = sb("s_y", [P, 2, CHUNK])
        log, inv, pos = conv[:, 0, :, :], conv[:, 1, :, :], y
        halves = g.banks[0:2, 0:CHUNK]
        with nc.Block() as block:
            @block.tensor
            def _(pe):
                pe.wait_ge(g.loaded[pack], 16)
                pe.wait_ge(cleared, 2)
                with pe.Fori(0, CHUNKS) as b:
                    pe.wait_ge(resid_done, b + 1)
                    for m in range(4):
                        nc.tensor.matmul(bank[m][:, :], w["in"][:, m * P:(m + 1) * P], chunk(g.normed, b),
                                         start=True, stop=True).then_inc(in_ready, 1)
                    for half in range(2):
                        mm = nc.tensor.matmul(bank[6 + half][:, :], g.ident_bf, zero[:, :], start=True, stop=True)
                    for r, rank in enumerate(ranks):
                        turn = b * BR + r
                        for half in range(2):
                            pe.wait_ge(u_ready, b * 2 + half + 1)
                            mm = nc.tensor.matmul(bank[4][0:rank, :], w[f"xdt{r}"][:, half * rank:(half + 1) * rank], u[:, half, :],
                                                  start=(half == 0), stop=(half == 1))
                        mm.then_inc(dt_ready, 1)
                        for half in range(2):
                            mm = nc.tensor.matmul(bank[5][0:32, :], w[f"xbc{r}"][:, half * 32:(half + 1) * 32], u[:, half, :],
                                                  start=(half == 0), stop=(half == 1))
                        mm.then_inc(bc_ready, 1)
                        pe.wait_ge(dt_kept, turn + 1)
                        for half in range(2):
                            nc.tensor.matmul(bank[half][:, :], w[f"dtw{r}"][:, half * P:(half + 1) * P], dt[0:rank, :],
                                             start=True, stop=True).then_inc(delta_ready, 1)
                        pe.wait_ge(hi_kept, turn + 1)
                        pe.wait_ge(mid_moved, turn + 1)
                        pe.wait_ge(lo_kept, turn + 1)
                        pe.wait_ge(abs_done, turn * 2 + 2)
                        pe.wait_ge(pos_done, turn * 2 + 2)
                        pe.wait_ge(z_ready, b * 2 + 2)
                        for n in range(N + 2):
                            if n < N:
                                if n >= 2:
                                    pe.wait_ge(b_kept, turn * N + n - 1)
                                nc.tensor.matmul(bank[n % 2][:, :], g.pick_b[0:96, n, :], bc[:, :],
                                                 start=True, stop=True).then_inc(b_spread, 1)
                                if n >= 2:
                                    pe.wait_ge(term_ready, turn * ITEMS + 2 * n - 2)
                                nc.tensor.matmul(bank[2 + n % 2][:, :], g.pick_c[0:96, n, :], bc[:, :],
                                                 start=True, stop=True).then_inc(c_spread, 1)
                            if n >= 2:
                                for half in range(2):
                                    i = 2 * (n - 2) + half
                                    pe.wait_ge(term_ready, turn * ITEMS + i + 1)
                                    nc.tensor.matmul(bank[6 + half][:, :], g.ident if r == 0 else g.minus, term[:, i % 4, :],
                                                     start=False, stop=True, skip_group_check=True).then_inc(y_added, 1)
                    for half in range(2):
                        pe.wait_ge(gated, b * 2 + half + 1)
                        mm = nc.tensor.matmul(bank[4][:, :], w["out"][:, half * P:(half + 1) * P], y[:, half, :],
                                              start=(half == 0), stop=(half == 1))
                    mm.then_inc(out_ready, 1)

            @block.scalar
            def _(act):
                act.wait_ge(g.loaded[pack], 16)
                for r in range(BR):
                    nc.scalar.activation(decay[:, r, :], w[f"alog{r}"], ACT.Exp).then_inc(decay_ready, 1)
                act.wait_ge(negated, 1)
                with act.Fori(0, CHUNKS) as b:
                    for half in range(2):
                        act.wait_ge(in_ready, b * 4 + half + 1)
                        nc.scalar.copy(xp[:, half, TAPS - 1:TAPS - 1 + CHUNK], bank[half][:, :]).then_inc(x_kept, 1)
                    for half in range(2):
                        act.wait_ge(in_ready, b * 4 + half + 3)
                        nc.scalar.activation(z[:, half, :], bank[2 + half][:, :], ACT.Silu).then_inc(z_ready, 1)
                    for half in range(2):
                        act.wait_ge(conv_done, b * 2 + half + 1)
                        nc.scalar.activation(u[:, half, :], conv[:, half, 1, :], ACT.Silu).then_inc(u_ready, 1)
                    for r, rank in enumerate(ranks):
                        turn = b * BR + r
                        act.wait_ge(dt_ready, turn + 1)
                        nc.scalar.copy(dt[0:rank, :], bank[4][0:rank, :]).then_inc(dt_kept, 1)
                        act.wait_ge(bc_ready, turn + 1)
                        nc.scalar.copy(bc[0:32, :], bank[5][0:32, :]).then_inc(hi_kept, 1)
                        for half in range(2):
                            act.wait_ge(delta_ready, turn * 2 + half + 1)
                            nc.scalar.activation(mag[:, half, :], bank[half][:, :], ACT.Abs,
                                                 bias=w[f"dtb{r}"][:, half:half + 1]).then_inc(abs_done, 1)
                        act.wait_ge(abs_done, turn * 2 + 2)
                        nc.scalar.activation(mag[:], mag[:], ACT.Exp, scale=-1.0).then_inc(exp_done, 1)
                        act.wait_ge(grown, turn + 1)
                        nc.scalar.activation(log, grow[:], ACT.Ln).then_inc(log_done, 1)
                        act.wait_ge(log_done, turn + 1)
                        nc.scalar.activation(inv, log, ACT.Exp, scale=-1.0).then_inc(inv_done, 1)
                        act.wait_ge(delta_done, turn + 1)
                        for n in range(N):
                            act.wait_ge(b_spread, turn * N + n + 1)
                            if n >= 3:
                                act.wait_ge(dbu_ready, turn * ITEMS + 2 * n - 4)
                            nc.scalar.copy(bb[:, n % 3, :], bank[n % 2][:, :]).then_inc(b_kept, 1)
                            for half in range(2):
                                i = 2 * n + half
                                if i >= 4:
                                    act.wait_ge(scan_done, turn * ITEMS + i - 3)
                                nc.scalar.activation(da[:, i % 4, :], delta[:, half, :], ACT.Exp,
                                                     scale=decay[:, r, half * N + n:half * N + n + 1]).then_inc(da_ready, 1)

            @block.gpsimd
            def _(pool):
                nc.gpsimd.memset(xp[:, :, 0:TAPS - 1], 0.0).then_inc(cleared, 1)
                nc.gpsimd.memset(zero[:, :], 0.0).then_inc(cleared, 1)
                with pool.Fori(0, CHUNKS) as b:
                    for r in range(BR):
                        turn = b * BR + r
                        pool.wait_ge(delta_done, turn + 1)
                        nc.gpsimd.tensor_tensor(du[:], delta[:], u[:], ALU.mult).then_inc(du_done, 1)
                        pool.wait_ge(du_done, turn + 1)
                        for i in range(ITEMS):
                            n, half = i // 2, i % 2
                            pool.wait_ge(b_kept, turn * N + n + 1)
                            if i >= 4:
                                pool.wait_ge(scan_done, turn * ITEMS + i - 3)
                            nc.gpsimd.tensor_tensor(dbu[:, i % 4, :], du[:, half, :], bb[:, n % 3, :], ALU.mult).then_inc(dbu_ready, 1)

            @block.vector
            def _(dve):
                dve.wait_ge(g.loaded[pack], 16)
                nc.vector.memset(g.mark, 0.0).then_inc(resid_done, 1)
                dve.wait_ge(decay_ready, BR)
                nc.vector.tensor_scalar(decay[:], decay[:], -1.0, None, ALU.mult).then_inc(negated, 1)
                if BR == 1:
                    nc.vector.tensor_copy(skip[:, :], w["d0"]).then_inc(skip_ready, 1)
                else:
                    nc.vector.tensor_tensor(skip[:, :], w["d0"], w["d1"], ALU.subtract).then_inc(skip_ready, 1)
                dve.wait_ge(skip_ready, 1)
                dve.wait_ge(cleared, 1)
                with dve.Fori(0, CHUNKS) as b:
                    for half in range(2):
                        dve.wait_ge(x_kept, b * 2 + half + 1)
                        tap = lambda k: w["conv"][:, half * TAPS + k:half * TAPS + k + 1]
                        nc.vector.tensor_scalar(conv[:, half, 0, :], xp[:, half, 0:CHUNK], tap(0), w["conv_b"][:, half:half + 1],
                                                ALU.mult, ALU.add).then_inc(tap_done, 1)
                        for k in range(1, TAPS):
                            dve.wait_ge(tap_done, (b * 2 + half) * (TAPS - 1) + k)
                            nc.vector.scalar_tensor_tensor(
                                out=conv[:, half, k % 2, :], in0=xp[:, half, k:k + CHUNK], scalar=tap(k),
                                in1=conv[:, half, (k - 1) % 2, :], op0=ALU.mult, op1=ALU.add).then_inc(
                                tap_done if k < TAPS - 1 else conv_done, 1)
                    for r in range(BR):
                        turn = b * BR + r
                        dve.wait_ge(hi_kept, turn + 1)
                        nc.vector.tensor_tensor(r1[:, :], bank[5][0:32, :], bc[0:32, :], ALU.subtract).then_inc(rest1, 1)
                        dve.wait_ge(rest1, turn + 1)
                        nc.vector.tensor_copy(mid[:, :], r1[:, :]).then_inc(mid_kept, 1)
                        dve.wait_ge(mid_kept, turn + 1)
                        nc.vector.tensor_copy(bc[32:64, :], mid[:, :]).then_inc(mid_moved, 1)
                        nc.vector.tensor_tensor(r1[:, :], r1[:, :], mid[:, :], ALU.subtract).then_inc(rest2, 1)
                        dve.wait_ge(rest2, turn + 1)
                        nc.vector.tensor_copy(bc[64:96, :], r1[:, :]).then_inc(lo_kept, 1)
                        for half in range(2):
                            dve.wait_ge(abs_done, turn * 2 + half + 1)
                            nc.vector.tensor_scalar(pos[:, half, :], bank[half][:, :], w[f"dtb{r}"][:, half:half + 1], 0.0,
                                                    ALU.add, ALU.max).then_inc(pos_done, 1)
                        dve.wait_ge(exp_done, turn + 1)
                        nc.vector.tensor_scalar(grow[:], mag[:], 1.0, None, ALU.add).then_inc(grown, 1)
                        dve.wait_ge(grown, turn + 1)
                        nc.vector.scalar_tensor_tensor(out=mag[:], in0=grow[:], scalar=-1.0, in1=mag[:], op0=ALU.add,
                                                       op1=ALU.subtract).then_inc(lost, 1)
                        dve.wait_ge(log_done, turn + 1)
                        dve.wait_ge(pos_done, turn * 2 + 2)
                        nc.vector.tensor_tensor(delta[:], pos[:], log, ALU.add).then_inc(delta_sum, 1)
                        dve.wait_ge(inv_done, turn + 1)
                        dve.wait_ge(lost, turn + 1)
                        nc.vector.tensor_tensor(mag[:], mag[:], inv, ALU.mult).then_inc(lost_part, 1)
                        dve.wait_ge(lost_part, turn + 1)
                        dve.wait_ge(delta_sum, turn + 1)
                        nc.vector.tensor_tensor(delta[:], delta[:], mag[:], ALU.subtract).then_inc(delta_done, 1)
                        for i in range(ITEMS + 1):
                            if i < ITEMS:
                                dve.wait_ge(da_ready, turn * ITEMS + i + 1)
                                dve.wait_ge(dbu_ready, turn * ITEMS + i + 1)
                                if i >= 2:
                                    dve.wait_ge(term_ready, turn * ITEMS + i - 1)
                                nc.vector.tensor_tensor_scan(hh[:, i % 2, :], da[:, i % 4, :], dbu[:, i % 4, :], 0.0,
                                                             ALU.mult, ALU.add).then_inc(scan_done, 1)
                            if i >= 1:
                                k = i - 1
                                dve.wait_ge(scan_done, turn * ITEMS + k + 1)
                                dve.wait_ge(c_spread, turn * N + k // 2 + 1)
                                if k >= 4:
                                    dve.wait_ge(y_added, turn * ITEMS + k - 3)
                                nc.vector.tensor_tensor(term[:, k % 4, :], hh[:, k % 2, :], bank[2 + k // 2 % 2][:, :],
                                                        ALU.mult).then_inc(term_ready, 1)
                    dve.wait_ge(y_added, b * BR * ITEMS + BR * ITEMS)
                    for half in range(2):
                        nc.vector.scalar_tensor_tensor(out=y[:, half, :], in0=u[:, half, :], scalar=skip[:, half:half + 1],
                                                       in1=bank[6 + half][:, :], op0=ALU.mult, op1=ALU.add).then_inc(skipped, 1)
                    for half in range(2):
                        dve.wait_ge(skipped, b * 2 + half + 1)
                        dve.wait_ge(z_ready, b * 2 + half + 1)
                        nc.vector.tensor_tensor(y[:, half, :], y[:, half, :], z[:, half, :], ALU.mult).then_inc(gated, 1)
                    dve.wait_ge(out_ready, b + 1)
                    nc.vector.tensor_tensor(chunk(g.resid, b), chunk(g.resid, b), bank[4][:, :], ALU.add).then_inc(resid_done, 1)


def selective_scan_one(g):
    selective_scan(g, "l2a", [64])


def selective_scan_two(g):
    selective_scan(g, "l2b", [8, 8])


def unit_attention(g):
    nc, bank, w = g.nc, g.bank, g.w["l3a"]
    HEADS, HD = 4, 64
    with stage(g, "x_kept proj_ready v_ready lowered exp_ready raised squared ss_ready rooted logged inv_ready unit_ready "
                  "ones_set v_kept score_ready masked copied pv_ready den_logged den_inv y_ready out_ready resid_done") as (sb, sems):
        (x_kept, proj_ready, v_ready, lowered, exp_ready, raised, squared, ss_ready, rooted, logged, inv_ready, unit_ready,
         ones_set, v_kept, score_ready, masked, copied, pv_ready, den_logged, den_inv, y_ready, out_ready, resid_done) = sems
        xb = sb("u_xb", [P, CHUNK])
        e = sb("u_e", [P, 4, CHUNK])
        qk = sb("u_qk", [P, 4, CHUNK])
        vw = sb("u_vw", [P, QT, HEADS, 2 * HD])
        st = sb("u_st", [P, 4, CHUNK])
        rd = sb("u_rd", [HD, 2, CHUNK])
        y = sb("u_y", [P, 2, CHUNK])
        items = [(h, kt) for h in range(HEADS) for kt in range(QT)]
        LOOK = 3
        with nc.Block() as block:
            @block.tensor
            def _(pe):
                pe.wait_ge(g.loaded["l3a"], 16)
                pe.wait_ge(ones_set, 1)
                with pe.Fori(0, CHUNKS) as b:
                    pe.wait_ge(resid_done, b + 1)
                    for m in range(4):
                        nc.tensor.matmul(bank[m][:, :], w["wqk"][:, m * P:(m + 1) * P], chunk(g.normed, b),
                                         start=True, stop=True).then_inc(proj_ready, 1)
                    pe.wait_ge(x_kept, b + 1)
                    for t in range(QT):
                        mm = nc.tensor.matmul(bank[4 + t // 2][:, t % 2 * 256:t % 2 * 256 + 256], xb[:, t * P:(t + 1) * P], w["wv"],
                                              start=True, stop=True)
                    mm.then_inc(v_ready, 1)
                    for m in range(4):
                        pe.wait_ge(squared, b * 4 + m + 1)
                        mm = nc.tensor.matmul(bank[m][:, :], g.same64, e[:, m, :], start=True, stop=True)
                    mm.then_inc(ss_ready, 1)
                    pe.wait_ge(unit_ready, b + 1)
                    pe.wait_ge(v_kept, b + 1)
                    for n in range(len(items) + LOOK):
                        if n < len(items):
                            h, kt = items[n]
                            rows = slice(HD * (h % 2), HD * (h % 2) + HD)
                            if n >= 4:
                                pe.wait_ge(masked, b * 16 + n - 3)
                                pe.wait_ge(copied, b * 16 + n - 3)
                            nc.tensor.matmul(bank[n % 4][:, kt * P:CHUNK], qk[rows, 2 + h // 2, kt * P:(kt + 1) * P],
                                             qk[rows, h // 2, kt * P:CHUNK], start=True, stop=True).then_inc(score_ready, 1)
                        if n >= LOOK:
                            i = n - LOOK
                            h, kt = items[i]
                            pe.wait_ge(masked, b * 16 + i + 1)
                            pe.wait_ge(copied, b * 16 + i + 1)
                            if kt == 0 and h >= 2:
                                pe.wait_ge(y_ready, b * HEADS + h - 1)
                            nc.tensor.matmul(bank[6 + h % 2][:, kt * P:CHUNK], vw[:, kt, h, :], st[:, i % 4, kt * P:CHUNK],
                                             start=(kt == 0), stop=(kt == QT - 1)).then_inc(pv_ready, 1)
                    pe.wait_ge(y_ready, b * HEADS + HEADS)
                    for half in range(2):
                        mm = nc.tensor.matmul(bank[5][:, :], w["wo"][:, half * P:(half + 1) * P], y[:, half, :],
                                              start=(half == 0), stop=(half == 1))
                    mm.then_inc(out_ready, 1)

            @block.scalar
            def _(act):
                with act.Fori(0, CHUNKS) as b:
                    nc.scalar.copy(xb[:, :], chunk(g.normed, b)).then_inc(x_kept, 1)
                    for m in range(4):
                        act.wait_ge(lowered, b * 4 + m + 1)
                        nc.scalar.activation(e[:, m, :], e[:, m, :], ACT.Exp).then_inc(exp_ready, 1)
                    for m in range(4):
                        act.wait_ge(raised, b * 4 + m + 1)
                        nc.scalar.activation(e[:, m, :], qk[:, m, :], ACT.Square).then_inc(squared, 1)
                    act.wait_ge(ss_ready, b + 1)
                    nc.scalar.activation(e[:], g.banks[0:4, 0:CHUNK], ACT.Sqrt).then_inc(rooted, 1)
                    act.wait_ge(rooted, b + 1)
                    nc.scalar.activation(e[:], e[:], ACT.Ln, bias=g.eps6).then_inc(logged, 1)
                    act.wait_ge(logged, b + 1)
                    nc.scalar.activation(e[:], e[:], ACT.Exp, scale=-1.0).then_inc(inv_ready, 1)
                    for n, (h, kt) in enumerate(items):
                        act.wait_ge(masked, b * 16 + n + 1)
                        if n >= 4:
                            act.wait_ge(pv_ready, b * 16 + n - 3)
                        if kt < QT - 1:
                            nc.scalar.copy(st[:, n % 4, (kt + 1) * P:CHUNK], bank[n % 4][:, (kt + 1) * P:CHUNK]).then_inc(copied, 1)
                        else:
                            nc.scalar.copy(g.mark2[:, 0:1], g.eps5).then_inc(copied, 1)
                        if kt == 1 and h >= 1:
                            act.wait_ge(pv_ready, b * 16 + 4 * h)
                            nc.scalar.activation(rd[:, (h - 1) % 2, :], bank[6 + (h - 1) % 2][HD:P, :], ACT.Ln,
                                                 bias=g.eps6[0:HD]).then_inc(den_logged, 1)
                            act.wait_ge(den_logged, b * HEADS + h)
                            nc.scalar.activation(rd[:, (h - 1) % 2, :], rd[:, (h - 1) % 2, :], ACT.Exp, scale=-1.0).then_inc(den_inv, 1)
                    act.wait_ge(pv_ready, b * 16 + 16)
                    nc.scalar.activation(rd[:, 1, :], bank[7][HD:P, :], ACT.Ln, bias=g.eps6[0:HD]).then_inc(den_logged, 1)
                    act.wait_ge(den_logged, b * HEADS + HEADS)
                    nc.scalar.activation(rd[:, 1, :], rd[:, 1, :], ACT.Exp, scale=-1.0).then_inc(den_inv, 1)

            @block.gpsimd
            def _(pool):
                nc.gpsimd.memset(vw[:, :, :, HD:2 * HD], 1.0).then_inc(ones_set, 1)

            @block.vector
            def _(dve):
                nc.vector.memset(g.mark, 0.0).then_inc(resid_done, 1)

                def weigh(b, h):
                    dve.wait_ge(den_inv, b * HEADS + h + 1)
                    nc.vector.tensor_tensor(y[HD * (h % 2):HD * (h % 2) + HD, h // 2, :], bank[6 + h % 2][0:HD, :], rd[:, h % 2, :],
                                            ALU.mult).then_inc(y_ready, 1)

                with dve.Fori(0, CHUNKS) as b:
                    for m in range(4):
                        dve.wait_ge(proj_ready, b * 4 + m + 1)
                        nc.vector.tensor_scalar(e[:, m, :], bank[m][:, :], 0.0, None, ALU.min).then_inc(lowered, 1)
                    dve.wait_ge(v_ready, b + 1)
                    for t in range(QT):
                        cp = nc.vector.tensor_copy(vw[:, t, :, 0:HD], bank[4 + t // 2][:, t % 2 * 256:t % 2 * 256 + 256].rearrange(
                            "p (h d) -> p h d", d=HD))
                    cp.then_inc(v_kept, 1)
                    for m in range(4):
                        dve.wait_ge(exp_ready, b * 4 + m + 1)
                        nc.vector.scalar_tensor_tensor(out=qk[:, m, :], in0=bank[m][:, :], scalar=0.0, in1=e[:, m, :],
                                                       op0=ALU.max, op1=ALU.add).then_inc(raised, 1)
                    dve.wait_ge(inv_ready, b + 1)
                    dve.wait_ge(raised, b * 4 + 4)
                    nc.vector.tensor_tensor(qk[:], qk[:], e[:], ALU.mult).then_inc(unit_ready, 1)
                    for n, (h, kt) in enumerate(items):
                        dve.wait_ge(score_ready, b * 16 + n + 1)
                        if n >= 4:
                            dve.wait_ge(pv_ready, b * 16 + n - 3)
                        nc.vector.tensor_tensor(st[:, n % 4, kt * P:(kt + 1) * P], bank[n % 4][:, kt * P:(kt + 1) * P], g.causal,
                                                ALU.mult).then_inc(masked, 1)
                        if kt == 2 and h >= 1:
                            weigh(b, h - 1)
                    weigh(b, HEADS - 1)
                    dve.wait_ge(out_ready, b + 1)
                    nc.vector.tensor_tensor(chunk(g.resid, b), chunk(g.resid, b), bank[5][:, :], ALU.add).then_inc(resid_done, 1)


def decayed_sum(g):
    nc, bank, w = g.nc, g.bank, g.w["l3b"]
    with stage(g, "rate_ready decay_ready bonus_ready filled spread first_set proj_ready k_kept gate_ready kv_ready scanned "
                  "summed y_ready out_ready resid_done") as (sb, sems):
        (rate_ready, decay_ready, bonus_ready, filled, spread, first_set, proj_ready, k_kept, gate_ready, kv_ready, scanned,
         summed, y_ready, out_ready, resid_done) = sems
        decay = sb("w_decay", [P, 1])
        bonus = sb("w_bonus", [P, 1])
        keep = sb("w_keep", [P, CHUNK])
        k = sb("w_k", [P, CHUNK])
        kv = sb("w_kv", [P, CHUNK])
        gate = sb("w_gate", [P, CHUNK])
        s = sb("w_s", [P, 1 + CHUNK])
        y = sb("w_y", [P, CHUNK])
        with nc.Block() as block:
            @block.tensor
            def _(pe):
                pe.wait_ge(g.loaded["l3b"], 16)
                with pe.Fori(0, CHUNKS) as b:
                    pe.wait_ge(resid_done, b + 1)
                    for m in range(3):
                        nc.tensor.matmul(bank[m][:, :], w["wkvr"][:, m * P:(m + 1) * P], chunk(g.normed, b),
                                         start=True, stop=True).then_inc(proj_ready, 1)
                    pe.wait_ge(y_ready, b + 1)
                    nc.tensor.matmul(bank[3][:, :], w["wo"], y[:, :], start=True, stop=True).then_inc(out_ready, 1)

            @block.scalar
            def _(act):
                act.wait_ge(g.loaded["l3b"], 16)
                nc.scalar.activation(decay[:, :], w["decay"], ACT.Exp).then_inc(rate_ready, 1)
                act.wait_ge(rate_ready, 1)
                nc.scalar.activation(decay[:, :], decay[:, :], ACT.Exp, scale=-1.0).then_inc(decay_ready, 1)
                nc.scalar.activation(bonus[:, :], w["first"], ACT.Exp).then_inc(bonus_ready, 1)
                with act.Fori(0, CHUNKS) as b:
                    act.wait_ge(proj_ready, b * 3 + 1)
                    nc.scalar.copy(k[:, :], bank[0][:, :]).then_inc(k_kept, 1)
                    act.wait_ge(proj_ready, b * 3 + 3)
                    nc.scalar.activation(gate[:, :], bank[2][:, :], ACT.Sigmoid).then_inc(gate_ready, 1)

            @block.vector
            def _(dve):
                nc.vector.memset(keep[:, :], 1.0).then_inc(filled, 1)
                nc.vector.memset(s[:, 0:1], 0.0).then_inc(first_set, 1)
                nc.vector.memset(g.mark, 0.0).then_inc(resid_done, 1)
                dve.wait_ge(filled, 1)
                dve.wait_ge(decay_ready, 1)
                nc.vector.tensor_scalar(keep[:, :], keep[:, :], decay[:, :], None, ALU.mult).then_inc(spread, 1)
                dve.wait_ge(spread, 1)
                dve.wait_ge(first_set, 1)
                dve.wait_ge(bonus_ready, 1)
                with dve.Fori(0, CHUNKS) as b:
                    dve.wait_ge(k_kept, b + 1)
                    dve.wait_ge(proj_ready, b * 3 + 2)
                    nc.vector.tensor_tensor(kv[:, :], k[:, :], bank[1][:, :], ALU.mult).then_inc(kv_ready, 1)
                    dve.wait_ge(kv_ready, b + 1)
                    nc.vector.tensor_tensor_scan(s[:, 1:1 + CHUNK], keep[:, :], kv[:, :], 0.0, ALU.mult, ALU.add).then_inc(scanned, 1)
                    dve.wait_ge(scanned, b + 1)
                    nc.vector.scalar_tensor_tensor(out=y[:, :], in0=kv[:, :], scalar=bonus[:, :], in1=s[:, 0:CHUNK],
                                                   op0=ALU.mult, op1=ALU.add).then_inc(summed, 1)
                    dve.wait_ge(summed, b + 1)
                    dve.wait_ge(gate_ready, b + 1)
                    nc.vector.tensor_tensor(y[:, :], y[:, :], gate[:, :], ALU.mult).then_inc(y_ready, 1)
                    dve.wait_ge(out_ready, b + 1)
                    nc.vector.tensor_tensor(chunk(g.resid, b), chunk(g.resid, b), bank[3][:, :], ALU.add).then_inc(resid_done, 1)


def soft_experts(g):
    nc, bank, w = g.nc, g.bank, g.w["l3f"]
    SLOTS, EXPERTS, SLOT = 2048, 64, 32
    PARTS, STILES = SLOTS // CHUNK, SLOTS // P
    PE_ = CHUNK // SLOT
    LOW, HIGH = -33000.0, 65000.0
    g.count += 1
    with ExitStack() as ctx:
        yt = ctx.enter_context(nc.sbuf_tensor(f"x_yt_{g.count}", [P, STILES, P], F32))

        with stage(g, "cleared zeroed x_kept turned xt_kept logit_ready max_ready lowered exp_ready sum_ready inv_ready "
                      "share_ready added") as (sb, sems):
            (cleared, zeroed, x_kept, turned, xt_kept, logit_ready, max_ready, lowered, exp_ready, sum_ready, inv_ready,
             share_ready, added) = sems
            zero = sb("x_zero", [P, CHUNK], BF16)
            xb = sb("x_xb", [P, CHUNK])
            xt = sb("x_xt", [P, QT, P])
            bias = sb("x_bias", [3, SLOTS], BF16)
            share = sb("x_share", [P, 2, SLOTS])
            mx = sb("x_mx", [P, 2, EXPERTS])
            total = sb("x_total", [P, 2, EXPERTS])

            def part(t, c):
                return share[:, t % 2, c * CHUNK:(c + 1) * CHUNK]

            def by_expert(x):
                return x.rearrange("p (n s) -> p n s", s=SLOT)

            with nc.Block() as block:
                @block.tensor
                def _(pe):
                    pe.wait_ge(g.loaded["l3f"], 16)
                    pe.wait_ge(cleared, 1)
                    for c in range(PARTS):
                        nc.tensor.matmul(bank[4 + c][:, :], g.ident_bf, zero[:, :], start=True, stop=True)
                    with pe.Fori(0, CHUNKS) as b:
                        pe.wait_ge(x_kept, b + 1)
                        for t in range(QT):
                            mm = nc.tensor.transpose(bank[0][:, t * P:(t + 1) * P], xb[:, t * P:(t + 1) * P], g.ident)
                        mm.then_inc(turned, 1)
                        pe.wait_ge(xt_kept, b + 1)
                        for t in range(QT + 1):
                            if t < QT:
                                for c in range(PARTS):
                                    if t >= 1:
                                        pe.wait_ge(lowered, (b * QT + t - 1) * PARTS + c + 1)
                                    nc.tensor.matmul(bank[c][:, :], g.ones_row, w["phi_b"][:, c * CHUNK:(c + 1) * CHUNK],
                                                     start=True, stop=False)
                                    nc.tensor.matmul(bank[c][:, :], xb[:, t * P:(t + 1) * P], w["phi"][:, c * CHUNK:(c + 1) * CHUNK],
                                                     start=False, stop=True).then_inc(logit_ready, 1)
                            if t >= 1:
                                pe.wait_ge(share_ready, b * QT + t)
                                for c in range(PARTS):
                                    mm = nc.tensor.matmul(bank[4 + c][:, :], xt[:, t - 1, :], part(t - 1, c), start=False, stop=True,
                                                          skip_group_check=True)
                                mm.then_inc(added, 1)

                @block.scalar
                def _(act):
                    with act.Fori(0, CHUNKS) as b:
                        nc.scalar.copy(xb[:, :], chunk(g.normed, b)).then_inc(x_kept, 1)
                        act.wait_ge(turned, b + 1)
                        nc.scalar.copy(xt[:].rearrange("p t c -> p (t c)"), bank[0][:, :]).then_inc(xt_kept, 1)
                        for t in range(QT):
                            for c in range(PARTS):
                                act.wait_ge(lowered, (b * QT + t) * PARTS + c + 1)
                                nc.scalar.activation(part(t, c), part(t, c), ACT.Exp).then_inc(exp_ready, 1)

                @block.gpsimd
                def _(pool):
                    nc.gpsimd.memset(zero[:, :], 0.0).then_inc(cleared, 1)
                    with pool.Fori(0, CHUNKS) as b:
                        for t in range(QT):
                            pool.wait_ge(inv_ready, b * QT + t + 1)
                            pool.wait_ge(exp_ready, (b * QT + t) * PARTS + PARTS)
                            e = by_expert(share[:, t % 2, :])
                            nc.gpsimd.tensor_tensor(e, e, total[:, t % 2, :].unsqueeze(2).broadcast_to([P, EXPERTS, SLOT]),
                                                    ALU.mult).then_inc(share_ready, 1)

                @block.vector
                def _(dve):
                    with dve.Fori(0, CHUNKS) as b:
                        for t in range(QT + 1):
                            if t < QT:
                                for c in range(PARTS):
                                    n = (b * QT + t) * PARTS + c
                                    m = mx[:, t % 2, c * PE_:(c + 1) * PE_]
                                    dve.wait_ge(logit_ready, n + 1)
                                    nc.vector.tensor_reduce(m, by_expert(bank[c][:, :]), AX.X, ALU.max).then_inc(max_ready, 1)
                                    if t >= 2 and c == 0:
                                        dve.wait_ge(added, b * QT + t - 1)
                                    dve.wait_ge(max_ready, n + 1)
                                    nc.vector.tensor_tensor(by_expert(part(t, c)), by_expert(bank[c][:, :]),
                                                            m.unsqueeze(2).broadcast_to([P, PE_, SLOT]), ALU.subtract).then_inc(lowered, 1)
                            if t >= 1:
                                n = b * QT + t
                                dve.wait_ge(exp_ready, n * PARTS)
                                nc.vector.tensor_reduce(total[:, (t - 1) % 2, :], by_expert(share[:, (t - 1) % 2, :]), AX.X,
                                                        ALU.add).then_inc(sum_ready, 1)
                                dve.wait_ge(sum_ready, n)
                                nc.vector.reciprocal(total[:, (t - 1) % 2, :], total[:, (t - 1) % 2, :]).then_inc(inv_ready, 1)

        with stage(g, "bounded mean_ready centred squared var_ready logged rstd_ready scaled tanh_ready y_ready y_kept") as (sb, sems):
            bounded, mean_ready, centred, squared, var_ready, logged, rstd_ready, scaled, tanh_ready, y_ready, y_kept = sems
            z = sb("x_z", [P, SLOTS])
            sq = sb("x_sq", [P, SLOTS])
            rstd = sb("x_rstd", [P, SLOTS])
            with nc.Block() as block:
                @block.tensor
                def _(pe):
                    for j in range(PARTS):
                        pe.wait_ge(bounded, j + 1)
                        nc.tensor.matmul(bank[j][:, :], g.mean_of, fixed(z, j), start=True, stop=True).then_inc(mean_ready, 1)
                    for j in range(PARTS):
                        pe.wait_ge(squared, j + 1)
                        nc.tensor.matmul(bank[4 + j][:, :], g.mean_of, fixed(sq, j), start=True, stop=True).then_inc(var_ready, 1)
                    for j in range(PARTS):
                        pe.wait_ge(tanh_ready, j + 1)
                        for i in range(4 * j, 4 * j + 4):
                            at = slice(i % 4 * P, (i % 4 + 1) * P)
                            nc.tensor.matmul(bank[j][:, at], w["of_expert"][:, i * P:(i + 1) * P], w["expert_b"], start=True, stop=True)
                            for q in range(4):
                                n = 4 * i + q
                                mm = nc.tensor.matmul(bank[j][SLOT * q:SLOT * (q + 1), at], z[:, n * SLOT:(n + 1) * SLOT],
                                                      w["expert_w"][:, n * P:(n + 1) * P], start=False, stop=True,
                                                      skip_group_check=True)
                        mm.then_inc(y_ready, 1)

                @block.scalar
                def _(act):
                    for j in range(PARTS):
                        act.wait_ge(centred, j + 1)
                        nc.scalar.activation(fixed(sq, j), fixed(z, j), ACT.Square).then_inc(squared, 1)
                    for j in range(PARTS):
                        act.wait_ge(var_ready, j + 1)
                        nc.scalar.activation(fixed(rstd, j), bank[4 + j][:, :], ACT.Ln, bias=g.eps5).then_inc(logged, 1)
                        act.wait_ge(logged, j + 1)
                        nc.scalar.activation(fixed(rstd, j), fixed(rstd, j), ACT.Exp, scale=-0.5).then_inc(rstd_ready, 1)
                    for j in range(PARTS):
                        act.wait_ge(scaled, j + 1)
                        nc.scalar.activation(fixed(z, j), fixed(z, j), ACT.Tanh).then_inc(tanh_ready, 1)
                    for j in range(PARTS):
                        act.wait_ge(y_ready, j + 1)
                        nc.scalar.copy(yt[:, 4 * j:4 * j + 4, :].rearrange("p i h -> p (i h)"), bank[j][:, :]).then_inc(y_kept, 1)

                @block.vector
                def _(dve):
                    for j in range(PARTS):
                        nc.vector.tensor_scalar(fixed(z, j), bank[4 + j][:, :], LOW, HIGH, ALU.max, ALU.min).then_inc(bounded, 1)
                    for j in range(PARTS):
                        dve.wait_ge(mean_ready, j + 1)
                        nc.vector.tensor_tensor(fixed(z, j), fixed(z, j), bank[j][:, :], ALU.subtract).then_inc(centred, 1)
                    for j in range(PARTS):
                        dve.wait_ge(rstd_ready, j + 1)
                        dve.wait_ge(centred, j + 1)
                        nc.vector.tensor_tensor(fixed(z, j), fixed(z, j), fixed(rstd, j), ALU.mult).then_inc(scaled, 1)

        with stage(g, "logit_ready kept max_step quarter_kept quarter_max max_spread low_dve low_pool exp_ready sum_ready inv_ready "
                      "share_dve share_pool out_ready resid_done") as (sb, sems):
            (logit_ready, kept, max_step, quarter_kept, quarter_max, max_spread, low_dve, low_pool, exp_ready, sum_ready, inv_ready,
             share_dve, share_pool, out_ready, resid_done) = sems
            lt = sb("x_lt", [P, STILES, CHUNK])
            top = sb("x_top", [P, CHUNK])
            side = sb("x_side", [SLOT, 3, CHUNK])
            inv = sb("x_inv", [P, CHUNK])
            on_pool = [i for i in range(STILES) if i % 3 == 2]
            on_dve = [i for i in range(STILES) if i % 3 != 2]

            def wait_for(eng, i, b, by_dve, by_pool):
                if i in on_pool:
                    eng.wait_ge(by_pool, b * len(on_pool) + on_pool.index(i) + 1)
                else:
                    eng.wait_ge(by_dve, b * len(on_dve) + on_dve.index(i) + 1)

            with nc.Block() as block:
                @block.tensor
                def _(pe):
                    with pe.Fori(0, CHUNKS) as b:
                        for i in range(STILES):
                            if i >= 3:
                                pe.wait_ge(kept, b * STILES + i - 2)
                            nc.tensor.matmul(bank[i % 3][:, :], w["phi"][:, i * P:(i + 1) * P], chunk(g.normed, b),
                                             start=True, stop=True).then_inc(logit_ready, 1)
                        for i in range(STILES):
                            pe.wait_ge(exp_ready, b * STILES + i + 1)
                            mm = nc.tensor.matmul(bank[4][:, :], g.mod32, lt[:, i, :], start=(i == 0), stop=(i == STILES - 1))
                        mm.then_inc(sum_ready, 1)
                        pe.wait_ge(resid_done, b + 1)
                        for i in range(STILES):
                            wait_for(pe, i, b, share_dve, share_pool)
                            mm = nc.tensor.matmul(bank[5][:, :], yt[:, i, :], lt[:, i, :], start=(i == 0), stop=(i == STILES - 1))
                        mm.then_inc(out_ready, 1)

                @block.scalar
                def _(act):
                    with act.Fori(0, CHUNKS) as b:
                        for i in range(STILES):
                            act.wait_ge(logit_ready, b * STILES + i + 1)
                            nc.scalar.activation(lt[:, i, :], bank[i % 3][:, :], ACT.Identity, bias=w["phi_bc"][:, i:i + 1]).then_inc(kept, 1)
                        for i in range(STILES):
                            wait_for(act, i, b, low_dve, low_pool)
                            nc.scalar.activation(lt[:, i, :], lt[:, i, :], ACT.Exp).then_inc(exp_ready, 1)

                @block.gpsimd
                def _(pool):
                    with pool.Fori(0, CHUNKS) as b:
                        pool.wait_ge(max_spread, b * 4 + 4)
                        for i in on_pool:
                            nc.gpsimd.tensor_tensor(lt[:, i, :], lt[:, i, :], top[:, :], ALU.subtract).then_inc(low_pool, 1)
                        pool.wait_ge(inv_ready, b + 1)
                        for i in on_pool:
                            nc.gpsimd.tensor_tensor(lt[:, i, :], lt[:, i, :], inv[:, :], ALU.mult).then_inc(share_pool, 1)

                @block.vector
                def _(dve):
                    nc.vector.memset(g.mark, 0.0).then_inc(resid_done, 1)
                    with dve.Fori(0, CHUNKS) as b:
                        steps = STILES - 1
                        for i in range(1, STILES):
                            dve.wait_ge(kept, b * STILES + i + 1)
                            if i >= 2:
                                dve.wait_ge(max_step, b * steps + i - 1)
                            nc.vector.tensor_tensor(top[:, :], lt[:, 0, :] if i == 1 else top[:, :], lt[:, i, :], ALU.max).then_inc(max_step, 1)
                        dve.wait_ge(max_step, b * steps + steps)
                        for q in range(3):
                            nc.vector.tensor_copy(side[:, q, :], top[SLOT * (q + 1):SLOT * (q + 2), :]).then_inc(quarter_kept, 1)
                        for q in range(3):
                            dve.wait_ge(quarter_kept, b * 3 + q + 1)
                            if q >= 1:
                                dve.wait_ge(quarter_max, b * 3 + q)
                            nc.vector.tensor_tensor(side[:, 0, :], top[0:SLOT, :] if q == 0 else side[:, 0, :], side[:, q, :],
                                                    ALU.max).then_inc(quarter_max, 1)
                        dve.wait_ge(quarter_max, b * 3 + 3)
                        for q in range(4):
                            nc.vector.tensor_copy(top[SLOT * q:SLOT * (q + 1), :], side[:, 0, :]).then_inc(max_spread, 1)
                        dve.wait_ge(max_spread, b * 4 + 4)
                        for i in on_dve:
                            nc.vector.tensor_tensor(lt[:, i, :], lt[:, i, :], top[:, :], ALU.subtract).then_inc(low_dve, 1)
                        dve.wait_ge(sum_ready, b + 1)
                        nc.vector.reciprocal(inv[:, :], bank[4][:, :]).then_inc(inv_ready, 1)
                        dve.wait_ge(inv_ready, b + 1)
                        for i in on_dve:
                            nc.vector.tensor_tensor(lt[:, i, :], lt[:, i, :], inv[:, :], ALU.mult).then_inc(share_dve, 1)
                        dve.wait_ge(out_ready, b + 1)
                        nc.vector.tensor_tensor(chunk(g.resid, b), chunk(g.resid, b), bank[5][:, :], ALU.add).then_inc(resid_done, 1)



def columns(v):
    return v.reshape(-1, P).T


def beside(m):
    return m.reshape(-1, P, m.shape[1]).transpose(1, 0, 2).reshape(P, -1)


def blocks(shape, places):
    out = np.zeros(shape, np.float32)
    for r, c, m in places:
        out[r:r + m.shape[0], c:c + m.shape[1]] = m
    return out


def constants():
    eye = np.eye(P, dtype=np.float32)
    k, q = np.meshgrid(np.arange(P), np.arange(P), indexing="ij")
    bf = {"ident": eye, "mask_qk": np.where(q > k, MASKED, 0.0), "mask_kq": np.where(k > q, MASKED, 0.0)}
    for name, off in (("pick_b", 0), ("pick_c", 16)):
        t = np.zeros((P, 16, P))
        for n in range(16):
            t[[off + n, 32 + off + n, 64 + off + n], n, :] = 1.0
        bf[name] = t.reshape(P, -1)
    for name, experts, width, tiles in (("route0", 8, 176, 14), ("route1", 16, 64, 9)):
        t = np.zeros((P, tiles * P))
        for unit in range(tiles * P):
            e = unit // width
            t[[e, 32 + e, 64 + e] if e < experts else [96], unit] = 1.0
        bf[name] = t
    bf["ones3"] = blocks((P, P), [(0, 0, np.ones((3, P)))])
    f = {"mean_of": np.full((P, P), 1.0 / P), "ident": eye, "ones": np.ones((P, P)),
         "causal": (k <= q), "same8": (k // 8 == q // 8), "same64": (k // 64 == q // 64), "mod32": (k % 32 == q % 32),
         "head_of": (np.arange(P)[:, None] // 8 == np.arange(16)[None, :]),
         "iota": np.broadcast_to(np.arange(16.0), (P, 16)), "eps5": np.full((P, 1), 1e-5), "eps4": np.full((P, 1), 1e-4),
         "minus": -eye, "one": np.ones((P, 1)), "eps6": np.full((P, 1), 1e-6)}
    as32 = lambda d: [(n, np.asarray(a, np.float32)) for n, a in d.items()]
    return as32(bf), as32(f)


def rotary():
    inv = (1.0 / 10000.0 ** (np.arange(0, 32, 2, dtype=np.float32) / np.float32(32))).astype(np.float32)
    angle = np.outer(np.repeat(inv, 2), np.arange(TIME, dtype=np.float32)).astype(np.float32)
    rot = np.zeros((P, P), np.float32)
    for i in range(0, P, 2):
        rot[i + 1, i] = -1.0
        rot[i, i + 1] = 1.0
    return np.tile(np.cos(angle), (4, 1)), np.tile(np.sin(angle), (4, 1)), rot


def weight_parts(a):
    cos, sin, rot = rotary()
    parts = {}

    def heads_to_latent(m):
        return np.concatenate([blocks((P, P), [(8 * (4 * grp + j), 32 * j, m.T) for j in range(4)])
                               for grp in range(4)], axis=1)

    n = "L0_attn_a_"
    parts["l0a"] = [
        ("wqkv", a[n + "c_attn_w"].T), ("bqkv", columns(a[n + "c_attn_b"])),
        ("q2l", heads_to_latent(a[n + "q2l_w"])), ("kv2l", heads_to_latent(a[n + "kv2l_w"])),
        ("q2l_b", np.tile(a[n + "q2l_b"], 4)[:, None]), ("kv2l_b", np.tile(a[n + "kv2l_b"], 4)[:, None]),
        ("wqk", blocks((P, P), [(32 * j, 32 * j, a[n + "wqk_w"].T) for j in range(4)])),
        ("wqk_b", np.tile(a[n + "wqk_b"], 4)[:, None]),
        ("l2o", blocks((P, 32), [(32 * j, 8 * j, a[n + "l2o_w"].T) for j in range(4)])),
        ("l2o_b", np.tile(a[n + "l2o_b"], 16)[:, None]),
        ("cproj", a[n + "cproj_w"].T), ("cproj_b", columns(a[n + "cproj_b"])),
        ("cos", cos), ("sin", sin), ("rot", rot),
    ]
    n = "L0_ffn_"

    def hidden(m):
        return m.transpose(1, 0, 2).reshape(P, -1)

    def down(*ms):
        m = np.concatenate(ms, axis=0)
        return beside(blocks((-(-len(m) // P) * P, m.shape[1]), [(0, 0, m)]))

    def filled(*ms):
        m = np.concatenate(ms, axis=1)
        return blocks((P, -(-m.shape[1] // P) * P), [(0, 0, m)])

    parts["l0f"] = [("router", a[n + "Wg"]), ("gate", filled(hidden(a[n + "W1"]), a[n + "Ws1"])),
                    ("up", filled(hidden(a[n + "W2"]), a[n + "Ws2"])),
                    ("down", down(a[n + "W3"].reshape(-1, P), a[n + "Ws3"]))]
    n = "L0_attn_b_"
    parts["l0b"] = [("wqkv", a[n + "w_qkv"].T), ("wfc", a[n + "w_fc"].T), ("b_fc", columns(a[n + "b_fc"])),
                    ("gamma", columns(a[n + "gamma"])), ("beta", columns(a[n + "beta"]))]
    n = "L1_ffn_"
    units = lambda m: m.reshape(-1, P).T
    parts["l1f"] = [("router", a[n + "router_weight"].T), ("e_bias", np.broadcast_to(a[n + "e_bias"], (P, 16))),
                    ("gate", filled(units(a[n + "gate_w"]), a[n + "sh_gate_w"].T)),
                    ("up", filled(units(a[n + "up_w"]), a[n + "sh_up_w"].T)),
                    ("down", down(a[n + "down_w"].transpose(0, 2, 1).reshape(-1, P), a[n + "sh_down_w"].T))]
    n = "L1_attn_a_"
    c_own = np.concatenate([blocks((P, P), [(64 * s, 8 * (2 * p + s), a[n + "c"][2 * p + s]) for s in range(2)])
                            for p in range(8)], axis=1)
    parts["l1a"] = [("a", a[n + "a"].reshape(8, P, 64).transpose(1, 0, 2).reshape(P, -1)), ("b", a[n + "b"].reshape(P, 64)),
                    ("c", c_own), ("norm_w", columns(a[n + "norm_w"])), ("skip", a[n + "skip"].reshape(P, 1)),
                    ("out", a[n + "w_out"].T), ("b_out", columns(a[n + "b_out"]))]
    n = "L1_attn_b_"
    parts["l1b"] = [("wqkv", a[n + "Wqkv"].T), ("bqkv", columns(a[n + "bqkv"])), ("wproj", a[n + "Wproj"].T),
                    ("bproj", columns(a[n + "bproj"])), ("scale", np.broadcast_to(a[n + "scale"], (P, 1)))]
    n = "L2_ffn_"
    parts["l2f"] = [("w1", a[n + "w1_w"].T), ("w2", a[n + "w2_w"].T), ("h1", beside(a[n + "h1_w"].T)),
                    ("h2", beside(a[n + "h2_w"].T)), ("w3", beside(a[n + "w3_w"].T)), ("s1", columns(a[n + "w1_s"])),
                    ("s2", columns(a[n + "w2_s"])), ("sh1", columns(a[n + "h1_s"])), ("sh2", columns(a[n + "h2_s"])),
                    ("s3", columns(a[n + "w3_s"]))]

    def scan_parts(n, ranks, names):
        def halves(m):
            return beside(m)
        out = [("in", a[n + "in_proj_w"].T), ("conv", halves(a[n + "conv_w"].reshape(256, 4))),
               ("conv_b", columns(a[n + "conv_b"])), ("out", beside(a[n + "out_proj_w"].T))]
        for r, (rank, (xp, dtw, dtb, alog, d)) in enumerate(zip(ranks, names)):
            x = a[n + xp].T
            out += [(f"xdt{r}", halves(x[:, :rank])), (f"xbc{r}", halves(x[:, rank:])), (f"dtw{r}", a[n + dtw].T),
                    (f"dtb{r}", columns(a[n + dtb])), (f"alog{r}", halves(a[n + alog])), (f"d{r}", columns(a[n + d]))]
        return out

    parts["l2a"] = scan_parts("L2_attn_a_", [64], [("x_proj_w", "dt_proj_w", "dt_proj_b", "A_log", "D")])
    parts["l2b"] = scan_parts("L2_attn_b_", [8, 8], [(f"x{i}_proj_w", f"dt{i}_proj_w", f"dt{i}_proj_b", f"A{i}_log", f"D{i}")
                                                     for i in (1, 2)])
    n = "L3_attn_a_"
    parts["l3a"] = [("wqk", np.concatenate([a[n + "Wq"].T, a[n + "Wk"].T], axis=1)), ("wv", a[n + "Wv"].T),
                    ("wo", beside(a[n + "Wo"].T))]
    n = "L3_attn_b_"
    parts["l3b"] = [("wkvr", np.concatenate([a[n + "Wk"].T, a[n + "Wv"].T, a[n + "Wr"].T], axis=1)), ("wo", a[n + "Wo"].T),
                    ("decay", columns(a[n + "time_decay"])), ("first", columns(a[n + "time_first"]))]
    n = "L3_ffn_"
    of_expert = blocks((64, 2048), [(e, 32 * e, np.ones((1, 32))) for e in range(64)])
    parts["l3f"] = [("phi", a[n + "phi_w"].T), ("phi_b", a[n + "phi_b"][None, :]), ("phi_bc", columns(a[n + "phi_b"])),
                    ("expert_w", a[n + "expert_w"].transpose(1, 0, 2).reshape(P, -1)), ("expert_b", a[n + "expert_b"]),
                    ("of_expert", of_expert)]
    return parts


def build(nc, args, places, first=0, last=99):
    g = Core(nc)
    with ExitStack() as ctx:
        def sb(name, shape, dtype=F32):
            return ctx.enter_context(nc.sbuf_tensor(name, shape, dtype))

        g.resid = sb("resid", [P, TOKENS])
        g.normed = sb("normed", [P, TOKENS])
        g.mark = sb("mark", [P, 1])[:, :]
        g.mark2 = sb("mark2", [P, 2])
        psum = ctx.enter_context(nc.psum_tensor("psum", [P, 8, CHUNK], F32))
        g.bank = [psum[:, i, :] for i in range(8)]
        g.banks = Banks(psum)
        g.loaded, g.w = {}, {}
        widths = {k: sum(c for _, _, c in v.values()) for k, v in places.items()}
        def place_weights(blocks, sb):
            for k in blocks:
                tensors[k] = sb(f"w_{k}", [P, widths[k]])[:, :]
                g.w[k] = {name: tensors[k][0:r, o:o + c] for name, (r, o, c) in places[k].items()}
                g.loaded[k] = nc.alloc_semaphore(f"loaded_{k}")

        tensors = {}
        place_weights(("c32", "l2a", "l3a"), sb)
        bf = sb("c_bf", [P, widths["cbf"]], BF16)
        cbf = {name: bf[0:r, o:o + c] for name, (r, o, c) in places["cbf"].items()}
        c32 = g.w["c32"]
        g.ident_bf, g.mask_qk, g.mask_kq, g.ones3 = (cbf[n] for n in ("ident", "mask_qk", "mask_kq", "ones3"))
        g.pick_b, g.pick_c, g.route0, g.route1 = (cbf[n].rearrange("p (n m) -> p n m", m=P)
                                                  for n in ("pick_b", "pick_c", "route0", "route1"))
        (g.mean_of, g.ident, g.ones, g.causal, g.same8, g.same64, g.mod32, g.head_of, g.iota, g.eps5, g.eps4, g.minus,
         g.one, g.eps6) = (
            c32[n] for n in ("mean_of", "ident", "ones", "causal", "same8", "same64", "mod32", "head_of", "iota", "eps5",
                             "eps4", "minus", "one", "eps6"))
        g.ones_row = g.ones[0:1, :]
        x_loaded = nc.alloc_semaphore("x_loaded")

        with stage(g, "table_loaded table_cast") as (sbs, (table_loaded, table_cast)):
            wide = sbs("c_wide", [P, widths["cbf"]])
            with nc.Block() as block:
                @block.sync
                def _(sp):
                    sp.dma_start(g.resid[:, :], args["x"]).then_inc(x_loaded, 16)
                    sp.dma_start(tensors["c32"], args["c32"]).then_inc(g.loaded["c32"], 16)
                    sp.dma_start(wide[:, :], args["cbf"]).then_inc(table_loaded, 16)
                    sp.wait_ge(x_loaded, 16)
                    sp.wait_ge(g.loaded["c32"], 16)

                @block.vector
                def _(dve):
                    dve.wait_ge(table_loaded, 16)
                    nc.vector.tensor_copy(bf[:, :], wide[:, :]).then_inc(table_cast, 1)

        def load(blocks):
            with nc.Block() as block:
                @block.sync
                def _(sp):
                    for k in blocks:
                        sp.dma_start(tensors[k], args[k]).then_inc(g.loaded[k], 16)

        def loaded(blocks):
            with nc.Block() as block:
                @block.sync
                def _(sp):
                    for k in blocks:
                        sp.wait_ge(g.loaded[k], 16)

        layers = [latent_attention, top_two_experts, plain_attention, top_two_experts, recurrent_heads, grouped_experts,
                  cumulative_attention, grouped_experts, selective_scan_one, dense_ffn, selective_scan_two, dense_ffn,
                  unit_attention, soft_experts, decayed_sum, soft_experts]
        for part, blocks in ((slice(0, 8), ("l0a", "l0f", "l0b", "l1a", "l1f", "l1b", "l2a", "l3a")),
                             (slice(8, 12), ("l2f", "l2b")), (slice(12, 16), ("l3f", "l3b"))):
            with ExitStack() as turn:
                place_weights([k for k in blocks if k not in tensors],
                              lambda name, shape: turn.enter_context(nc.sbuf_tensor(name, shape, F32)))
                load(blocks)
                for i, layer in list(enumerate(layers))[part]:
                    if first <= i < last:
                        layernorm(g)
                        layer(g)
                loaded(blocks)
                nc.all_engine_barrier()
        out_stored = nc.alloc_semaphore("out_stored")
        with nc.Block() as block:
            @block.sync
            def _(sp):
                sp.dma_start(args["out"], g.resid[:, :]).then_inc(out_stored, 16)
                sp.wait_ge(out_stored, 16)


class Banks:

    def __init__(self, psum):
        self.psum = psum

    def __getitem__(self, at):
        return self.psum[:, at[0], at[1]]


def packed(inputs):
    cbf, c32 = constants()
    every = {"c32": c32, "cbf": cbf} | weight_parts(inputs)
    arrays, places = {}, {}
    for k, parts in every.items():
        rows, o, places[k] = [], 0, {}
        for name, m in parts:
            places[k][name] = (m.shape[0], o, m.shape[1])
            o += m.shape[1]
            rows.append(blocks((P, m.shape[1]), [(0, 0, m)]))
        arrays[k] = np.concatenate(rows, axis=1)
    return arrays, places


def kernel(**inputs):
    import numpy as _np
    import concourse.bacc as _bacc
    from concourse import mybir as _mybir
    from concourse.bass_utils import run_bass_kernel_spmd as _run

    inputs = {k: _np.asarray(v) for k, v in inputs.items()}
    arrays, places = packed(inputs)
    arrays["x"] = _np.ascontiguousarray(inputs["L0_attn_a_x"].reshape(TOKENS, P).T)
    nc = _bacc.Bacc("TRN2", target_bir_lowering=False, num_devices=1)
    args, sent = {}, {}
    for k, v in arrays.items():
        sent[f"in_{k}"] = v
        args[k] = nc.dram_tensor(f"in_{k}", v.shape, _mybir.dt.float32, kind="ExternalInput").ap()
    args["out"] = nc.dram_tensor("out_0", (P, TOKENS), _mybir.dt.float32, kind="ExternalOutput").ap()
    build(nc, args, places)
    r = _run(nc, [sent], core_ids=[0])
    out = r.results[0]["out_0"]
    return _np.ascontiguousarray(out.T).reshape(BATCH, TIME, P)
```

```python
from contextlib import ExitStack, contextmanager

import numpy as np

import concourse.bass as bass
from concourse import mybir

F32 = mybir.dt.float32
BF16 = mybir.dt.bfloat16
U32 = mybir.dt.uint32
ALU = mybir.AluOpType
ACT = mybir.ActivationFunctionType
AX = mybir.AxisListType

P = 128
BATCH, TIME = 4, 512
TOKENS = BATCH * TIME
CHUNK = 512
CHUNKS = TOKENS // CHUNK
TILES = TOKENS // P
QT = CHUNK // P
MASKED = -1e30
LOWEST = -3e38


class Core:

    def __init__(self, nc):
        self.nc = nc
        self.count = 0


@contextmanager
def stage(g, semaphores):
    nc = g.nc
    g.count += 1
    n = g.count
    with ExitStack() as ctx:
        def sb(name, shape, dtype=F32):
            return ctx.enter_context(nc.sbuf_tensor(f"{name}_{n}", shape, dtype))

        sems = [nc.alloc_semaphore(f"{name}_{n}") for name in semaphores.split()]
        yield sb, sems
        nc.clear_and_free_semaphores(sems)
        nc.all_engine_barrier()


def chunk(tensor, b):
    return tensor[:, bass.ds(b * CHUNK, CHUNK)]


def fixed(tensor, j):
    return tensor[:, j * CHUNK:(j + 1) * CHUNK]


def layernorm(g):
    nc, bank, x, y = g.nc, g.bank, g.resid, g.normed
    with stage(g, "table_there centred squared var_ready logged rstd_ready normed_ready") as (sb, sems):
        table_there, centred, squared, var_ready, logged, rstd_ready, normed_ready = sems
        sq = sb("ln_sq", [P, TOKENS])
        rstd = sb("ln_rstd", [P, TOKENS])
        with nc.Block() as block:
            @block.tensor
            def _(pe):
                for j in range(CHUNKS):
                    nc.tensor.matmul(bank[j][:, :], g.centre, fixed(x, j), start=True, stop=True).then_inc(centred, 1)
                for j in range(CHUNKS):
                    pe.wait_ge(squared, j + 1)
                    nc.tensor.matmul(bank[4 + j][:, :], g.mean_of, fixed(sq, j), start=True, stop=True).then_inc(var_ready, 1)

            @block.vector
            def _(dve):
                for j in range(CHUNKS):
                    dve.wait_ge(rstd_ready, j + 1)
                    nc.vector.tensor_tensor(fixed(y, j), bank[j][:, :], fixed(rstd, j), ALU.mult).then_inc(normed_ready, 1)

            @block.scalar
            def _(act):
                nc.scalar.activation(g.mark2[:, 0:1], g.one, ACT.Ln).then_inc(table_there, 1)
                for j in range(CHUNKS):
                    act.wait_ge(centred, j + 1)
                    nc.scalar.activation(fixed(sq, j), bank[j][:, :], ACT.Square).then_inc(squared, 1)
                for j in range(CHUNKS):
                    act.wait_ge(var_ready, j + 1)
                    nc.scalar.activation(fixed(rstd, j), bank[4 + j][:, :], ACT.Ln, bias=g.eps5).then_inc(logged, 1)
                for j in range(CHUNKS):
                    act.wait_ge(logged, j + 1)
                    nc.scalar.activation(fixed(rstd, j), fixed(rstd, j), ACT.Exp, scale=-0.5).then_inc(rstd_ready, 1)


def latent_attention(g):
    nc, bank, w = g.nc, g.bank, g.w["l0a"]
    HEADS, HD, LAT, GROUPS, STEP = 16, 8, 32, 4, 4
    ITEMS = STEP * QT
    LAG = 2
    SCALE = LAT ** -0.5
    HALF = HEADS // 2
    PARTS_DMA = 12 * 16
    MAXIMA = slice(96, 96 + 2 * STEP)
    with stage(g, "qkv_ready qkv_kept lat_ready turned roped qk_ready x_kept q1_kept k1_kept rest_ready k2_kept q2_kept low_kept "
                  "vlat_ready vl_kept v2_ready v_kept stacked cleared score_ready max_ready maxt_ready hi_kept m_placed "
                  "st_ready exp_ready pv_ready half_kept recip_done y_half out_ready resid_done biased bounced rows_set max_twice") as (sb, sems):
        (qkv_ready, qkv_kept, lat_ready, turned, roped, qk_ready, x_kept, q1_kept, k1_kept, rest_ready, k2_kept, q2_kept, low_kept,
         vlat_ready, vl_kept, v2_ready, v_kept, stacked, cleared, score_ready, max_ready, maxt_ready, hi_kept, m_placed,
         st_ready, exp_ready, pv_ready, half_kept, recip_done, y_half, out_ready, resid_done, biased, bounced, rows_set, max_twice) = sems
        spread = nc.dram_tensor("a_spread", (GROUPS, 2, 3, P, CHUNK), BF16).ap()
        qkv = sb("a_qkv", [P, 3, CHUNK])
        rc = sb("a_rc", [P, CHUNK])
        rs = sb("a_rs", [P, CHUNK])
        qr = sb("a_qr", [P, CHUNK])
        kr = sb("a_kr", [P, CHUNK])
        x = sb("a_x", [P, CHUNK])
        rest = sb("a_rest", [P, 2, CHUNK])
        kp = sb("a_kp", [P, 3, CHUNK], BF16)
        qp = sb("a_qp", [P, 3, CHUNK], BF16)
        ks1, ks2, qs1, qs2 = (sb(f"a_{n}", [104, GROUPS, STEP, CHUNK], BF16) for n in ("ks1", "ks2", "qs1", "qs2"))
        moves = [(ks1, 0, kp, 0), (ks1, 1, kp, 1), (ks1, 2, kp, 0), (ks2, 0, kp, 1), (ks2, 1, kp, 2), (ks2, 2, kp, 0),
                 (qs1, 0, qp, 0), (qs1, 1, qp, 0), (qs1, 2, qp, 1), (qs2, 0, qp, 1), (qs2, 1, qp, 0), (qs2, 2, qp, 2)]
        vl = sb("a_vl", [P, CHUNK])
        wide = sb("a_wide", [P, QT, 2, HALF * (P + HD)])
        mx = sb("a_mx", [P, QT, 2 * STEP])
        hi = sb("a_hi", [104, CHUNK], BF16)
        pt = sb("a_pt", [P, 4, CHUNK])
        pvs = sb("a_pvs", [P, 2, CHUNK])
        rd = sb("a_rd", [64, CHUNK])
        y = sb("a_y", [P, CHUNK])

        def windows(half):
            return wide[:, :, half, :].rearrange("p k (j e) -> p k j e", e=P + HD)

        def after(eng, sem, n):
            if not (isinstance(n, int) and n <= 0):
                eng.wait_ge(sem, n)

        with nc.Block() as block:
            @block.tensor
            def _(pe):
                def project_qkv(c, m):
                    if isinstance(c, int):
                        xs = fixed(g.normed, c)
                    else:
                        xs = chunk(g.normed, c & (CHUNKS - 1))
                    for i in range(3):
                        if i == 0:
                            after(pe, v_kept, m)
                        elif i == 1:
                            after(pe, m_placed, m - 1)
                            after(pe, q1_kept, m)
                        else:
                            pe.wait_ge(qkv_kept, c * 3 + 1)
                        nc.tensor.matmul(bank[6 + i % 2][:, :], w["wqkv"][:, i * P:(i + 1) * P], xs,
                                         start=True, stop=True).then_inc(qkv_ready, 1)

                def latents(i, c, grp, m):
                    src = ("q2l", "kv2l")[i]
                    at = slice(grp * P, (grp + 1) * P)
                    pe.wait_ge(qkv_kept, c * 3 + (3 if grp == 0 else i + 1))
                    if i == 0:
                        after(pe, v_kept, m)
                    else:
                        pe.wait_ge(turned, m * 4 + 1)
                    nc.tensor.matmul(bank[6][:, :], w[src][:, at], qkv[:, i, :], start=True, stop=True).then_inc(lat_ready, 1)
                    if i == 0:
                        after(pe, m_placed, m - 1)
                        after(pe, q1_kept, m)
                    else:
                        pe.wait_ge(turned, m * 4 + 2)
                    nc.tensor.matmul(bank[7][:, :], w[src + "_s"][:, at], qkv[:, i, :], start=True, stop=True).then_inc(lat_ready, 1)

                def queries(m):
                    pe.wait_ge(turned, m * 4 + 4)
                    pe.wait_ge(roped, m * 2 + 1)
                    nc.tensor.matmul(bank[7][:, :], w["wqk"], qr[:, :], start=True, stop=True).then_inc(qk_ready, 1)

                def value_latents(c, grp, m):
                    pe.wait_ge(qkv_kept, c * 3 + 3)
                    pe.wait_ge(turned, m * 4 + 3)
                    nc.tensor.matmul(bank[6][:, :], w["kv2l"][:, grp * P:(grp + 1) * P], qkv[:, 2, :],
                                     start=True, stop=True).then_inc(vlat_ready, 1)

                def values(m):
                    pe.wait_ge(vl_kept, m + 1)
                    for kt in range(QT):
                        mm = nc.tensor.matmul(bank[6][:, kt * LAT:(kt + 1) * LAT], vl[:, kt * P:(kt + 1) * P], w["l2o"],
                                              start=True, stop=True)
                    mm.then_inc(v2_ready, 1)

                def scores(p, grp, m):
                    j, qt = p // QT, p % QT
                    if p == 0:
                        pe.wait_ge(stacked, (m + 1) * PARTS_DMA)
                    after(pe, max_ready, m * ITEMS + p - 1)
                    s = bank[4 + p % 2]
                    nc.tensor.matmul(s[:, 0:(qt + 1) * P], qs1[0:96, grp, j, qt * P:(qt + 1) * P],
                                     ks1[0:96, grp, j, 0:(qt + 1) * P], start=True, stop=False)
                    nc.tensor.matmul(s[:, qt * P:(qt + 1) * P], g.ident_bf, g.mask_qk, start=False, stop=True).then_inc(score_ready, 1)

                def maxima_rows(m):
                    pe.wait_ge(max_twice, m + 1)
                    pe.wait_ge(q1_kept, m + 2)
                    for qt in range(QT):
                        mm = nc.tensor.matmul(bank[7][MAXIMA, qt * P:(qt + 1) * P], mx[:, qt, :], g.ident,
                                              start=True, stop=True)
                    mm.then_inc(maxt_ready, 1)

                def scores_t(n, grp, m):
                    j, kt = n // QT, n % QT
                    if n == 0:
                        pe.wait_ge(m_placed, m + 1)
                    pe.wait_ge(exp_ready, m * ITEMS + n + 1)
                    s = bank[n % 2]
                    at, to = slice(kt * P, (kt + 1) * P), slice(kt * P, CHUNK)
                    nc.tensor.matmul(s[:, to], ks1[0:104, grp, j, at], qs1[0:104, grp, j, to], start=True, stop=False)
                    nc.tensor.matmul(s[:, at], g.ident_bf, g.mask_kq, start=False, stop=False)
                    nc.tensor.matmul(s[:, to], ks2[0:96, grp, j, at], qs2[0:96, grp, j, to], start=False, stop=True).then_inc(st_ready, 1)

                def weigh(n, grp, m, b):
                    j, kt = n // QT, n % QT
                    half, jj = grp // 2, grp % 2 * STEP + j
                    if n == 0:
                        pe.wait_ge(v_kept, m + 1)
                        if grp % 2 == 0:
                            pe.wait_ge(half_kept, b * 2 + half + 1)
                    pe.wait_ge(exp_ready, m * ITEMS + n + 3)
                    nc.tensor.matmul(bank[2 + half][:, kt * P:CHUNK], wide[:, kt, half, jj * P:(jj + 1) * P],
                                     pt[:, n % 4, kt * P:CHUNK], start=(jj == 0 and kt == 0),
                                     stop=(jj == HALF - 1 and kt == QT - 1)).then_inc(pv_ready, 1)

                def project_out(c):
                    pe.wait_ge(y_half, c * 2 + 2)
                    nc.tensor.matmul(bank[4][:, :], w["cproj"], y[:, :], start=True, stop=True).then_inc(out_ready, 1)

                pe.wait_ge(g.loaded["l0a"], 16)
                pe.wait_ge(cleared, 5)
                pe.wait_ge(rows_set, GROUPS)
                project_qkv(0, 0)
                for m in range(2):
                    latents(0, 0, m, m)
                    latents(1, 0, m, m)
                    queries(m)
                    value_latents(0, m, m)
                    values(m)
                for p in range(ITEMS):
                    scores(p, 0, 0)
                maxima_rows(0)
                with pe.Fori(0, CHUNKS) as b:
                    for grp in range(GROUPS):
                        m = b * GROUPS + grp
                        grp1, grp2, c2 = (grp + 1) % GROUPS, (grp + 2) % GROUPS, b + (grp + 2) // GROUPS
                        for n in range(ITEMS + LAG):
                            if n < ITEMS:
                                scores_t(n, grp, m)
                            if n == 0:
                                if grp2 == 0:
                                    project_qkv(c2, m + 2)
                                latents(0, c2, grp2, m + 2)
                            elif n == 1:
                                latents(1, c2, grp2, m + 2)
                            if 1 <= n < 9:
                                if n == 1 and grp == 1:
                                    pe.wait_ge(resid_done, b + 1)
                                for p in range(2 * n - 2, 2 * n):
                                    scores(p, grp1, m + 1)
                                if n == 4:
                                    queries(m + 2)
                            elif n == 9:
                                maxima_rows(m + 1)
                            elif n == 13:
                                value_latents(c2, grp2, m + 2)
                            elif n == 16:
                                values(m + 2)
                            elif n == 17 and grp == 0:
                                project_out(b)
                            if n >= LAG:
                                weigh(n - LAG, grp, m, b)
                project_out(CHUNKS)

            @block.scalar
            def _(act):
                def keep_qkv(c):
                    for i in range(3):
                        act.wait_ge(qkv_ready, c * 3 + i + 1)
                        nc.scalar.activation(qkv[:, i, :], bank[6 + i % 2][:, :], ACT.Identity,
                                             bias=w["bqkv"][:, i:i + 1]).then_inc(qkv_kept, 1)

                def keys_first(m):
                    act.wait_ge(roped, m * 2 + 2)
                    after(act, stacked, m * PARTS_DMA)
                    nc.scalar.copy(kp[:, 0, :], kr[:, :]).then_inc(k1_kept, 1)

                def keys_second(m):
                    act.wait_ge(rest_ready, m * 2 + 1)
                    nc.scalar.copy(kp[:, 1, :], rest[:, 0, :]).then_inc(k2_kept, 1)

                def queries_first(m):
                    act.wait_ge(qk_ready, m + 1)
                    after(act, rest_ready, m * 2)
                    nc.scalar.activation(x[:, :], bank[7][:, :], ACT.Identity, bias=w["wqk_b"]).then_inc(x_kept, 1)
                    after(act, stacked, m * PARTS_DMA)
                    nc.scalar.activation(qp[:, 0, :], bank[7][:, :], ACT.Identity, bias=w["wqk_b"]).then_inc(q1_kept, 1)

                def queries_second(m):
                    act.wait_ge(rest_ready, m * 2 + 2)
                    nc.scalar.copy(qp[:, 1, :], rest[:, 1, :]).then_inc(q2_kept, 1)

                def keep_value_latents(m):
                    act.wait_ge(vlat_ready, m + 1)
                    after(act, v2_ready, m)
                    nc.scalar.activation(vl[:, :], bank[6][:, :], ACT.Identity, bias=w["kv2l_b"]).then_inc(vl_kept, 1)

                def maxima_high(m):
                    act.wait_ge(maxt_ready, m + 1)
                    after(act, m_placed, m)
                    nc.scalar.copy(hi[MAXIMA, :], bank[7][MAXIMA, :]).then_inc(hi_kept, 1)

                act.wait_ge(g.loaded["l0a"], 16)
                keep_qkv(0)
                for m in range(2):
                    keys_first(m)
                    keys_second(m)
                    queries_first(m)
                    queries_second(m)
                    keep_value_latents(m)
                maxima_high(0)
                with act.Fori(0, CHUNKS) as b:
                    for grp in range(GROUPS):
                        m = b * GROUPS + grp
                        for n in range(ITEMS):
                            kt = n % QT
                            act.wait_ge(st_ready, m * ITEMS + n + 1)
                            act.wait_ge(pv_ready, m * ITEMS + n + 1)
                            nc.scalar.activation(pt[:, n % 4, kt * P:CHUNK], bank[n % 2][:, kt * P:CHUNK], ACT.Exp,
                                                 scale=SCALE).then_inc(exp_ready, 1)
                            if n == 0 and grp == 2:
                                keep_qkv(b + 1)
                            elif n == 2:
                                keys_first(m + 2)
                            elif n == 4:
                                keys_second(m + 2)
                            elif n == 5:
                                queries_first(m + 2)
                            elif n == 7:
                                queries_second(m + 2)
                            elif n == 9:
                                maxima_high(m + 1)
                            elif n == 14:
                                keep_value_latents(m + 2)

            @block.gpsimd
            def _(pool):
                nc.gpsimd.memset(wide[:], 0.0).then_inc(cleared, 1)
                pool.wait_ge(cleared, 1)
                nc.gpsimd.memset(pvs[0:64, :, :], 0.0).then_inc(cleared, 1)
                pool.wait_ge(cleared, 2)
                nc.gpsimd.memset(pvs[64:P, :, :], 1.0).then_inc(cleared, 1)
                for half in range(2):
                    pool.wait_ge(cleared, 3 + half)
                    nc.gpsimd.memset(windows(half)[:, :, :, 64:64 + HD], 1.0).then_inc(cleared, 1)

            @block.sync
            def _(sp):
                def stack(grp, m):
                    for n, (part, done) in enumerate(((kp, low_kept), (qp, low_kept))):
                        sp.wait_ge(done, m * 2 + n + 1)
                        sp.dma_start(spread[grp, n].rearrange("i p t -> p i t"), part[:, :, :]).then_inc(bounced, 16)
                        sp.wait_ge(bounced, (m * 2 + n + 1) * 16)
                        for t, row, src, i in moves:
                            if src is part:
                                sp.dma_start(t[row * LAT:(row + 1) * LAT, grp, :, :],
                                             spread[grp, n, i].rearrange("(j l) t -> l j t", l=LAT)).then_inc(stacked, 16)

                stack(0, 0)
                stack(1, 1)
                with sp.Fori(0, CHUNKS) as b:
                    for grp in range(GROUPS):
                        m = b * GROUPS + grp
                        stack((grp + 2) % GROUPS, m + 2)
                sp.wait_ge(stacked, (CHUNKS * GROUPS + 2) * PARTS_DMA)

            @block.vector
            def _(dve):
                def rope(i, m):
                    bias = ("q2l_b", "kv2l_b")[i]
                    after(dve, roped, m * 2 + i)
                    dve.wait_ge(lat_ready, m * 4 + 2 * i + 1)
                    nc.vector.scalar_tensor_tensor(out=rc[:, :], in0=bank[6][:, :], scalar=w[bias], in1=w["cos"],
                                                   op0=ALU.add, op1=ALU.mult).then_inc(turned, 1)
                    dve.wait_ge(lat_ready, m * 4 + 2 * i + 2)
                    nc.vector.scalar_tensor_tensor(out=rs[:, :], in0=bank[7][:, :], scalar=w[bias + "_s"], in1=w["sin"],
                                                   op0=ALU.add, op1=ALU.mult).then_inc(turned, 1)
                    dve.wait_ge(turned, m * 4 + 2 * i + 2)
                    if i == 0:
                        after(dve, qk_ready, m)
                    else:
                        after(dve, k1_kept, m)
                        after(dve, rest_ready, m * 2)
                    nc.vector.tensor_tensor((qr, kr)[i][:, :], rc[:, :], rs[:, :], ALU.add).then_inc(roped, 1)

                def left(i, m):
                    dve.wait_ge((k1_kept, q1_kept)[i], m + 1)
                    after(dve, (k2_kept, q2_kept)[i], m)
                    after(dve, low_kept, m * 2)
                    nc.vector.tensor_tensor(rest[:, i, :], (kr, x)[i][:, :], (kp, qp)[i][:, 0, :], ALU.subtract).then_inc(rest_ready, 1)

                def third(i, m):
                    dve.wait_ge((k2_kept, q2_kept)[i], m + 1)
                    dve.wait_ge(rest_ready, m * 2 + i + 1)
                    after(dve, stacked, m * PARTS_DMA)
                    nc.vector.tensor_tensor((kp, qp)[i][:, 2, :], rest[:, i, :], (kp, qp)[i][:, 1, :], ALU.subtract).then_inc(low_kept, 1)

                def keep_values(grp, m):
                    dve.wait_ge(v2_ready, m + 1)
                    j = grp % 2 * STEP
                    nc.vector.tensor_tensor(windows(grp // 2)[:, :, j:j + STEP, 0:HD],
                                            bank[6][:, 0:QT * LAT].rearrange("p (k j d) -> p k j d", k=QT, d=HD),
                                            w["l2o_b"].unsqueeze(1).unsqueeze(1).broadcast_to([P, QT, STEP, HD]),
                                            ALU.add).then_inc(v_kept, 1)

                def maximum(p, m):
                    j, qt = p // QT, p % QT
                    dve.wait_ge(score_ready, m * ITEMS + p + 1)
                    if p == 0:
                        after(dve, maxt_ready, m)
                    nc.vector.tensor_reduce(mx[:, qt, j:j + 1], bank[4 + p % 2][:, 0:(qt + 1) * P], AX.X, ALU.max).then_inc(max_ready, 1)
                    if p == ITEMS - 1:
                        dve.wait_ge(max_ready, (m + 1) * ITEMS)
                        nc.vector.tensor_copy(mx[:, :, STEP:2 * STEP], mx[:, :, 0:STEP]).then_inc(max_twice, 1)

                def place_maxima(grp, m):
                    dve.wait_ge(hi_kept, m + 1)
                    nc.vector.scalar_tensor_tensor(out=qs1[MAXIMA, grp, :, :],
                                                   in0=hi[MAXIMA, :].unsqueeze(1).broadcast_to([2 * STEP, STEP, CHUNK]),
                                                   scalar=g.is_rest[MAXIMA, :],
                                                   in1=bank[7][MAXIMA, :].unsqueeze(1).broadcast_to([2 * STEP, STEP, CHUNK]),
                                                   op0=ALU.mult, op1=ALU.subtract).then_inc(m_placed, 1)

                def keep_half(half, b):
                    dve.wait_ge(pv_ready, 4 + (b * GROUPS + 2 * half + 2) * ITEMS)
                    dve.wait_ge(y_half, b * 2 + half + 1)
                    nc.vector.tensor_copy(pvs[:, half, :], bank[2 + half][:, :]).then_inc(half_kept, 1)

                def divide(half, n):
                    after(dve, y_half, n)
                    dve.wait_ge(half_kept, n + 1)
                    nc.vector.reciprocal(rd[:, :], pvs[64:P, half, :]).then_inc(recip_done, 1)
                    dve.wait_ge(recip_done, n + 1)
                    nc.vector.tensor_tensor(y[64 * half:64 * half + 64, :], pvs[0:64, half, :], rd[:, :], ALU.mult).then_inc(y_half, 1)

                def add_out(c, at):
                    dve.wait_ge(out_ready, c + 1)
                    nc.vector.tensor_tensor(at, at, bank[4][:, :], ALU.add).then_inc(resid_done, 1)

                dve.wait_ge(g.loaded["l0a"], 16)
                dve.wait_ge(cleared, 5)
                nc.vector.memset(g.mark, 0.0).then_inc(exp_ready, 2)
                dve.wait_ge(exp_ready, 2)
                nc.vector.memset(g.mark, 0.0).then_inc(pv_ready, 4)
                dve.wait_ge(pv_ready, 4)
                nc.vector.memset(g.mark, 0.0).then_inc(half_kept, 2)
                dve.wait_ge(half_kept, 2)
                for grp in range(GROUPS):
                    nc.vector.tensor_copy(ks1[MAXIMA, grp, :, :], g.own_row[MAXIMA, :].unsqueeze(2).broadcast_to(
                        [2 * STEP, STEP, CHUNK])).then_inc(rows_set, 1)
                divide(0, 0)
                for j in range(CHUNKS):
                    nc.vector.tensor_scalar(fixed(g.resid, j), fixed(g.resid, j), w["cproj_b"], None, ALU.add).then_inc(biased, 1)
                for m in range(2):
                    rope(0, m)
                    rope(1, m)
                    left(0, m)
                    third(0, m)
                    left(1, m)
                    third(1, m)
                    keep_values(m, m)
                for p in range(ITEMS):
                    maximum(p, 0)
                place_maxima(0, 0)
                dve.wait_ge(biased, CHUNKS)
                with dve.Fori(0, CHUNKS) as b:
                    for grp in range(GROUPS):
                        m = b * GROUPS + grp
                        if grp == 1:
                            add_out(b, chunk(g.resid, (b + CHUNKS - 1) & (CHUNKS - 1)))
                        rope(0, m + 2)
                        rope(1, m + 2)
                        for n in range(1, 9):
                            for p in range(2 * n - 2, 2 * n):
                                maximum(p, m + 1)
                            if n == 3:
                                left(0, m + 2)
                            elif n == 5:
                                third(0, m + 2)
                            elif n == 6:
                                left(1, m + 2)
                        third(1, m + 2)
                        place_maxima((grp + 1) % GROUPS, m + 1)
                        if grp % 2 == 0:
                            divide(1 - grp // 2, b * 2 + 1 + grp // 2)
                        keep_values((grp + 2) % GROUPS, m + 2)
                        if grp % 2 == 1:
                            keep_half(grp // 2, b)
                divide(1, CHUNKS * 2 + 1)
                add_out(CHUNKS, fixed(g.resid, CHUNKS - 1))


def spread_weights(g, router, experts):
    nc, bank = g.nc, g.bank
    with stage(g, "logit_ready score_kept step weight_ready turned cleared hi_kept rest1 mid_kept mid_moved rest2 "
                  "lo_kept") as (sb, sems):
        (logit_ready, score_kept, step, weight_ready, turned, cleared, hi_kept, rest1, mid_kept, mid_moved, rest2,
         lo_kept) = sems
        scores = sb("r_scores", [P, TILES, experts])
        weights = sb("r_weights", [P, TILES, experts])
        mid = sb("r_mid", [experts, TOKENS], BF16)
        r1 = sb("r_r1", [experts, TOKENS])
        spread = g.banks[4:8, 0:CHUNK][0:experts].rearrange("e a c -> e (a c)")
        with nc.Block() as block:
            @block.tensor
            def _(pe):
                pe.wait_ge(g.loaded[router.pack], 16)
                for t in range(TILES):
                    mm = nc.tensor.matmul(bank[0][:, t * experts:(t + 1) * experts], g.normed[:, t * P:(t + 1) * P],
                                          g.w[router.pack]["router"], start=True, stop=True)
                mm.then_inc(logit_ready, 1)
                pe.wait_ge(weight_ready, 1)
                for t in range(TILES):
                    mm = nc.tensor.transpose(bank[4 + t // QT][0:experts, t % QT * P:(t % QT + 1) * P], weights[:, t, :], g.ident)
                mm.then_inc(turned, 1)

            @block.scalar
            def _(act):
                act.wait_ge(logit_ready, 1)
                nc.scalar.activation(scores[:], bank[0][:, 0:TILES * experts].rearrange("p (t e) -> p t e", e=experts),
                                     router.squash).then_inc(score_kept, 1)
                router.scalar(nc, act, step)
                act.wait_ge(turned, 1)
                act.wait_ge(cleared, 2)
                nc.scalar.copy(g.rows[0:experts, :], spread).then_inc(hi_kept, 1)

            @block.gpsimd
            def _(pool):
                nc.gpsimd.memset(g.rows[:, :], 0.0).then_inc(cleared, 1)
                pool.wait_ge(cleared, 1)
                nc.gpsimd.memset(g.rows[96:97, :], 1.0).then_inc(cleared, 1)

            @block.vector
            def _(dve):
                dve.wait_ge(score_kept, 1)
                router.vector(nc, dve, step, sb, scores, weights).then_inc(weight_ready, 1)
                dve.wait_ge(hi_kept, 1)
                nc.vector.tensor_tensor(r1[:, :], spread, g.rows[0:experts, :], ALU.subtract).then_inc(rest1, 1)
                dve.wait_ge(rest1, 1)
                nc.vector.tensor_copy(mid[:, :], r1[:, :]).then_inc(mid_kept, 1)
                dve.wait_ge(mid_kept, 1)
                nc.vector.tensor_copy(g.rows[32:32 + experts, :], mid[:, :]).then_inc(mid_moved, 1)
                nc.vector.tensor_tensor(r1[:, :], r1[:, :], mid[:, :], ALU.subtract).then_inc(rest2, 1)
                dve.wait_ge(rest2, 1)
                nc.vector.tensor_copy(g.rows[64:64 + experts, :], r1[:, :]).then_inc(lo_kept, 1)


def chosen(nc, link, sb, g, name, values, pick, width):
    top = sb(f"{name}_top", [P, TILES, 8])
    at = sb(f"{name}_at", [P, TILES, 8], U32)
    atf = sb(f"{name}_atf", [P, TILES, 8])
    hot = [sb(f"{name}_hot{k}", [P, TILES, width]) for k in range(pick)]
    for t in range(TILES):
        last = nc.vector.max(top[:, t, :], values[:, t, :])
    link(last)
    for t in range(TILES):
        last = nc.vector.max_index(at[:, t, :], top[:, t, :], values[:, t, :])
    link(last)
    link(nc.vector.tensor_copy(atf[:], at[:]))
    for k in range(pick):
        last = nc.vector.tensor_tensor(hot[k][:], g.iota[:, 0:width].unsqueeze(1).broadcast_to([P, TILES, width]),
                                       atf[:, :, k:k + 1].broadcast_to([P, TILES, width]), ALU.is_equal)
    link(last)
    return top, hot


def linked(dve, step):
    count = [0]

    def link(ins):
        count[0] += 1
        ins.then_inc(step, 1)
        dve.wait_ge(step, count[0])
    return link


class TopTwoRouter:
    pack, squash, experts = "l0f", ACT.Copy, 8

    def __init__(self, g):
        self.g = g

    def scalar(self, nc, act, step):
        act.wait_ge(step, 5)
        nc.scalar.activation(self.e[:], self.e[:], ACT.Exp).then_inc(step, 1)

    def vector(self, nc, dve, step, sb, scores, weights):
        link = linked(dve, step)
        top, (first, second) = chosen(nc, link, sb, self.g, "r_e", scores, 2, 8)
        den = sb("r_den", [P, TILES])
        wide = [P, TILES, 8]
        link(nc.vector.tensor_tensor(self.e[:], top[:, :, 1], top[:, :, 0], ALU.subtract))
        dve.wait_ge(step, 6)
        nc.vector.tensor_scalar(den[:], self.e[:], 1.0, None, ALU.add).then_inc(step, 1)
        dve.wait_ge(step, 7)
        nc.vector.reciprocal(den[:], den[:]).then_inc(step, 1)
        dve.wait_ge(step, 8)
        nc.vector.tensor_tensor(self.e[:], self.e[:], den[:], ALU.mult).then_inc(step, 1)
        nc.vector.tensor_tensor(first[:], first[:], den[:].unsqueeze(2).broadcast_to(wide), ALU.mult).then_inc(step, 1)
        dve.wait_ge(step, 10)
        nc.vector.tensor_tensor(second[:], second[:], self.e[:].unsqueeze(2).broadcast_to(wide), ALU.mult).then_inc(step, 1)
        dve.wait_ge(step, 11)
        return nc.vector.tensor_tensor(weights[:], first[:], second[:], ALU.add)


class GroupedRouter:
    pack, squash, experts = "l1f", ACT.Sigmoid, 16
    SCALE, TINY = 2.5, 1e-20

    def __init__(self, g):
        self.g = g

    def scalar(self, nc, act, step):
        pass

    def vector(self, nc, dve, step, sb, scores, weights):
        link = linked(dve, step)
        wide = [P, TILES, 16]
        biased = sb("r_biased", wide)
        hi = sb("r_hi", [P, TILES, 4, 2])
        lo = sb("r_lo", [P, TILES, 4, 2])
        best = sb("r_best", [P, TILES, 4])
        next1 = sb("r_next1", [P, TILES, 4])
        next2 = sb("r_next2", [P, TILES, 4])
        group = sb("r_group", [P, TILES, 8])
        total = sb("r_total", [P, TILES])
        tt = nc.vector.tensor_tensor
        link(nc.vector.memset(group[:], LOWEST))
        link(tt(biased[:], scores[:], self.g.w["l1f"]["e_bias"].unsqueeze(1).broadcast_to(wide), ALU.add))
        pairs = biased[:].rearrange("p t (q a) -> p t q a", a=2)
        pair = lambda x: x[:].rearrange("p t q a -> p t (q a)")
        link(tt(pair(hi), pairs[:, :, :, 0], pairs[:, :, :, 1], ALU.max))
        link(tt(pair(lo), pairs[:, :, :, 0], pairs[:, :, :, 1], ALU.min))
        link(tt(best[:], hi[:, :, :, 0], hi[:, :, :, 1], ALU.max))
        link(tt(next1[:], hi[:, :, :, 0], hi[:, :, :, 1], ALU.min))
        link(tt(next2[:], lo[:, :, :, 0], lo[:, :, :, 1], ALU.max))
        link(tt(next1[:], next1[:], next2[:], ALU.max))
        link(tt(group[:, :, 0:4], best[:], next1[:], ALU.add))
        _, (g1, g2) = chosen(nc, link, sb, self.g, "r_g", group, 2, 4)
        link(tt(g1[:], g1[:], g2[:], ALU.add))
        quads = lambda x: x[:].rearrange("p t (q a) -> p (t q) a", a=4)
        link(tt(quads(biased), quads(biased), g1[:].rearrange("p t q -> p (t q)").unsqueeze(2).broadcast_to([P, TILES * 4, 4]),
                ALU.mult))
        _, hot = chosen(nc, link, sb, self.g, "r_e", biased, 4, 16)
        for other in hot[1:]:
            link(tt(hot[0][:], hot[0][:], other[:], ALU.add))
        link(tt(weights[:], scores[:], hot[0][:], ALU.mult))
        link(nc.vector.tensor_reduce(total[:], weights[:], AX.X, ALU.add))
        link(nc.vector.tensor_scalar(total[:], total[:], self.TINY, None, ALU.add))
        link(nc.vector.reciprocal(total[:], total[:]))
        link(nc.vector.tensor_scalar(total[:], total[:], self.SCALE, None, ALU.mult))
        return tt(weights[:], weights[:], total[:].unsqueeze(2).broadcast_to(wide), ALU.mult)


def gated_experts(g, router, pick, tiles):
    nc, bank, w = g.nc, g.bank, g.w[router.pack]
    with ExitStack() as ctx:
        g.count += 1
        g.rows = ctx.enter_context(nc.sbuf_tensor(f"rows_{g.count}", [P, TOKENS], BF16))
        router.e = ctx.enter_context(nc.sbuf_tensor(f"router_e_{g.count}", [P, TILES], F32))
        spread_weights(g, router, router.experts)
        with stage(g, "gate_ready up_ready weight_ready gated product_done hidden_ready down_done out_free") as (sb, sems):
            gate_ready, up_ready, weight_ready, gated, product_done, hidden_ready, down_done, out_free = sems
            gate = sb("f_gate", [P, 2, CHUNK])
            prod = sb("f_prod", [P, 2, CHUNK])
            hid = sb("f_hid", [P, 3, CHUNK])
            with nc.Block() as block:
                @block.tensor
                def _(pe):
                    with pe.Fori(0, CHUNKS) as b:
                        x = chunk(g.normed, b)
                        for m in range(tiles + 1):
                            if m < tiles:
                                if m >= 2:
                                    pe.wait_ge(gated, b * tiles + m - 1)
                                nc.tensor.matmul(bank[m % 2][:, :], w["gate"][:, m * P:(m + 1) * P], x,
                                                 start=True, stop=True).then_inc(gate_ready, 1)
                                if m >= 2:
                                    pe.wait_ge(product_done, b * tiles + m - 1)
                                nc.tensor.matmul(bank[2 + m % 2][:, :], w["up"][:, m * P:(m + 1) * P], x,
                                                 start=True, stop=True).then_inc(up_ready, 1)
                                if m >= 2:
                                    pe.wait_ge(hidden_ready, b * tiles + m - 1)
                                nc.tensor.matmul(bank[4 + m % 2][:, :], pick[0:97, m, :], chunk(g.rows, b)[0:97],
                                                 start=True, stop=True).then_inc(weight_ready, 1)
                            if m >= 1:
                                if m == 1:
                                    pe.wait_ge(out_free, b + 1)
                                pe.wait_ge(hidden_ready, b * tiles + m)
                                nc.tensor.matmul(bank[6][:, :], w["down"][:, (m - 1) * P:m * P], hid[:, (m - 1) % 3, :],
                                                      start=(m == 1), stop=(m == tiles)).then_inc(down_done, 1)

                @block.scalar
                def _(act):
                    with act.Fori(0, CHUNKS) as b:
                        for m in range(tiles):
                            act.wait_ge(gate_ready, b * tiles + m + 1)
                            if m >= 2:
                                act.wait_ge(product_done, b * tiles + m - 1)
                            nc.scalar.activation(gate[:, m % 2, :], bank[m % 2][:, :], ACT.Silu).then_inc(gated, 1)

                @block.vector
                def _(dve):
                    nc.vector.memset(g.mark, 0.0).then_inc(out_free, 1)
                    with dve.Fori(0, CHUNKS) as b:
                        for m in range(tiles):
                            dve.wait_ge(up_ready, b * tiles + m + 1)
                            dve.wait_ge(gated, b * tiles + m + 1)
                            nc.vector.tensor_tensor(prod[:, m % 2, :], gate[:, m % 2, :], bank[2 + m % 2][:, :],
                                                    ALU.mult).then_inc(product_done, 1)
                            dve.wait_ge(product_done, b * tiles + m + 1)
                            dve.wait_ge(weight_ready, b * tiles + m + 1)
                            if m >= 3:
                                dve.wait_ge(down_done, b * tiles + m - 2)
                            nc.vector.tensor_tensor(hid[:, m % 3, :], prod[:, m % 2, :], bank[4 + m % 2][:, :],
                                                    ALU.mult).then_inc(hidden_ready, 1)
                        dve.wait_ge(down_done, b * tiles + tiles)
                        nc.vector.tensor_tensor(chunk(g.resid, b), chunk(g.resid, b), bank[6][:, :], ALU.add).then_inc(out_free, 1)


def top_two_experts(g):
    gated_experts(g, TopTwoRouter(g), g.route0, 14)


def grouped_experts(g):
    gated_experts(g, GroupedRouter(g), g.route1, 9)


def plain_attention(g):
    nc, bank, w = g.nc, g.bank, g.w["l0b"]
    SCALE = P ** -0.5
    with stage(g, "proj_ready proj_kept vsum_ready score_ready max_ready negated exp_ready sum_inv row_ready diag_ready "
                  "spread_ready fc_ready fc_kept scaled h_ready mean_ready centred squared var_ready logged rstd_ready "
                  "normed affine resid_done") as (sb, sems):
        (proj_ready, proj_kept, vsum_ready, score_ready, max_ready, negated, exp_ready, sum_inv, row_ready, diag_ready,
         spread_ready, fc_ready, fc_kept, scaled, h_ready, mean_ready, centred, squared, var_ready, logged, rstd_ready,
         normed, affine, resid_done) = sems
        qk = sb("p_qk", [P, 2, CHUNK])
        vsum = sb("p_vsum", [P, 1])
        mx = sb("p_mx", [P, QT])
        exp = sb("p_exp", [P, CHUNK])
        total = sb("p_total", [P, QT])
        inv = sb("p_inv", [P, QT])
        diag = sb("p_diag", [P, QT, P])
        fc = sb("p_fc", [P, 1])
        h = sb("p_h", [P, CHUNK])
        sq = sb("p_sq", [P, CHUNK])
        rstd = sb("p_rstd", [P, CHUNK])
        with nc.Block() as block:
            @block.tensor
            def _(pe):
                pe.wait_ge(g.loaded["l0b"], 16)
                with pe.Fori(0, CHUNKS) as b:
                    pe.wait_ge(resid_done, b + 1)
                    for i in range(3):
                        nc.tensor.matmul(bank[i][:, :], w["wqkv"][:, i * P:(i + 1) * P], chunk(g.normed, b),
                                         start=True, stop=True).then_inc(proj_ready, 1)
                    pe.wait_ge(proj_kept, b * 2 + 2)
                    for qt in range(QT):
                        mm = nc.tensor.matmul(bank[4 + qt][:, :], qk[:, 0, qt * P:(qt + 1) * P], qk[:, 1, :], start=True, stop=True)
                    mm.then_inc(score_ready, 1)
                    pe.wait_ge(vsum_ready, b + 1)
                    nc.tensor.matmul(bank[3][:, 0:1], w["wfc"], vsum[:, :], start=True, stop=True).then_inc(fc_ready, 1)
                    pe.wait_ge(diag_ready, b * QT + QT)
                    for qt in range(QT):
                        mm = nc.tensor.matmul(bank[0][:, qt * P:(qt + 1) * P], g.ones, diag[:, qt, :], start=True, stop=True)
                    mm.then_inc(spread_ready, 1)
                    pe.wait_ge(h_ready, b + 1)
                    nc.tensor.matmul(bank[1][:, :], g.mean_of, h[:, :], start=True, stop=True).then_inc(mean_ready, 1)
                    pe.wait_ge(squared, b + 1)
                    nc.tensor.matmul(bank[2][:, :], g.mean_of, sq[:, :], start=True, stop=True).then_inc(var_ready, 1)

            @block.scalar
            def _(act):
                with act.Fori(0, CHUNKS) as b:
                    for i in range(2):
                        act.wait_ge(proj_ready, b * 3 + i + 1)
                        nc.scalar.copy(qk[:, i, :], bank[i][:, :]).then_inc(proj_kept, 1)
                    act.wait_ge(negated, b + 1)
                    for qt in range(QT):
                        if qt >= 1:
                            act.wait_ge(exp_ready, b * QT + qt)
                        nc.scalar.activation(exp[:, :], bank[4 + qt][:, :], ACT.Exp, bias=mx[:, qt:qt + 1], scale=SCALE,
                                             accum_out=total[:, qt:qt + 1]).then_inc(exp_ready, 1)
                    act.wait_ge(fc_ready, b + 1)
                    nc.scalar.copy(fc[:, :], bank[3][:, 0:1]).then_inc(fc_kept, 1)
                    act.wait_ge(centred, b + 1)
                    nc.scalar.activation(sq[:, :], h[:, :], ACT.Square).then_inc(squared, 1)
                    act.wait_ge(var_ready, b + 1)
                    nc.scalar.activation(rstd[:, :], bank[2][:, :], ACT.Ln, bias=g.eps5).then_inc(logged, 1)
                    act.wait_ge(logged, b + 1)
                    nc.scalar.activation(rstd[:, :], rstd[:, :], ACT.Exp, scale=-0.5).then_inc(rstd_ready, 1)

            @block.vector
            def _(dve):
                nc.vector.memset(g.mark, 0.0).then_inc(resid_done, 1)
                with dve.Fori(0, CHUNKS) as b:
                    dve.wait_ge(proj_ready, b * 3 + 3)
                    nc.vector.tensor_reduce(vsum[:, :], bank[2][:, :], AX.X, ALU.add).then_inc(vsum_ready, 1)
                    dve.wait_ge(score_ready, b + 1)
                    nc.vector.tensor_reduce(mx[:, :], g.banks[4:8, 0:CHUNK], AX.X, ALU.max).then_inc(max_ready, 1)
                    dve.wait_ge(max_ready, b + 1)
                    nc.vector.tensor_scalar(mx[:, :], mx[:, :], -SCALE, None, ALU.mult).then_inc(negated, 1)
                    dve.wait_ge(exp_ready, b * QT + QT)
                    nc.vector.reciprocal(inv[:, :], total[:, :]).then_inc(sum_inv, 1)
                    dve.wait_ge(sum_inv, b + 1)
                    nc.vector.tensor_tensor(inv[:, :], inv[:, :], total[:, :], ALU.mult).then_inc(row_ready, 1)
                    dve.wait_ge(row_ready, b + 1)
                    for qt in range(QT):
                        nc.vector.tensor_scalar(diag[:, qt, :], g.ident, inv[:, qt:qt + 1], None, ALU.mult).then_inc(diag_ready, 1)
                    dve.wait_ge(spread_ready, b + 1)
                    dve.wait_ge(fc_kept, b + 1)
                    nc.vector.tensor_scalar(h[:, :], bank[0][:, :], fc[:, :], w["b_fc"], ALU.mult, ALU.add).then_inc(scaled, 1)
                    dve.wait_ge(scaled, b + 1)
                    nc.vector.tensor_tensor(h[:, :], h[:, :], chunk(g.normed, b), ALU.add).then_inc(h_ready, 1)
                    dve.wait_ge(mean_ready, b + 1)
                    nc.vector.tensor_tensor(h[:, :], h[:, :], bank[1][:, :], ALU.subtract).then_inc(centred, 1)
                    dve.wait_ge(rstd_ready, b + 1)
                    dve.wait_ge(centred, b + 1)
                    nc.vector.tensor_tensor(h[:, :], h[:, :], rstd[:, :], ALU.mult).then_inc(normed, 1)
                    dve.wait_ge(normed, b + 1)
                    nc.vector.tensor_scalar(h[:, :], h[:, :], w["gamma"], w["beta"], ALU.mult, ALU.add).then_inc(affine, 1)
                    dve.wait_ge(affine, b + 1)
                    nc.vector.tensor_tensor(chunk(g.resid, b), chunk(g.resid, b), h[:, :], ALU.add).then_inc(resid_done, 1)


def recurrent_heads(g):
    nc, bank, w = g.nc, g.bank, g.w["l1a"]
    PAIRS, S, BLOCK = 8, 64, 8
    GROUP = PAIRS // 2
    WIDTH = GROUP * BATCH
    TURN = 2 * BLOCK
    TURNS, SPAN = TIME // TURN, 128
    with stage(g, "weights_bounded a1_kept a_rest a2_kept a_rest2 a_split squared ms_ready logged rms_ready x_ready cleared "
                  "laid_free laid drive0 drive1 summed0 summed1 state0 state1 rest0 rest1 last0 last1 kept mix_ready mix_kept "
                  "out_ready biased resid_done") as (sb, sems):
        (weights_bounded, a1_kept, a_rest, a2_kept, a_rest2, a_split, squared, ms_ready, logged, rms_ready, x_ready, cleared,
         laid_free, laid, drive0, drive1, summed0, summed1, state0, state1, rest0, rest1, last0, last1, kept, mix_ready, mix_kept,
         out_ready, biased, resid_done) = sems
        drive, summed, state, rest, last = (drive0, drive1), (summed0, summed1), (state0, state1), (rest0, rest1), (last0, last1)
        at = sb("h_at", [P, PAIRS * P])
        left = sb("h_left", [P, PAIRS * P])
        parts = sb("h_parts", [P, 3, PAIRS, P], BF16)
        sq = sb("h_sq", [P, TOKENS])
        rms = sb("h_rms", [P, TOKENS])
        xt = sb("h_xt", [P, TIME, BATCH])
        lay = sb("h_lay", [P, 2, 2, BLOCK, WIDTH])
        ring = sb("h_ring", [P, TURN, 2, 3, WIDTH])
        pre = sb("h_pre", [P, 2, WIDTH])
        hist = sb("h_hist", [P, TIME, 2, WIDTH])
        mix = sb("h_mix", [P, BATCH, TIME])
        upper = ring[:].rearrange("p s g q c -> p (s g q c)").bitcast(BF16).rearrange(
            "p (s g q c two) -> p s g q c two", g=2, q=3, c=WIDTH, two=2)[:, :, :, :, :, 1]

        def columns_of(blk, grp):
            return bank[2 * blk + grp][:, 0:BLOCK * 3 * WIDTH].rearrange("p (s q c) -> p s q c", q=3, c=WIDTH)

        with nc.Block() as block:
            @block.tensor
            def _(pe):
                pe.wait_ge(g.loaded["l1a"], 16)
                for j in range(CHUNKS):
                    pe.wait_ge(squared, j + 1)
                    nc.tensor.matmul(bank[4 + j][:, :], g.mean_of, fixed(sq, j), start=True, stop=True).then_inc(ms_ready, 1)

                def lay_inputs(blk, grp, n):
                    pe.wait_ge(laid, n)
                    nc.tensor.matmul(columns_of(blk, grp)[:, :, 0, :], w["b"], lay[:, blk, grp, :, :],
                                     start=True, stop=True).then_inc(laid_free, 1)

                def add_part(part, s, grp):
                    for p in range(GROUP):
                        cols = slice(BATCH * p, BATCH * p + BATCH)
                        mm = nc.tensor.matmul(columns_of(s // BLOCK, grp)[:, s % BLOCK, 0:3 - part, cols],
                                              parts[:, part, GROUP * grp + p, :], upper[:, (s - 1) % TURN, grp, 0:3 - part, cols],
                                              start=False, stop=True, skip_group_check=True)
                    return mm

                for grp in range(2):
                    lay_inputs(0, grp, 1)
                pe.wait_ge(a_split, 1)
                with pe.Fori(0, TURNS) as i:
                    for s in range(TURN):
                        n = i * TURN + s + 1
                        if s % BLOCK in (2, 3):
                            lay_inputs(1 - s // BLOCK, s % BLOCK - 2, i * 2 + 2 + s // BLOCK)
                        for grp in range(2):
                            pe.wait_ge(state[grp], n)
                            add_part(2, s, grp)
                        for grp in range(2):
                            pe.wait_ge(rest[grp], n)
                            add_part(1, s, grp)
                        for grp in range(2):
                            pe.wait_ge(last[grp], n)
                            add_part(0, s, grp).then_inc(drive[grp], 1)
                pe.wait_ge(kept, 2 * TURNS + 2)
                for c in range(TIME // SPAN):
                    for p in range(PAIRS):
                        grp, col = p // GROUP, p % GROUP * BATCH
                        mm = nc.tensor.matmul(bank[4 + c][:, :], w["c"][:, p * P:(p + 1) * P],
                                              hist[:, c * SPAN:(c + 1) * SPAN, grp, col:col + BATCH],
                                              start=(p == 0), stop=(p == PAIRS - 1))
                    mm.then_inc(mix_ready, 1)
                pe.wait_ge(mix_kept, TIME // SPAN)
                for j in range(CHUNKS):
                    nc.tensor.matmul(bank[j][:, :], w["out"], mix[:, j, :], start=True, stop=True).then_inc(out_ready, 1)

            @block.scalar
            def _(act):
                act.wait_ge(g.loaded["l1a"], 16)
                for j in range(CHUNKS):
                    nc.scalar.activation(fixed(sq, j), fixed(g.normed, j), ACT.Square).then_inc(squared, 1)
                for j in range(CHUNKS):
                    act.wait_ge(ms_ready, j + 1)
                    nc.scalar.activation(fixed(rms, j), bank[4 + j][:, :], ACT.Ln, bias=g.eps4).then_inc(logged, 1)
                for j in range(CHUNKS):
                    act.wait_ge(logged, j + 1)
                    nc.scalar.activation(fixed(rms, j), fixed(rms, j), ACT.Exp, scale=-0.5).then_inc(rms_ready, 1)
                nc.scalar.activation(at[:, :], w["a"], ACT.Tanh).then_inc(weights_bounded, 1)
                act.wait_ge(cleared, 1)
                with act.Fori(0, TURNS) as i:
                    for s in range(TURN):
                        if s % BLOCK == 0:
                            act.wait_ge(kept, i * 2 + s // BLOCK + 1)
                        for grp in range(2):
                            act.wait_ge(summed[grp], i * TURN + s + 1)
                            nc.scalar.activation(ring[:, s, grp, 0, :], pre[:, grp, :], ACT.Tanh).then_inc(state[grp], 1)

            @block.gpsimd
            def _(pool):
                nc.gpsimd.memset(ring[:], 0.0).then_inc(cleared, 1)
                pool.wait_ge(cleared, 1)
                nc.gpsimd.memset(g.mark2[:, 0:1], 0.0).then_inc(kept, 2)

                def put(blk, x):
                    for grp in range(2):
                        own = g.pair_of[:, GROUP * grp:GROUP * grp + GROUP]
                        done = nc.gpsimd.tensor_tensor(
                            lay[:, blk, grp, :, :].rearrange("p s (a b) -> p s a b", b=BATCH),
                            own.unsqueeze(1).unsqueeze(3).broadcast_to([P, BLOCK, GROUP, BATCH]),
                            x.unsqueeze(2).broadcast_to([P, BLOCK, GROUP, BATCH]), ALU.mult)
                    done.then_inc(laid, 1)

                def keep(blk, i):
                    for grp in range(2):
                        pool.wait_ge(state[grp], i * TURN + blk * BLOCK + BLOCK + 1)
                    nc.gpsimd.tensor_copy(hist[:, bass.ds(i * TURN + blk * BLOCK, BLOCK), :, :],
                                          ring[:, blk * BLOCK:(blk + 1) * BLOCK, :, 0, :]).then_inc(kept, 1)

                pool.wait_ge(x_ready, CHUNKS)
                for blk in range(2):
                    put(blk, xt[:, blk * BLOCK:(blk + 1) * BLOCK, :])
                with pool.Fori(0, TURNS) as i:
                    for blk in range(2):
                        pool.wait_ge(laid_free, i * 4 + blk * 2 + 2)
                        put(blk, xt[:, bass.ds(((i + 1) & (TURNS - 1)) * TURN + blk * BLOCK, BLOCK), :])
                        keep(blk, i)

            @block.vector
            def _(dve):
                dve.wait_ge(g.loaded["l1a"], 16)
                for sem in state + rest + last:
                    nc.vector.memset(g.mark, 0.0).then_inc(sem, 1)
                    dve.wait_ge(sem, 1)
                dve.wait_ge(cleared, 1)
                for j in range(CHUNKS):
                    dve.wait_ge(rms_ready, j + 1)
                    nc.vector.scalar_tensor_tensor(out=xt[:, :, j], in0=fixed(g.normed, j), scalar=w["norm_w"],
                                                   in1=fixed(rms, j), op0=ALU.mult, op1=ALU.mult).then_inc(x_ready, 1)
                a_part = [parts[:, q, :, :].rearrange("p a t -> p (a t)") for q in range(3)]
                dve.wait_ge(weights_bounded, 1)
                nc.vector.tensor_copy(a_part[0], at[:, :]).then_inc(a1_kept, 1)
                dve.wait_ge(a1_kept, 1)
                nc.vector.tensor_tensor(left[:, :], at[:, :], a_part[0], ALU.subtract).then_inc(a_rest, 1)
                dve.wait_ge(a_rest, 1)
                nc.vector.tensor_copy(a_part[1], left[:, :]).then_inc(a2_kept, 1)
                dve.wait_ge(a2_kept, 1)
                nc.vector.tensor_tensor(a_part[2], left[:, :], a_part[1], ALU.subtract).then_inc(a_split, 1)

                def sum_up(s, grp, n):
                    dve.wait_ge(drive[grp], n)
                    nc.vector.tensor_reduce(pre[:, grp, :], columns_of(s // BLOCK, grp)[:, s % BLOCK, :, :].rearrange("p q c -> p c q"),
                                            AX.X, ALU.add).then_inc(summed[grp], 1)

                def cut_first(s, grp, n):
                    dve.wait_ge(state[grp], n)
                    nc.vector.tensor_tensor(ring[:, s, grp, 1, :], ring[:, s, grp, 0, :], upper[:, s, grp, 0, :],
                                            ALU.subtract).then_inc(rest[grp], 1)

                def cut_second(s, grp, n):
                    dve.wait_ge(rest[grp], n)
                    nc.vector.tensor_tensor(ring[:, s, grp, 2, :], ring[:, s, grp, 1, :], upper[:, s, grp, 1, :],
                                            ALU.subtract).then_inc(last[grp], 1)

                with dve.Fori(0, TURNS) as i:
                    for s in range(TURN):
                        n = i * TURN + s + 1
                        for grp in range(2):
                            sum_up(s, grp, n)
                        for grp in range(2):
                            cut_first(s, grp, n + 1)
                        for grp in range(2):
                            cut_second(s, grp, n + 1)
                for c in range(TIME // SPAN):
                    at_span = slice(c * SPAN, (c + 1) * SPAN)
                    dve.wait_ge(mix_ready, c + 1)
                    nc.vector.scalar_tensor_tensor(
                        out=mix[:, :, at_span].rearrange("p b t -> p t b"), in0=xt[:, at_span, :], scalar=w["skip"],
                        in1=bank[4 + c][:, :].rearrange("p (t b) -> p t b", b=BATCH), op0=ALU.mult, op1=ALU.add).then_inc(mix_kept, 1)
                for j in range(CHUNKS):
                    nc.vector.tensor_tensor(fixed(g.resid, j), fixed(g.resid, j), fixed(g.normed, j), ALU.add).then_inc(biased, 1)
                for j in range(CHUNKS):
                    dve.wait_ge(out_ready, j + 1)
                    dve.wait_ge(biased, j + 1)
                    nc.vector.scalar_tensor_tensor(out=fixed(g.resid, j), in0=bank[j][:, :], scalar=w["b_out"],
                                                   in1=fixed(g.resid, j), op0=ALU.add, op1=ALU.add).then_inc(resid_done, 1)


def cumulative_attention(g):
    nc, bank, w = g.nc, g.bank, g.w["l1b"]
    EPS = 1e-3
    with stage(g, "proj_ready shifted lowered exp_ready v_kept raised kv_done ksum kvsum weighed den_ready clipped inverted "
                  "numer y_ready out_ready resid_done ones_set") as (sb, sems):
        (proj_ready, shifted, lowered, exp_ready, v_kept, raised, kv_done, ksum, kvsum, weighed, den_ready, clipped, inverted,
         numer, y_ready, out_ready, resid_done, ones_set) = sems
        one = sb("c_one", [P, CHUNK])
        t = sb("c_t", [P, 2, CHUNK])
        e = sb("c_e", [P, 2, CHUNK])
        qk = sb("c_qk", [P, 2, CHUNK])
        v = sb("c_v", [P, CHUNK])
        kc = sb("c_kc", [P, CHUNK])
        kvc = sb("c_kvc", [P, CHUNK])
        r = sb("c_r", [P, CHUNK])
        with nc.Block() as block:
            @block.tensor
            def _(pe):
                pe.wait_ge(g.loaded["l1b"], 16)
                with pe.Fori(0, CHUNKS) as b:
                    pe.wait_ge(resid_done, b + 1)
                    for i in range(3):
                        nc.tensor.matmul(bank[i][:, :], w["wqkv"][:, i * P:(i + 1) * P], chunk(g.normed, b),
                                         start=True, stop=True).then_inc(proj_ready, 1)
                    pe.wait_ge(weighed, b + 1)
                    nc.tensor.matmul(bank[3][:, :], g.same8, r[:, :], start=True, stop=True).then_inc(den_ready, 1)
                    pe.wait_ge(y_ready, b + 1)
                    nc.tensor.matmul(bank[4][:, :], w["wproj"], v[:, :], start=True, stop=True).then_inc(out_ready, 1)

            @block.scalar
            def _(act):
                act.wait_ge(g.loaded["l1b"], 16)
                with act.Fori(0, CHUNKS) as b:
                    for i in range(2):
                        act.wait_ge(lowered, b * 2 + i + 1)
                        nc.scalar.activation(e[:, i, :], e[:, i, :], ACT.Exp).then_inc(exp_ready, 1)
                    act.wait_ge(proj_ready, b * 3 + 3)
                    nc.scalar.activation(v[:, :], bank[2][:, :], ACT.Identity, bias=w["bqkv"][:, 2:3]).then_inc(v_kept, 1)

            @block.vector
            def _(dve):
                dve.wait_ge(g.loaded["l1b"], 16)
                nc.vector.memset(one[:, :], 1.0).then_inc(ones_set, 1)
                nc.vector.memset(g.mark, 0.0).then_inc(resid_done, 1)
                dve.wait_ge(ones_set, 1)
                with dve.Fori(0, CHUNKS) as b:
                    for i in range(2):
                        dve.wait_ge(proj_ready, b * 3 + i + 1)
                        nc.vector.tensor_scalar(t[:, i, :], bank[i][:, :], w["bqkv"][:, i:i + 1], w["scale"], ALU.add,
                                                ALU.mult).then_inc(shifted, 1)
                        dve.wait_ge(shifted, b * 2 + i + 1)
                        nc.vector.tensor_scalar(e[:, i, :], t[:, i, :], 0.0, None, ALU.min).then_inc(lowered, 1)
                    for i in range(2):
                        dve.wait_ge(exp_ready, b * 2 + i + 1)
                        nc.vector.scalar_tensor_tensor(out=qk[:, i, :], in0=t[:, i, :], scalar=0.0, in1=e[:, i, :],
                                                       op0=ALU.max, op1=ALU.add).then_inc(raised, 1)
                    dve.wait_ge(raised, b * 2 + 2)
                    nc.vector.tensor_tensor_scan(kc[:, :], one[:, :], qk[:, 1, :], 0.0, ALU.mult, ALU.add).then_inc(ksum, 1)
                    dve.wait_ge(v_kept, b + 1)
                    nc.vector.tensor_tensor(t[:, 0, :], qk[:, 1, :], v[:, :], ALU.mult).then_inc(kv_done, 1)
                    dve.wait_ge(ksum, b + 1)
                    nc.vector.tensor_tensor(r[:, :], qk[:, 0, :], kc[:, :], ALU.mult).then_inc(weighed, 1)
                    dve.wait_ge(kv_done, b + 1)
                    nc.vector.tensor_tensor_scan(kvc[:, :], one[:, :], t[:, 0, :], 0.0, ALU.mult, ALU.add).then_inc(kvsum, 1)
                    dve.wait_ge(den_ready, b + 1)
                    nc.vector.tensor_scalar(r[:, :], bank[3][:, :], EPS, None, ALU.max).then_inc(clipped, 1)
                    dve.wait_ge(clipped, b + 1)
                    nc.vector.reciprocal(r[:, :], r[:, :]).then_inc(inverted, 1)
                    dve.wait_ge(kvsum, b + 1)
                    nc.vector.tensor_tensor(kvc[:, :], kvc[:, :], qk[:, 0, :], ALU.mult).then_inc(numer, 1)
                    dve.wait_ge(numer, b + 1)
                    dve.wait_ge(inverted, b + 1)
                    nc.vector.tensor_tensor(v[:, :], kvc[:, :], r[:, :], ALU.mult).then_inc(y_ready, 1)
                    dve.wait_ge(out_ready, b + 1)
                    nc.vector.scalar_tensor_tensor(out=chunk(g.resid, b), in0=bank[4][:, :], scalar=w["bproj"],
                                                   in1=chunk(g.resid, b), op0=ALU.add, op1=ALU.add).then_inc(resid_done, 1)


def dense_ffn(g):
    nc, bank, w = g.nc, g.bank, g.w["l2f"]
    HID = 4
    with stage(g, "gate_ready gated up_ready h_ready act_ready act_done out_ready resid_done") as (sb, sems):
        gate_ready, gated, up_ready, h_ready, act_ready, act_done, out_ready, resid_done = sems
        gate = sb("d_gate", [P, 2, CHUNK])
        h = sb("d_h", [P, 3, HID, CHUNK])
        with nc.Block() as block:
            @block.tensor
            def _(pe):
                pe.wait_ge(g.loaded["l2f"], 16)
                with pe.Fori(0, CHUNKS) as b:
                    for m in range(HID):
                        if m >= 2:
                            pe.wait_ge(gated, b * HID + m - 1)
                        nc.tensor.matmul(bank[m % 2][:, :], w["w1"][:, m * P:(m + 1) * P], chunk(g.normed, b),
                                         start=True, stop=True).then_inc(gate_ready, 1)
                        if m >= 2:
                            pe.wait_ge(h_ready, b * HID + m - 1)
                        nc.tensor.matmul(bank[2 + m % 2][:, :], w["w2"][:, m * P:(m + 1) * P], chunk(g.normed, b),
                                         start=True, stop=True).then_inc(up_ready, 1)
                    for layer, name in ((0, "h1"), (1, "h2")):
                        for m in range(HID):
                            n = layer * HID + m
                            if n >= 3:
                                pe.wait_ge(act_done, b * 2 * HID + n - 2)
                            for k in range(HID):
                                if layer == 0:
                                    pe.wait_ge(h_ready, b * HID + k + 1)
                                else:
                                    pe.wait_ge(act_done, b * 2 * HID + k + 1)
                                mm = nc.tensor.matmul(bank[4 + n % 3][:, :], w[name][:, k * CHUNK + m * P:k * CHUNK + (m + 1) * P],
                                                      h[:, layer, k, :], start=(k == 0), stop=(k == HID - 1))
                            mm.then_inc(act_ready, 1)
                    pe.wait_ge(resid_done, b + 1)
                    for k in range(HID):
                        pe.wait_ge(act_done, b * 2 * HID + HID + k + 1)
                        mm = nc.tensor.matmul(bank[7][:, :], w["w3"][:, k * P:(k + 1) * P], h[:, 2, k, :],
                                              start=(k == 0), stop=(k == HID - 1))
                    mm.then_inc(out_ready, 1)

            @block.scalar
            def _(act):
                act.wait_ge(g.loaded["l2f"], 16)
                with act.Fori(0, CHUNKS) as b:
                    for m in range(HID):
                        act.wait_ge(gate_ready, b * HID + m + 1)
                        if m >= 2:
                            act.wait_ge(h_ready, b * HID + m - 1)
                        nc.scalar.activation(gate[:, m % 2, :], bank[m % 2][:, :], ACT.Silu,
                                             scale=w["s1"][:, m:m + 1]).then_inc(gated, 1)
                    for n in range(2 * HID):
                        act.wait_ge(act_ready, b * 2 * HID + n + 1)
                        scale = w["sh1" if n < HID else "sh2"][:, n % HID:n % HID + 1]
                        nc.scalar.activation(h[:, 1 + n // HID, n % HID, :], bank[4 + n % 3][:, :], ACT.Gelu,
                                             scale=scale).then_inc(act_done, 1)

            @block.vector
            def _(dve):
                dve.wait_ge(g.loaded["l2f"], 16)
                nc.vector.memset(g.mark, 0.0).then_inc(resid_done, 1)
                with dve.Fori(0, CHUNKS) as b:
                    for m in range(HID):
                        dve.wait_ge(up_ready, b * HID + m + 1)
                        dve.wait_ge(gated, b * HID + m + 1)
                        nc.vector.scalar_tensor_tensor(out=h[:, 0, m, :], in0=bank[2 + m % 2][:, :], scalar=w["s2"][:, m:m + 1],
                                                       in1=gate[:, m % 2, :], op0=ALU.mult, op1=ALU.mult).then_inc(h_ready, 1)
                    dve.wait_ge(out_ready, b + 1)
                    nc.vector.scalar_tensor_tensor(out=chunk(g.resid, b), in0=bank[7][:, :], scalar=w["s3"],
                                                   in1=chunk(g.resid, b), op0=ALU.mult, op1=ALU.add).then_inc(resid_done, 1)


def selective_scan(g, pack, ranks):
    nc, bank, w = g.nc, g.bank, g.w[pack]
    N, TAPS, BR = 16, 4, len(ranks)
    ITEMS = 2 * N
    with stage(g, "decay_ready negated skip_ready cleared in_ready x_kept z_ready tap_done conv_done u_ready dt_ready bc_ready dt_kept "
                  "hi_kept rest1 mid_kept mid_moved rest2 lo_kept delta_ready abs_done pos_done exp_done grown log_done inv_done "
                  "lost lost_part delta_sum delta_done du_done y_zeroed b_spread c_spread b_kept da_ready dbu_ready scan_done "
                  "term_ready y_added skipped gated out_ready resid_done") as (sb, sems):
        (decay_ready, negated, skip_ready, cleared, in_ready, x_kept, z_ready, tap_done, conv_done, u_ready, dt_ready, bc_ready, dt_kept,
         hi_kept, rest1, mid_kept, mid_moved, rest2, lo_kept, delta_ready, abs_done, pos_done, exp_done, grown, log_done, inv_done,
         lost, lost_part, delta_sum, delta_done, du_done, y_zeroed, b_spread, c_spread, b_kept, da_ready, dbu_ready, scan_done,
         term_ready, y_added, skipped, gated, out_ready, resid_done) = sems
        decay = sb("s_decay", [P, BR, 2 * N])
        skip = sb("s_skip", [P, 2])
        xp = sb("s_xp", [P, 2, TAPS - 1 + CHUNK])
        conv = sb("s_conv", [P, 2, 2, CHUNK])
        u = sb("s_u", [P, 2, CHUNK])
        z = sb("s_z", [P, 2, CHUNK])
        dt = sb("s_dt", [64, CHUNK])
        bc = sb("s_bc", [96, CHUNK], BF16)
        mid = sb("s_mid", [32, CHUNK], BF16)
        r1 = sb("s_r1", [32, CHUNK])
        mag = sb("s_mag", [P, 2, CHUNK])
        grow = sb("s_grow", [P, 2, CHUNK])
        delta = sb("s_delta", [P, 2, CHUNK])
        du = sb("s_du", [P, 2, CHUNK])
        zero = sb("s_zero", [P, CHUNK], BF16)
        bb = sb("s_bb", [P, 3, CHUNK])
        da = sb("s_da", [P, 4, CHUNK])
        dbu = sb("s_dbu", [P, 4, CHUNK])
        hh = sb("s_hh", [P, 4, CHUNK])
        term = sb("s_term", [P, 4, CHUNK])
        y = sb("s_y", [P, 2, CHUNK])
        log, inv, pos = conv[:, 0, :, :], conv[:, 1, :, :], y
        halves = g.banks[0:2, 0:CHUNK]
        with nc.Block() as block:
            @block.tensor
            def _(pe):
                pe.wait_ge(g.loaded[pack], 16)
                pe.wait_ge(cleared, 2)

                def project(xs):
                    for m in range(4):
                        nc.tensor.matmul(bank[m][:, :], w["in"][:, m * P:(m + 1) * P], xs, start=True, stop=True).then_inc(in_ready, 1)

                project(fixed(g.normed, 0))
                with pe.Fori(0, CHUNKS) as b:
                    pe.wait_ge(resid_done, b + 1)
                    for half in range(2):
                        mm = nc.tensor.matmul(bank[6 + half][:, :], g.ident_bf, zero[:, :], start=True, stop=True)
                    for r, rank in enumerate(ranks):
                        turn = b * BR + r
                        for half in range(2):
                            pe.wait_ge(u_ready, b * 2 + half + 1)
                            mm = nc.tensor.matmul(bank[4][0:rank, :], w[f"xdt{r}"][:, half * rank:(half + 1) * rank], u[:, half, :],
                                                  start=(half == 0), stop=(half == 1))
                        mm.then_inc(dt_ready, 1)
                        for half in range(2):
                            mm = nc.tensor.matmul(bank[5][0:32, :], w[f"xbc{r}"][:, half * 32:(half + 1) * 32], u[:, half, :],
                                                  start=(half == 0), stop=(half == 1))
                        mm.then_inc(bc_ready, 1)
                        pe.wait_ge(dt_kept, turn + 1)
                        for half in range(2):
                            nc.tensor.matmul(bank[half][:, :], w[f"dtw{r}"][:, half * P:(half + 1) * P], dt[0:rank, :],
                                             start=True, stop=True).then_inc(delta_ready, 1)
                        pe.wait_ge(hi_kept, turn + 1)
                        pe.wait_ge(mid_moved, turn + 1)
                        pe.wait_ge(lo_kept, turn + 1)
                        pe.wait_ge(abs_done, turn * 2 + 2)
                        pe.wait_ge(pos_done, turn * 2 + 2)
                        pe.wait_ge(z_ready, b * 2 + 2)
                        for n in range(-1, N + 2):
                            if n + 1 < N:
                                if n + 1 >= 2:
                                    pe.wait_ge(b_kept, turn * N + n)
                                nc.tensor.matmul(bank[(n + 1) % 2][:, :], g.pick_b[0:96, n + 1, :], bc[:, :],
                                                 start=True, stop=True).then_inc(b_spread, 1)
                            if 0 <= n < N:
                                if n >= 2:
                                    pe.wait_ge(term_ready, turn * ITEMS + 2 * n - 2)
                                nc.tensor.matmul(bank[2 + n % 2][:, :], g.pick_c[0:96, n, :], bc[:, :],
                                                 start=True, stop=True).then_inc(c_spread, 1)
                            if n >= 2:
                                for half in range(2):
                                    i = 2 * (n - 2) + half
                                    pe.wait_ge(term_ready, turn * ITEMS + i + 1)
                                    nc.tensor.matmul(bank[6 + half][:, :], g.ident if r == 0 else g.minus, term[:, i % 4, :],
                                                     start=False, stop=True, skip_group_check=True).then_inc(y_added, 1)
                    pe.wait_ge(term_ready, (b + 1) * BR * ITEMS)
                    project(chunk(g.normed, (b + 1) & (CHUNKS - 1)))
                    for half in range(2):
                        pe.wait_ge(gated, b * 2 + half + 2)
                        mm = nc.tensor.matmul(bank[4][:, :], w["out"][:, half * P:(half + 1) * P], y[:, half, :],
                                              start=(half == 0), stop=(half == 1))
                    mm.then_inc(out_ready, 1)

            @block.scalar
            def _(act):
                act.wait_ge(g.loaded[pack], 16)
                for r in range(BR):
                    nc.scalar.activation(decay[:, r, :], w[f"alog{r}"], ACT.Exp).then_inc(decay_ready, 1)
                act.wait_ge(negated, 1)
                with act.Fori(0, CHUNKS) as b:
                    for half in range(2):
                        act.wait_ge(in_ready, b * 4 + half + 1)
                        nc.scalar.copy(xp[:, half, TAPS - 1:TAPS - 1 + CHUNK], bank[half][:, :]).then_inc(x_kept, 1)
                    for half in range(2):
                        act.wait_ge(in_ready, b * 4 + half + 3)
                        act.wait_ge(gated, b * 2 + 1)
                        nc.scalar.activation(z[:, half, :], bank[2 + half][:, :], ACT.Silu).then_inc(z_ready, 1)
                    for half in range(2):
                        act.wait_ge(conv_done, b * 2 + half + 1)
                        nc.scalar.activation(u[:, half, :], conv[:, half, 1, :], ACT.Silu).then_inc(u_ready, 1)
                    for r, rank in enumerate(ranks):
                        turn = b * BR + r
                        act.wait_ge(dt_ready, turn + 1)
                        nc.scalar.copy(dt[0:rank, :], bank[4][0:rank, :]).then_inc(dt_kept, 1)
                        act.wait_ge(bc_ready, turn + 1)
                        nc.scalar.copy(bc[0:32, :], bank[5][0:32, :]).then_inc(hi_kept, 1)
                        for half in range(2):
                            act.wait_ge(delta_ready, turn * 2 + half + 1)
                            nc.scalar.activation(mag[:, half, :], bank[half][:, :], ACT.Abs,
                                                 bias=w[f"dtb{r}"][:, half:half + 1]).then_inc(abs_done, 1)
                        act.wait_ge(abs_done, turn * 2 + 2)
                        nc.scalar.activation(mag[:], mag[:], ACT.Exp, scale=-1.0).then_inc(exp_done, 1)
                        act.wait_ge(grown, turn + 1)
                        nc.scalar.activation(log, grow[:], ACT.Ln).then_inc(log_done, 1)
                        act.wait_ge(log_done, turn + 1)
                        nc.scalar.activation(inv, log, ACT.Exp, scale=-1.0).then_inc(inv_done, 1)
                        act.wait_ge(delta_done, turn + 1)
                        for n in range(N):
                            act.wait_ge(b_spread, turn * N + n + 1)
                            if n >= 3:
                                act.wait_ge(dbu_ready, turn * ITEMS + 2 * n - 4)
                            nc.scalar.copy(bb[:, n % 3, :], bank[n % 2][:, :]).then_inc(b_kept, 1)
                            for half in range(2):
                                i = 2 * n + half
                                if i >= 4:
                                    act.wait_ge(scan_done, turn * ITEMS + i - 3)
                                nc.scalar.activation(da[:, i % 4, :], delta[:, half, :], ACT.Exp,
                                                     scale=decay[:, r, half * N + n:half * N + n + 1]).then_inc(da_ready, 1)

            @block.gpsimd
            def _(pool):
                nc.gpsimd.memset(xp[:, :, 0:TAPS - 1], 0.0).then_inc(cleared, 1)
                nc.gpsimd.memset(zero[:, :], 0.0).then_inc(cleared, 1)
                with pool.Fori(0, CHUNKS) as b:
                    for r in range(BR):
                        turn = b * BR + r
                        pool.wait_ge(delta_done, turn + 1)
                        nc.gpsimd.tensor_tensor(du[:], delta[:], u[:], ALU.mult).then_inc(du_done, 1)
                        pool.wait_ge(du_done, turn + 1)
                        for i in range(ITEMS):
                            n, half = i // 2, i % 2
                            pool.wait_ge(b_kept, turn * N + n + 1)
                            if i >= 4:
                                pool.wait_ge(scan_done, turn * ITEMS + i - 3)
                            nc.gpsimd.tensor_tensor(dbu[:, i % 4, :], du[:, half, :], bb[:, n % 3, :], ALU.mult).then_inc(dbu_ready, 1)

            @block.vector
            def _(dve):
                dve.wait_ge(g.loaded[pack], 16)
                nc.vector.memset(g.mark, 0.0).then_inc(resid_done, 1)
                dve.wait_ge(resid_done, 1)
                nc.vector.memset(g.mark, 0.0).then_inc(gated, 1)
                dve.wait_ge(decay_ready, BR)
                nc.vector.tensor_scalar(decay[:], decay[:], -1.0, None, ALU.mult).then_inc(negated, 1)
                if BR == 1:
                    nc.vector.tensor_copy(skip[:, :], w["d0"]).then_inc(skip_ready, 1)
                else:
                    nc.vector.tensor_tensor(skip[:, :], w["d0"], w["d1"], ALU.subtract).then_inc(skip_ready, 1)
                dve.wait_ge(skip_ready, 1)
                dve.wait_ge(cleared, 1)
                with dve.Fori(0, CHUNKS) as b:
                    for k in range(TAPS):
                        for half in range(2):
                            tap = w["conv"][:, half * TAPS + k:half * TAPS + k + 1]
                            if k == 0:
                                dve.wait_ge(x_kept, b * 2 + half + 1)
                                nc.vector.tensor_scalar(conv[:, half, 0, :], xp[:, half, 0:CHUNK], tap, w["conv_b"][:, half:half + 1],
                                                        ALU.mult, ALU.add).then_inc(tap_done, 1)
                            else:
                                dve.wait_ge(tap_done, b * 2 * (TAPS - 1) + 2 * (k - 1) + half + 1)
                                nc.vector.scalar_tensor_tensor(
                                    out=conv[:, half, k % 2, :], in0=xp[:, half, k:k + CHUNK], scalar=tap,
                                    in1=conv[:, half, (k - 1) % 2, :], op0=ALU.mult, op1=ALU.add).then_inc(
                                    tap_done if k < TAPS - 1 else conv_done, 1)
                    for r in range(BR):
                        turn = b * BR + r
                        dve.wait_ge(hi_kept, turn + 1)
                        nc.vector.tensor_tensor(r1[:, :], bank[5][0:32, :], bc[0:32, :], ALU.subtract).then_inc(rest1, 1)
                        dve.wait_ge(rest1, turn + 1)
                        nc.vector.tensor_copy(mid[:, :], r1[:, :]).then_inc(mid_kept, 1)
                        dve.wait_ge(mid_kept, turn + 1)
                        nc.vector.tensor_copy(bc[32:64, :], mid[:, :]).then_inc(mid_moved, 1)
                        nc.vector.tensor_tensor(r1[:, :], r1[:, :], mid[:, :], ALU.subtract).then_inc(rest2, 1)
                        dve.wait_ge(rest2, turn + 1)
                        nc.vector.tensor_copy(bc[64:96, :], r1[:, :]).then_inc(lo_kept, 1)
                        for half in range(2):
                            dve.wait_ge(abs_done, turn * 2 + half + 1)
                            nc.vector.tensor_scalar(pos[:, half, :], bank[half][:, :], w[f"dtb{r}"][:, half:half + 1], 0.0,
                                                    ALU.add, ALU.max).then_inc(pos_done, 1)
                        dve.wait_ge(exp_done, turn + 1)
                        nc.vector.tensor_scalar(grow[:], mag[:], 1.0, None, ALU.add).then_inc(grown, 1)
                        dve.wait_ge(grown, turn + 1)
                        nc.vector.scalar_tensor_tensor(out=mag[:], in0=grow[:], scalar=-1.0, in1=mag[:], op0=ALU.add,
                                                       op1=ALU.subtract).then_inc(lost, 1)
                        dve.wait_ge(log_done, turn + 1)
                        dve.wait_ge(pos_done, turn * 2 + 2)
                        nc.vector.tensor_tensor(delta[:], pos[:], log, ALU.add).then_inc(delta_sum, 1)
                        dve.wait_ge(inv_done, turn + 1)
                        dve.wait_ge(lost, turn + 1)
                        nc.vector.tensor_tensor(mag[:], mag[:], inv, ALU.mult).then_inc(lost_part, 1)
                        dve.wait_ge(lost_part, turn + 1)
                        dve.wait_ge(delta_sum, turn + 1)
                        nc.vector.tensor_tensor(delta[:], delta[:], mag[:], ALU.subtract).then_inc(delta_done, 1)
                        for i in range(ITEMS + 1):
                            if i < ITEMS:
                                dve.wait_ge(da_ready, turn * ITEMS + i + 1)
                                dve.wait_ge(dbu_ready, turn * ITEMS + i + 1)
                                if i >= 4:
                                    dve.wait_ge(term_ready, turn * ITEMS + i - 3)
                                nc.vector.tensor_tensor_scan(hh[:, i % 4, :], da[:, i % 4, :], dbu[:, i % 4, :], 0.0,
                                                             ALU.mult, ALU.add).then_inc(scan_done, 1)
                            if i >= 1:
                                k = i - 1
                                dve.wait_ge(scan_done, turn * ITEMS + k + 1)
                                dve.wait_ge(c_spread, turn * N + k // 2 + 1)
                                if k >= 4:
                                    dve.wait_ge(y_added, turn * ITEMS + k - 3)
                                nc.vector.tensor_tensor(term[:, k % 4, :], hh[:, k % 4, :], bank[2 + k // 2 % 2][:, :],
                                                        ALU.mult).then_inc(term_ready, 1)
                    dve.wait_ge(y_added, b * BR * ITEMS + BR * ITEMS)
                    for half in range(2):
                        nc.vector.scalar_tensor_tensor(out=y[:, half, :], in0=u[:, half, :], scalar=skip[:, half:half + 1],
                                                       in1=bank[6 + half][:, :], op0=ALU.mult, op1=ALU.add).then_inc(skipped, 1)
                    for half in range(2):
                        dve.wait_ge(skipped, b * 2 + half + 1)
                        dve.wait_ge(z_ready, b * 2 + half + 1)
                        nc.vector.tensor_tensor(y[:, half, :], y[:, half, :], z[:, half, :], ALU.mult).then_inc(gated, 1)
                    dve.wait_ge(out_ready, b + 1)
                    nc.vector.tensor_tensor(chunk(g.resid, b), chunk(g.resid, b), bank[4][:, :], ALU.add).then_inc(resid_done, 1)


def selective_scan_one(g):
    selective_scan(g, "l2a", [64])


def selective_scan_two(g):
    selective_scan(g, "l2b", [8, 8])


def unit_attention(g):
    nc, bank, w = g.nc, g.bank, g.w["l3a"]
    HEADS, HD = 4, 64
    with stage(g, "x_kept proj_ready v_ready lowered exp_ready raised squared ss_ready rooted logged inv_ready unit_ready "
                  "ones_set v_kept score_ready masked pv_ready den_logged den_inv y_ready out_ready resid_done") as (sb, sems):
        (x_kept, proj_ready, v_ready, lowered, exp_ready, raised, squared, ss_ready, rooted, logged, inv_ready, unit_ready,
         ones_set, v_kept, score_ready, masked, pv_ready, den_logged, den_inv, y_ready, out_ready, resid_done) = sems
        xb = sb("u_xb", [P, CHUNK])
        e = sb("u_e", [P, 4, CHUNK])
        qk = sb("u_qk", [P, 4, CHUNK])
        vw = sb("u_vw", [P, QT, HEADS, 2 * HD])
        st = sb("u_st", [P, 4, CHUNK])
        rd = sb("u_rd", [HD, 2, CHUNK])
        y = sb("u_y", [P, 2, CHUNK])
        items = [(h, kt) for h in range(HEADS) for kt in range(QT)]
        LOOK = 3
        with nc.Block() as block:
            @block.tensor
            def _(pe):
                pe.wait_ge(g.loaded["l3a"], 16)
                pe.wait_ge(ones_set, 1)
                with pe.Fori(0, CHUNKS) as b:
                    pe.wait_ge(resid_done, b + 1)
                    for m in range(4):
                        nc.tensor.matmul(bank[m][:, :], w["wqk"][:, m * P:(m + 1) * P], chunk(g.normed, b),
                                         start=True, stop=True).then_inc(proj_ready, 1)
                    pe.wait_ge(x_kept, b + 1)
                    for t in range(QT):
                        mm = nc.tensor.matmul(bank[4 + t // 2][:, t % 2 * 256:t % 2 * 256 + 256], xb[:, t * P:(t + 1) * P], w["wv"],
                                              start=True, stop=True)
                    mm.then_inc(v_ready, 1)
                    for m in range(4):
                        pe.wait_ge(squared, b * 4 + m + 1)
                        mm = nc.tensor.matmul(bank[m][:, :], g.same64, e[:, m, :], start=True, stop=True)
                    mm.then_inc(ss_ready, 1)
                    pe.wait_ge(unit_ready, b + 1)
                    pe.wait_ge(v_kept, b + 1)
                    for n in range(len(items) + LOOK):
                        if n < len(items):
                            h, kt = items[n]
                            rows = slice(HD * (h % 2), HD * (h % 2) + HD)
                            if n >= 4:
                                pe.wait_ge(masked, b * 16 + n - 3)
                            nc.tensor.matmul(bank[n % 4][:, kt * P:CHUNK], qk[rows, 2 + h // 2, kt * P:(kt + 1) * P],
                                             qk[rows, h // 2, kt * P:CHUNK], start=True, stop=True).then_inc(score_ready, 1)
                        if n >= LOOK:
                            i = n - LOOK
                            h, kt = items[i]
                            pe.wait_ge(masked, b * 16 + i + 1)
                            if kt == 0 and h >= 2:
                                pe.wait_ge(y_ready, b * HEADS + h - 1)
                            nc.tensor.matmul(bank[6 + h % 2][:, kt * P:CHUNK], vw[:, kt, h, :], st[:, i % 4, kt * P:CHUNK],
                                             start=(kt == 0), stop=(kt == QT - 1)).then_inc(pv_ready, 1)
                    pe.wait_ge(y_ready, b * HEADS + HEADS)
                    for half in range(2):
                        mm = nc.tensor.matmul(bank[5][:, :], w["wo"][:, half * P:(half + 1) * P], y[:, half, :],
                                              start=(half == 0), stop=(half == 1))
                    mm.then_inc(out_ready, 1)

            @block.scalar
            def _(act):
                with act.Fori(0, CHUNKS) as b:
                    nc.scalar.copy(xb[:, :], chunk(g.normed, b)).then_inc(x_kept, 1)
                    for m in range(4):
                        act.wait_ge(lowered, b * 4 + m + 1)
                        nc.scalar.activation(e[:, m, :], e[:, m, :], ACT.Exp).then_inc(exp_ready, 1)
                    for m in range(4):
                        act.wait_ge(raised, b * 4 + m + 1)
                        nc.scalar.activation(e[:, m, :], qk[:, m, :], ACT.Square).then_inc(squared, 1)
                    act.wait_ge(ss_ready, b + 1)
                    nc.scalar.activation(e[:], g.banks[0:4, 0:CHUNK], ACT.Sqrt).then_inc(rooted, 1)
                    act.wait_ge(rooted, b + 1)
                    nc.scalar.activation(e[:], e[:], ACT.Ln, bias=g.eps6).then_inc(logged, 1)
                    act.wait_ge(logged, b + 1)
                    nc.scalar.activation(e[:], e[:], ACT.Exp, scale=-1.0).then_inc(inv_ready, 1)
                    for h in range(HEADS):
                        act.wait_ge(pv_ready, b * 16 + QT * (h + 1))
                        if h >= 2:
                            act.wait_ge(y_ready, b * HEADS + h - 1)
                        nc.scalar.activation(rd[:, h % 2, :], bank[6 + h % 2][HD:P, :], ACT.Ln, bias=g.eps6[0:HD]).then_inc(den_logged, 1)
                        act.wait_ge(den_logged, b * HEADS + h + 1)
                        nc.scalar.activation(rd[:, h % 2, :], rd[:, h % 2, :], ACT.Exp, scale=-1.0).then_inc(den_inv, 1)

            @block.gpsimd
            def _(pool):
                nc.gpsimd.memset(vw[:, :, :, HD:2 * HD], 1.0).then_inc(ones_set, 1)

            @block.vector
            def _(dve):
                nc.vector.memset(g.mark, 0.0).then_inc(resid_done, 1)

                def weigh(b, h):
                    dve.wait_ge(den_inv, b * HEADS + h + 1)
                    nc.vector.tensor_tensor(y[HD * (h % 2):HD * (h % 2) + HD, h // 2, :], bank[6 + h % 2][0:HD, :], rd[:, h % 2, :],
                                            ALU.mult).then_inc(y_ready, 1)

                with dve.Fori(0, CHUNKS) as b:
                    for m in range(4):
                        dve.wait_ge(proj_ready, b * 4 + m + 1)
                        nc.vector.tensor_scalar(e[:, m, :], bank[m][:, :], 0.0, None, ALU.min).then_inc(lowered, 1)
                    dve.wait_ge(v_ready, b + 1)
                    for t in range(QT):
                        cp = nc.vector.tensor_copy(vw[:, t, :, 0:HD], bank[4 + t // 2][:, t % 2 * 256:t % 2 * 256 + 256].rearrange(
                            "p (h d) -> p h d", d=HD))
                    cp.then_inc(v_kept, 1)
                    for m in range(4):
                        dve.wait_ge(exp_ready, b * 4 + m + 1)
                        nc.vector.scalar_tensor_tensor(out=qk[:, m, :], in0=bank[m][:, :], scalar=0.0, in1=e[:, m, :],
                                                       op0=ALU.max, op1=ALU.add).then_inc(raised, 1)
                    dve.wait_ge(inv_ready, b + 1)
                    dve.wait_ge(raised, b * 4 + 4)
                    nc.vector.tensor_tensor(qk[:], qk[:], e[:], ALU.mult).then_inc(unit_ready, 1)
                    for n, (h, kt) in enumerate(items):
                        dve.wait_ge(score_ready, b * 16 + n + 1)
                        if n >= 4:
                            dve.wait_ge(pv_ready, b * 16 + n - 3)
                        nc.vector.tensor_tensor(st[:, n % 4, kt * P:CHUNK], bank[n % 4][:, kt * P:CHUNK],
                                                g.causal[:, 0:CHUNK - kt * P], ALU.mult).then_inc(masked, 1)
                        if kt == 2 and h >= 1:
                            weigh(b, h - 1)
                    weigh(b, HEADS - 1)
                    dve.wait_ge(out_ready, b + 1)
                    nc.vector.tensor_tensor(chunk(g.resid, b), chunk(g.resid, b), bank[5][:, :], ALU.add).then_inc(resid_done, 1)


def decayed_sum(g):
    nc, bank, w = g.nc, g.bank, g.w["l3b"]
    with stage(g, "rate_ready decay_ready bonus_ready filled spread first_set proj_ready k_kept gate_ready kv_ready scanned "
                  "summed y_ready out_ready resid_done") as (sb, sems):
        (rate_ready, decay_ready, bonus_ready, filled, spread, first_set, proj_ready, k_kept, gate_ready, kv_ready, scanned,
         summed, y_ready, out_ready, resid_done) = sems
        decay = sb("w_decay", [P, 1])
        bonus = sb("w_bonus", [P, 1])
        keep = sb("w_keep", [P, CHUNK])
        k = sb("w_k", [P, CHUNK])
        kv = sb("w_kv", [P, CHUNK])
        gate = sb("w_gate", [P, CHUNK])
        s = sb("w_s", [P, 1 + CHUNK])
        y = sb("w_y", [P, CHUNK])
        with nc.Block() as block:
            @block.tensor
            def _(pe):
                pe.wait_ge(g.loaded["l3b"], 16)
                with pe.Fori(0, CHUNKS) as b:
                    pe.wait_ge(resid_done, b + 1)
                    for m in range(3):
                        nc.tensor.matmul(bank[m][:, :], w["wkvr"][:, m * P:(m + 1) * P], chunk(g.normed, b),
                                         start=True, stop=True).then_inc(proj_ready, 1)
                    pe.wait_ge(y_ready, b + 1)
                    nc.tensor.matmul(bank[3][:, :], w["wo"], y[:, :], start=True, stop=True).then_inc(out_ready, 1)

            @block.scalar
            def _(act):
                act.wait_ge(g.loaded["l3b"], 16)
                nc.scalar.activation(decay[:, :], w["decay"], ACT.Exp).then_inc(rate_ready, 1)
                act.wait_ge(rate_ready, 1)
                nc.scalar.activation(decay[:, :], decay[:, :], ACT.Exp, scale=-1.0).then_inc(decay_ready, 1)
                nc.scalar.activation(bonus[:, :], w["first"], ACT.Exp).then_inc(bonus_ready, 1)
                with act.Fori(0, CHUNKS) as b:
                    act.wait_ge(proj_ready, b * 3 + 1)
                    nc.scalar.copy(k[:, :], bank[0][:, :]).then_inc(k_kept, 1)
                    act.wait_ge(proj_ready, b * 3 + 3)
                    nc.scalar.activation(gate[:, :], bank[2][:, :], ACT.Sigmoid).then_inc(gate_ready, 1)

            @block.vector
            def _(dve):
                nc.vector.memset(keep[:, :], 1.0).then_inc(filled, 1)
                nc.vector.memset(s[:, 0:1], 0.0).then_inc(first_set, 1)
                nc.vector.memset(g.mark, 0.0).then_inc(resid_done, 1)
                dve.wait_ge(filled, 1)
                dve.wait_ge(decay_ready, 1)
                nc.vector.tensor_scalar(keep[:, :], keep[:, :], decay[:, :], None, ALU.mult).then_inc(spread, 1)
                dve.wait_ge(spread, 1)
                dve.wait_ge(first_set, 1)
                dve.wait_ge(bonus_ready, 1)
                with dve.Fori(0, CHUNKS) as b:
                    dve.wait_ge(k_kept, b + 1)
                    dve.wait_ge(proj_ready, b * 3 + 2)
                    nc.vector.tensor_tensor(kv[:, :], k[:, :], bank[1][:, :], ALU.mult).then_inc(kv_ready, 1)
                    dve.wait_ge(kv_ready, b + 1)
                    nc.vector.tensor_tensor_scan(s[:, 1:1 + CHUNK], keep[:, :], kv[:, :], 0.0, ALU.mult, ALU.add).then_inc(scanned, 1)
                    dve.wait_ge(scanned, b + 1)
                    nc.vector.scalar_tensor_tensor(out=y[:, :], in0=kv[:, :], scalar=bonus[:, :], in1=s[:, 0:CHUNK],
                                                   op0=ALU.mult, op1=ALU.add).then_inc(summed, 1)
                    dve.wait_ge(summed, b + 1)
                    dve.wait_ge(gate_ready, b + 1)
                    nc.vector.tensor_tensor(y[:, :], y[:, :], gate[:, :], ALU.mult).then_inc(y_ready, 1)
                    dve.wait_ge(out_ready, b + 1)
                    nc.vector.tensor_tensor(chunk(g.resid, b), chunk(g.resid, b), bank[3][:, :], ALU.add).then_inc(resid_done, 1)


def soft_experts(g):
    nc, bank, w = g.nc, g.bank, g.w["l3f"]
    SLOTS, EXPERTS, SLOT = 2048, 64, 32
    PARTS, STILES = SLOTS // CHUNK, SLOTS // P
    PE_ = CHUNK // SLOT
    LOW, HIGH = -33000.0, 65000.0
    g.count += 1
    with ExitStack() as ctx:
        yt = ctx.enter_context(nc.sbuf_tensor(f"x_yt_{g.count}", [P, STILES, P], F32))

        with stage(g, "cleared hi_kept rest mid_kept rest2 bias_set x_kept turned xt_kept logit_ready max_ready lowered exp_ready "
                      "sum_ready inv_ready share_ready added") as (sb, sems):
            (cleared, hi_kept, rest, mid_kept, rest2, bias_set, x_kept, turned, xt_kept, logit_ready, max_ready, lowered, exp_ready,
             sum_ready, inv_ready, share_ready, added) = sems
            zero = sb("x_zero", [P, CHUNK], BF16)
            xb = sb("x_xb", [P, 2, CHUNK])
            xt = sb("x_xt", [P, 2, QT, P])
            bias = sb("x_bias", [96, SLOTS], BF16)
            left = sb("x_left", [96, SLOTS])
            share = sb("x_share", [P, 4, SLOTS])
            mx = sb("x_mx", [P, 4, EXPERTS])
            total = sb("x_total", [P, 4, EXPERTS])
            TURN = 2 * QT
            TURNS = TOKENS // P // TURN

            def part(t, c):
                return share[:, t % 4, c * CHUNK:(c + 1) * CHUNK]

            def by_expert(x):
                return x.rearrange("p (n s) -> p n s", s=SLOT)

            with nc.Block() as block:
                @block.tensor
                def _(pe):
                    pe.wait_ge(g.loaded["l3f"], 16)
                    pe.wait_ge(cleared, 3)

                    def add_tile(t, n):
                        pe.wait_ge(share_ready, n + 3)
                        for c in range(PARTS):
                            mm = nc.tensor.matmul(bank[4 + c][:, :], xt[:, t // QT % 2, t % QT, :], part(t, c), start=False, stop=True,
                                                  skip_group_check=True)
                        mm.then_inc(added, 1)

                    for c in range(PARTS):
                        nc.tensor.matmul(bank[4 + c][:, :], g.ident_bf, zero[:, :], start=True, stop=True)
                    pe.wait_ge(bias_set, PARTS)
                    with pe.Fori(0, TURNS) as i:
                        for t in range(TURN):
                            n = i * TURN + t
                            half = t // QT
                            if t % QT == 0:
                                pe.wait_ge(x_kept, i * 2 + half + 1)
                            if t % QT == 1:
                                pe.wait_ge(xt_kept, i * 2 + half + 1)
                            for c in range(PARTS):
                                pe.wait_ge(lowered, n * PARTS + c + 1)
                                nc.tensor.matmul(bank[c][:, :], g.ones3[0:96, :], bias[:, c * CHUNK:(c + 1) * CHUNK],
                                                 start=True, stop=False)
                                nc.tensor.matmul(bank[c][:, :], xb[:, half, t % QT * P:(t % QT + 1) * P],
                                                 w["phi"][:, c * CHUNK:(c + 1) * CHUNK], start=False, stop=True).then_inc(logit_ready, 1)
                            add_tile((t - 2) % TURN, n - 2)
                            if t % QT == 0:
                                pe.wait_ge(lowered, n * PARTS + PARTS + 1)
                                for q in range(QT):
                                    mm = nc.tensor.transpose(bank[0][:, q * P:(q + 1) * P], xb[:, half, q * P:(q + 1) * P], g.ident)
                                mm.then_inc(turned, 1)
                    for t in (TURN - 2, TURN - 1):
                        add_tile(t, TOKENS // P - TURN + t)

                @block.scalar
                def _(act):
                    nc.scalar.copy(xb[:, 0, :], fixed(g.normed, 0)).then_inc(x_kept, 1)
                    act.wait_ge(cleared, 3)
                    with act.Fori(0, TURNS) as i:
                        for t in range(TURN):
                            half = t // QT
                            for c in range(PARTS):
                                act.wait_ge(lowered, (i * TURN + t) * PARTS + PARTS + c + 1)
                                nc.scalar.activation(part(t, c), part(t, c), ACT.Exp).then_inc(exp_ready, 1)
                                if t % QT == 0 and c == 0:
                                    act.wait_ge(turned, i * 2 + half + 1)
                                    nc.scalar.copy(xt[:, half, :, :].rearrange("p t c -> p (t c)"), bank[0][:, :]).then_inc(xt_kept, 1)
                            if t % QT == 1:
                                nc.scalar.copy(xb[:, 1 - half, :], chunk(g.normed, (i * 2 + half + 1) & (CHUNKS - 1))).then_inc(x_kept, 1)

                @block.gpsimd
                def _(pool):
                    nc.gpsimd.memset(zero[:, :], 0.0).then_inc(cleared, 1)
                    nc.gpsimd.memset(xt[:, 1, QT - 2:QT, :], 0.0).then_inc(cleared, 1)
                    nc.gpsimd.memset(share[:, 2:4, :], 1.0).then_inc(cleared, 1)

                    def divide(t, n):
                        pool.wait_ge(inv_ready, n + 2)
                        pool.wait_ge(exp_ready, n * PARTS + 2 * PARTS)
                        e = by_expert(share[:, t % 4, :])
                        nc.gpsimd.tensor_tensor(e, e, total[:, t % 4, :].unsqueeze(2).broadcast_to([P, EXPERTS, SLOT]),
                                                ALU.mult).then_inc(share_ready, 1)

                    pool.wait_ge(cleared, 3)
                    with pool.Fori(0, TURNS) as i:
                        for t in range(TURN):
                            divide((t - 1) % TURN, i * TURN + t - 1)
                    divide(TURN - 1, TOKENS // P - 1)

                @block.vector
                def _(dve):
                    dve.wait_ge(g.loaded["l3f"], 16)
                    nc.vector.memset(g.mark, 0.0).then_inc(lowered, PARTS)
                    dve.wait_ge(lowered, PARTS)
                    nc.vector.memset(g.mark, 0.0).then_inc(exp_ready, PARTS)
                    dve.wait_ge(exp_ready, PARTS)
                    nc.vector.memset(g.mark, 0.0).then_inc(added, 2)
                    dve.wait_ge(added, 2)
                    nc.vector.memset(g.mark, 0.0).then_inc(share_ready, 1)
                    for c in range(PARTS):
                        at = slice(c * CHUNK, (c + 1) * CHUNK)
                        nc.vector.tensor_copy(bias[:, at], w["phi_b"][:, at]).then_inc(hi_kept, 1)
                        dve.wait_ge(hi_kept, c + 1)
                        nc.vector.tensor_tensor(left[:, at], w["phi_b"][:, at], bias[:, at], ALU.subtract).then_inc(rest, 1)
                        dve.wait_ge(rest, c + 1)
                        for r in (32, 64):
                            nc.vector.tensor_copy(bias[r:r + 32, at], left[r:r + 32, at]).then_inc(mid_kept, 1)
                        dve.wait_ge(mid_kept, 2 * c + 2)
                        nc.vector.tensor_tensor(left[64:96, at], left[64:96, at], bias[64:96, at], ALU.subtract).then_inc(rest2, 1)
                        dve.wait_ge(rest2, c + 1)
                        nc.vector.tensor_copy(bias[64:96, at], left[64:96, at]).then_inc(bias_set, 1)

                    def total_of(t, n):
                        dve.wait_ge(exp_ready, n * PARTS + 2 * PARTS)
                        nc.vector.tensor_reduce(total[:, t % 4, :], by_expert(share[:, t % 4, :]), AX.X, ALU.add).then_inc(sum_ready, 1)
                        dve.wait_ge(sum_ready, n + 2)
                        nc.vector.reciprocal(total[:, t % 4, :], total[:, t % 4, :]).then_inc(inv_ready, 1)

                    dve.wait_ge(cleared, 3)
                    with dve.Fori(0, TURNS) as i:
                        for t in range(TURN):
                            n = i * TURN + t
                            for c in range(PARTS):
                                m = mx[:, t % 4, c * PE_:(c + 1) * PE_]
                                dve.wait_ge(logit_ready, n * PARTS + c + 1)
                                nc.vector.tensor_reduce(m, by_expert(bank[c][:, :]), AX.X, ALU.max).then_inc(max_ready, 1)
                                if c == 0:
                                    dve.wait_ge(added, n + 1)
                                dve.wait_ge(max_ready, n * PARTS + c + 1)
                                nc.vector.tensor_tensor(by_expert(part(t, c)), by_expert(bank[c][:, :]),
                                                        m.unsqueeze(2).broadcast_to([P, PE_, SLOT]), ALU.subtract).then_inc(lowered, 1)
                            total_of((t - 1) % TURN, n - 1)
                    total_of(TURN - 1, TOKENS // P - 1)

        with stage(g, "bounded mean_ready centred squared var_ready logged rstd_ready scaled tanh_ready y_ready y_kept") as (sb, sems):
            bounded, mean_ready, centred, squared, var_ready, logged, rstd_ready, scaled, tanh_ready, y_ready, y_kept = sems
            z = sb("x_z", [P, SLOTS])
            sq = sb("x_sq", [P, SLOTS])
            rstd = sb("x_rstd", [P, SLOTS])
            with nc.Block() as block:
                @block.tensor
                def _(pe):
                    for j in range(PARTS):
                        pe.wait_ge(bounded, j + 1)
                        nc.tensor.matmul(bank[j][:, :], g.mean_of, fixed(z, j), start=True, stop=True).then_inc(mean_ready, 1)
                    for j in range(PARTS):
                        pe.wait_ge(squared, j + 1)
                        nc.tensor.matmul(bank[4 + j][:, :], g.mean_of, fixed(sq, j), start=True, stop=True).then_inc(var_ready, 1)
                    for j in range(PARTS):
                        pe.wait_ge(tanh_ready, j + 1)
                        for i in range(4 * j, 4 * j + 4):
                            at = slice(i % 4 * P, (i % 4 + 1) * P)
                            nc.tensor.matmul(bank[j][:, at], w["of_expert"][:, i * P:(i + 1) * P], w["expert_b"], start=True, stop=True)
                            for q in range(4):
                                n = 4 * i + q
                                mm = nc.tensor.matmul(bank[j][SLOT * q:SLOT * (q + 1), at], z[:, n * SLOT:(n + 1) * SLOT],
                                                      w["expert_w"][:, n * P:(n + 1) * P], start=False, stop=True,
                                                      skip_group_check=True)
                        mm.then_inc(y_ready, 1)

                @block.scalar
                def _(act):
                    for j in range(PARTS):
                        act.wait_ge(centred, j + 1)
                        nc.scalar.activation(fixed(sq, j), fixed(z, j), ACT.Square).then_inc(squared, 1)
                    for j in range(PARTS):
                        act.wait_ge(var_ready, j + 1)
                        nc.scalar.activation(fixed(rstd, j), bank[4 + j][:, :], ACT.Ln, bias=g.eps5).then_inc(logged, 1)
                    for j in range(PARTS):
                        act.wait_ge(logged, j + 1)
                        nc.scalar.activation(fixed(rstd, j), fixed(rstd, j), ACT.Exp, scale=-0.5).then_inc(rstd_ready, 1)
                    for j in range(PARTS):
                        act.wait_ge(scaled, j + 1)
                        nc.scalar.activation(fixed(z, j), fixed(z, j), ACT.Tanh).then_inc(tanh_ready, 1)
                    for j in range(PARTS):
                        act.wait_ge(y_ready, j + 1)
                        nc.scalar.copy(yt[:, 4 * j:4 * j + 4, :].rearrange("p i h -> p (i h)"), bank[j][:, :]).then_inc(y_kept, 1)

                @block.vector
                def _(dve):
                    for j in range(PARTS):
                        nc.vector.tensor_scalar(fixed(z, j), bank[4 + j][:, :], LOW, HIGH, ALU.max, ALU.min).then_inc(bounded, 1)
                    for j in range(PARTS):
                        dve.wait_ge(mean_ready, j + 1)
                        nc.vector.tensor_tensor(fixed(z, j), fixed(z, j), bank[j][:, :], ALU.subtract).then_inc(centred, 1)
                    for j in range(PARTS):
                        dve.wait_ge(rstd_ready, j + 1)
                        dve.wait_ge(centred, j + 1)
                        nc.vector.tensor_tensor(fixed(z, j), fixed(z, j), fixed(rstd, j), ALU.mult).then_inc(scaled, 1)

        with stage(g, "logit_ready kept max_step quarter_kept quarter_max max_spread low_dve low_pool exp_ready partial sum_ready "
                      "inv_ready share_dve share_pool weighed resid_done") as (sb, sems):
            (logit_ready, kept, max_step, quarter_kept, quarter_max, max_spread, low_dve, low_pool, exp_ready, partial, sum_ready,
             inv_ready, share_dve, share_pool, weighed, resid_done) = sems
            lt = sb("x_lt", [P, 2, STILES, CHUNK])
            top = sb("x_top", [P, CHUNK])
            side = sb("x_side", [SLOT, 3, CHUNK])
            inv = sb("x_inv", [P, CHUNK])
            acc = sb("x_acc", [P, CHUNK])
            on_pool = [i for i in range(STILES) if i % 4 == 3]
            on_dve = [i for i in range(STILES) if i % 4 != 3]
            ADDED = 12
            AHEAD = STILES // 2

            def tile(b, i):
                if isinstance(b, int):
                    return lt[:, b % 2, i, :]
                return lt[:, bass.ds(b & 1, 1), i, :].rearrange("p o t -> p (o t)")

            def wait_for(eng, i, b, by_dve, by_pool):
                if i in on_pool:
                    eng.wait_ge(by_pool, b * len(on_pool) + on_pool.index(i) + 1)
                else:
                    eng.wait_ge(by_dve, b * len(on_dve) + on_dve.index(i) + 1)

            with nc.Block() as block:
                @block.tensor
                def _(pe):
                    def logits(b, i):
                        if not (isinstance(b, int) and b == 0 and i < 4):
                            pe.wait_ge(kept, b * STILES + i - 3)
                        nc.tensor.matmul(bank[i % 4][:, :], w["phi"][:, i * P:(i + 1) * P], chunk(g.normed, b),
                                         start=True, stop=True).then_inc(logit_ready, 1)

                    def weigh(b, i):
                        wait_for(pe, i, b, share_dve, share_pool)
                        if i == 0 and not (isinstance(b, int) and b == 0):
                            pe.wait_ge(resid_done, b)
                        nc.tensor.matmul(bank[5][:, :], yt[:, i, :], tile(b, i), start=(i == 0),
                                         stop=(i == STILES - 1)).then_inc(weighed, 1)

                    def sums(b):
                        for i in range(ADDED, STILES):
                            pe.wait_ge(exp_ready, b * STILES + i + 1)
                            if i == ADDED and not (isinstance(b, int) and b == 0):
                                pe.wait_ge(inv_ready, b)
                            nc.tensor.matmul(bank[4][:, :], g.mod32, tile(b, i), start=(i == ADDED), stop=False)
                        pe.wait_ge(partial, b * (ADDED - 1) + ADDED - 1)
                        nc.tensor.matmul(bank[4][:, :], g.mod32, acc[:, :], start=False, stop=True).then_inc(sum_ready, 1)

                    for b in range(2):
                        for i in range(STILES):
                            logits(b, i)
                    sums(0)
                    with pe.Fori(1, CHUNKS - 1) as b:
                        for i in range(STILES):
                            weigh(b - 1, i)
                            logits(b + 1, i)
                        sums(b)
                    for i in range(STILES):
                        weigh(CHUNKS - 2, i)
                    sums(CHUNKS - 1)
                    for i in range(STILES):
                        weigh(CHUNKS - 1, i)

                @block.scalar
                def _(act):
                    def keep(b, i):
                        act.wait_ge(logit_ready, b * STILES + i + 1)
                        if not (isinstance(b, int) and b < 2):
                            act.wait_ge(weighed, (b - 2) * STILES + i + 1)
                        nc.scalar.activation(tile(b, i), bank[i % 4][:, :], ACT.Identity, bias=w["phi_bc"][:, i:i + 1]).then_inc(kept, 1)

                    def raise_e(b, i):
                        wait_for(act, i, b, low_dve, low_pool)
                        nc.scalar.activation(tile(b, i), tile(b, i), ACT.Exp).then_inc(exp_ready, 1)

                    def mixed(b):
                        for i in range(AHEAD):
                            keep(b + 1, i)
                        for i in range(AHEAD):
                            raise_e(b, i)
                            keep(b + 1, AHEAD + i)
                        for i in range(AHEAD, STILES):
                            raise_e(b, i)

                    for i in range(STILES):
                        keep(0, i)
                    mixed(0)
                    with act.Fori(1, CHUNKS - 1) as b:
                        mixed(b)
                    for i in range(STILES):
                        raise_e(CHUNKS - 1, i)

                @block.gpsimd
                def _(pool):
                    def lower_and_add(b):
                        pool.wait_ge(max_spread, b * 4 + 4)
                        for i in on_pool:
                            nc.gpsimd.tensor_tensor(tile(b, i), tile(b, i), top[:, :], ALU.subtract).then_inc(low_pool, 1)
                        for i in range(1, ADDED):
                            pool.wait_ge(exp_ready, b * STILES + i + 1)
                            if i > 1:
                                pool.wait_ge(partial, b * (ADDED - 1) + i - 1)
                            elif not (isinstance(b, int) and b == 0):
                                pool.wait_ge(sum_ready, b)
                            nc.gpsimd.tensor_tensor(acc[:, :], tile(b, 0) if i == 1 else acc[:, :], tile(b, i), ALU.add).then_inc(partial, 1)

                    def divide(b):
                        pool.wait_ge(inv_ready, b + 1)
                        for i in on_pool:
                            nc.gpsimd.tensor_tensor(tile(b, i), tile(b, i), inv[:, :], ALU.mult).then_inc(share_pool, 1)

                    lower_and_add(0)
                    for b in range(1, CHUNKS):
                        divide(b - 1)
                        lower_and_add(b)
                    divide(CHUNKS - 1)

                @block.vector
                def _(dve):
                    steps = STILES - 1

                    def maximum(b):
                        if not (isinstance(b, int) and b == 0):
                            dve.wait_ge(low_pool, b * len(on_pool))
                            dve.wait_ge(low_dve, b * len(on_dve))
                        for i in range(1, STILES):
                            dve.wait_ge(kept, b * STILES + i + 1)
                            if i >= 2:
                                dve.wait_ge(max_step, b * steps + i - 1)
                            nc.vector.tensor_tensor(top[:, :], tile(b, 0) if i == 1 else top[:, :], tile(b, i), ALU.max).then_inc(max_step, 1)
                        dve.wait_ge(max_step, b * steps + steps)
                        for q in range(3):
                            nc.vector.tensor_copy(side[:, q, :], top[SLOT * (q + 1):SLOT * (q + 2), :]).then_inc(quarter_kept, 1)
                        for q in range(3):
                            dve.wait_ge(quarter_kept, b * 3 + q + 1)
                            if q >= 1:
                                dve.wait_ge(quarter_max, b * 3 + q)
                            nc.vector.tensor_tensor(side[:, 0, :], top[0:SLOT, :] if q == 0 else side[:, 0, :], side[:, q, :],
                                                    ALU.max).then_inc(quarter_max, 1)
                        dve.wait_ge(quarter_max, b * 3 + 3)
                        for q in range(4):
                            nc.vector.tensor_copy(top[SLOT * q:SLOT * (q + 1), :], side[:, 0, :]).then_inc(max_spread, 1)

                    def lower(b):
                        dve.wait_ge(max_spread, b * 4 + 4)
                        for i in on_dve:
                            nc.vector.tensor_tensor(tile(b, i), tile(b, i), top[:, :], ALU.subtract).then_inc(low_dve, 1)

                    def divide(b):
                        dve.wait_ge(sum_ready, b + 1)
                        if not (isinstance(b, int) and b == 0):
                            dve.wait_ge(share_pool, b * len(on_pool))
                            dve.wait_ge(share_dve, b * len(on_dve))
                        nc.vector.reciprocal(inv[:, :], bank[4][:, :]).then_inc(inv_ready, 1)
                        dve.wait_ge(inv_ready, b + 1)
                        for i in on_dve:
                            nc.vector.tensor_tensor(tile(b, i), tile(b, i), inv[:, :], ALU.mult).then_inc(share_dve, 1)

                    def add(b):
                        dve.wait_ge(weighed, b * STILES + STILES)
                        nc.vector.tensor_tensor(chunk(g.resid, b), chunk(g.resid, b), bank[5][:, :], ALU.add).then_inc(resid_done, 1)

                    maximum(0)
                    lower(0)
                    maximum(1)
                    with dve.Fori(1, CHUNKS - 1) as b:
                        divide(b - 1)
                        lower(b)
                        maximum(b + 1)
                        add(b - 1)
                    divide(CHUNKS - 2)
                    lower(CHUNKS - 1)
                    add(CHUNKS - 2)
                    divide(CHUNKS - 1)
                    add(CHUNKS - 1)



def columns(v):
    return v.reshape(-1, P).T


def beside(m):
    return m.reshape(-1, P, m.shape[1]).transpose(1, 0, 2).reshape(P, -1)


def blocks(shape, places):
    out = np.zeros(shape, np.float32)
    for r, c, m in places:
        out[r:r + m.shape[0], c:c + m.shape[1]] = m
    return out


def constants():
    eye = np.eye(P, dtype=np.float32)
    k, q = np.meshgrid(np.arange(P), np.arange(P), indexing="ij")
    bf = {"ident": eye, "mask_qk": np.where(q > k, MASKED, 0.0), "mask_kq": np.where(k > q, MASKED, 0.0)}
    for name, off in (("pick_b", 0), ("pick_c", 16)):
        t = np.zeros((P, 16, P))
        for n in range(16):
            t[[off + n, 32 + off + n, 64 + off + n], n, :] = 1.0
        bf[name] = t.reshape(P, -1)
    for name, experts, width, tiles in (("route0", 8, 176, 14), ("route1", 16, 64, 9)):
        t = np.zeros((P, tiles * P))
        for unit in range(tiles * P):
            e = unit // width
            t[[e, 32 + e, 64 + e] if e < experts else [96], unit] = 1.0
        bf[name] = t
    bf["ones3"] = blocks((P, P), [(r, 0, np.ones((1, P))) for r in (0, 32, 64)])
    f = {"mean_of": np.full((P, P), 1.0 / P), "ident": eye, "ones": np.ones((P, P)),
         "causal": np.concatenate([k <= q, np.ones((P, CHUNK - P))], axis=1), "same8": (k // 8 == q // 8), "same64": (k // 64 == q // 64), "mod32": (k % 32 == q % 32),
         "pair_of": (np.arange(P)[:, None] // 16 == np.arange(8)[None, :]),
         "iota": np.broadcast_to(np.arange(16.0), (P, 16)), "eps5": np.full((P, 1), 1e-5), "eps4": np.full((P, 1), 1e-4),
         "minus": -eye, "one": np.ones((P, 1)), "eps6": np.full((P, 1), 1e-6),
         "centre": eye - 1.0 / P, "is_rest": np.arange(P)[:, None] % 8 >= 4, "own_row": np.arange(P)[:, None] % 4 == np.arange(4)[None, :]}
    as32 = lambda d: [(n, np.asarray(a, np.float32)) for n, a in d.items()]
    return as32(bf), as32(f)


def rotary():
    inv = (1.0 / 10000.0 ** (np.arange(0, 32, 2, dtype=np.float32) / np.float32(32))).astype(np.float32)
    angle = np.outer(np.repeat(inv, 2), np.arange(TIME, dtype=np.float32)).astype(np.float32)
    sign = np.where(np.arange(32) % 2 == 0, -1.0, 1.0)[:, None]
    return np.tile(np.cos(angle), (4, 1)), np.tile(sign * np.sin(angle), (4, 1))


def weight_parts(a):
    cos, sin = rotary()
    parts = {}

    def heads_to_latent(m):
        return np.concatenate([blocks((P, P), [(8 * (4 * grp + j), 32 * j, m.T) for j in range(4)])
                               for grp in range(4)], axis=1)

    def four(v):
        return np.tile(v, 4)[:, None]

    n = "L0_attn_a_"
    swapped = np.arange(32) ^ 1
    parts["l0a"] = [
        ("wqkv", a[n + "c_attn_w"].T), ("bqkv", columns(a[n + "c_attn_b"])),
        ("q2l", heads_to_latent(a[n + "q2l_w"])), ("kv2l", heads_to_latent(a[n + "kv2l_w"])),
        ("q2l_s", heads_to_latent(a[n + "q2l_w"][swapped])), ("kv2l_s", heads_to_latent(a[n + "kv2l_w"][swapped])),
        ("q2l_b", four(a[n + "q2l_b"])), ("kv2l_b", four(a[n + "kv2l_b"])),
        ("q2l_b_s", four(a[n + "q2l_b"][swapped])), ("kv2l_b_s", four(a[n + "kv2l_b"][swapped])),
        ("wqk", blocks((P, P), [(32 * j, 32 * j, a[n + "wqk_w"].T) for j in range(4)])),
        ("wqk_b", four(a[n + "wqk_b"])),
        ("l2o", blocks((P, 32), [(32 * j, 8 * j, a[n + "l2o_w"].T) for j in range(4)])),
        ("l2o_b", np.broadcast_to(a[n + "l2o_b"], (P, 8))),
        ("cproj", a[n + "cproj_w"].T), ("cproj_b", columns(a[n + "cproj_b"])),
        ("cos", cos), ("sin", sin),
    ]
    n = "L0_ffn_"

    def hidden(m):
        return m.transpose(1, 0, 2).reshape(P, -1)

    def down(*ms):
        m = np.concatenate(ms, axis=0)
        return beside(blocks((-(-len(m) // P) * P, m.shape[1]), [(0, 0, m)]))

    def filled(*ms):
        m = np.concatenate(ms, axis=1)
        return blocks((P, -(-m.shape[1] // P) * P), [(0, 0, m)])

    parts["l0f"] = [("router", a[n + "Wg"]), ("gate", filled(hidden(a[n + "W1"]), a[n + "Ws1"])),
                    ("up", filled(hidden(a[n + "W2"]), a[n + "Ws2"])),
                    ("down", down(a[n + "W3"].reshape(-1, P), a[n + "Ws3"]))]
    n = "L0_attn_b_"
    parts["l0b"] = [("wqkv", a[n + "w_qkv"].T), ("wfc", a[n + "w_fc"].T), ("b_fc", columns(a[n + "b_fc"])),
                    ("gamma", columns(a[n + "gamma"])), ("beta", columns(a[n + "beta"]))]
    n = "L1_ffn_"
    units = lambda m: m.reshape(-1, P).T
    parts["l1f"] = [("router", a[n + "router_weight"].T), ("e_bias", np.broadcast_to(a[n + "e_bias"], (P, 16))),
                    ("gate", filled(units(a[n + "gate_w"]), a[n + "sh_gate_w"].T)),
                    ("up", filled(units(a[n + "up_w"]), a[n + "sh_up_w"].T)),
                    ("down", down(a[n + "down_w"].transpose(0, 2, 1).reshape(-1, P), a[n + "sh_down_w"].T))]
    n = "L1_attn_a_"
    c_own = np.concatenate([blocks((P, P), [(64 * s, 8 * (2 * p + s), a[n + "c"][2 * p + s]) for s in range(2)])
                            for p in range(8)], axis=1)
    a_two = np.concatenate([blocks((P, P), [(64 * s, 64 * s, a[n + "a"][2 * p + s]) for s in range(2)]) for p in range(8)], axis=1)
    b_two = blocks((P, P), [(8 * h, 64 * (h % 2), a[n + "b"][h]) for h in range(16)])
    parts["l1a"] = [("a", a_two), ("b", b_two),
                    ("c", c_own), ("norm_w", columns(a[n + "norm_w"])), ("skip", a[n + "skip"].reshape(P, 1)),
                    ("out", a[n + "w_out"].T), ("b_out", columns(a[n + "b_out"]))]
    n = "L1_attn_b_"
    parts["l1b"] = [("wqkv", a[n + "Wqkv"].T), ("bqkv", columns(a[n + "bqkv"])), ("wproj", a[n + "Wproj"].T),
                    ("bproj", columns(a[n + "bproj"])), ("scale", np.broadcast_to(a[n + "scale"], (P, 1)))]
    n = "L2_ffn_"
    parts["l2f"] = [("w1", a[n + "w1_w"].T), ("w2", a[n + "w2_w"].T), ("h1", beside(a[n + "h1_w"].T)),
                    ("h2", beside(a[n + "h2_w"].T)), ("w3", beside(a[n + "w3_w"].T)), ("s1", columns(a[n + "w1_s"])),
                    ("s2", columns(a[n + "w2_s"])), ("sh1", columns(a[n + "h1_s"])), ("sh2", columns(a[n + "h2_s"])),
                    ("s3", columns(a[n + "w3_s"]))]

    def scan_parts(n, ranks, names):
        def halves(m):
            return beside(m)
        out = [("in", a[n + "in_proj_w"].T), ("conv", halves(a[n + "conv_w"].reshape(256, 4))),
               ("conv_b", columns(a[n + "conv_b"])), ("out", beside(a[n + "out_proj_w"].T))]
        for r, (rank, (xp, dtw, dtb, alog, d)) in enumerate(zip(ranks, names)):
            x = a[n + xp].T
            out += [(f"xdt{r}", halves(x[:, :rank])), (f"xbc{r}", halves(x[:, rank:])), (f"dtw{r}", a[n + dtw].T),
                    (f"dtb{r}", columns(a[n + dtb])), (f"alog{r}", halves(a[n + alog])), (f"d{r}", columns(a[n + d]))]
        return out

    parts["l2a"] = scan_parts("L2_attn_a_", [64], [("x_proj_w", "dt_proj_w", "dt_proj_b", "A_log", "D")])
    parts["l2b"] = scan_parts("L2_attn_b_", [8, 8], [(f"x{i}_proj_w", f"dt{i}_proj_w", f"dt{i}_proj_b", f"A{i}_log", f"D{i}")
                                                     for i in (1, 2)])
    n = "L3_attn_a_"
    parts["l3a"] = [("wqk", np.concatenate([a[n + "Wq"].T, a[n + "Wk"].T], axis=1)), ("wv", a[n + "Wv"].T),
                    ("wo", beside(a[n + "Wo"].T))]
    n = "L3_attn_b_"
    parts["l3b"] = [("wkvr", np.concatenate([a[n + "Wk"].T, a[n + "Wv"].T, a[n + "Wr"].T], axis=1)), ("wo", a[n + "Wo"].T),
                    ("decay", columns(a[n + "time_decay"])), ("first", columns(a[n + "time_first"]))]
    n = "L3_ffn_"
    of_expert = blocks((64, 2048), [(e, 32 * e, np.ones((1, 32))) for e in range(64)])
    parts["l3f"] = [("phi", a[n + "phi_w"].T), ("phi_b", blocks((96, 2048), [(r, 0, a[n + "phi_b"][None, :]) for r in (0, 32, 64)])), ("phi_bc", columns(a[n + "phi_b"])),
                    ("expert_w", a[n + "expert_w"].transpose(1, 0, 2).reshape(P, -1)), ("expert_b", a[n + "expert_b"]),
                    ("of_expert", of_expert)]
    return parts


def build(nc, args, places, first=0, last=99):
    g = Core(nc)
    with ExitStack() as ctx:
        def sb(name, shape, dtype=F32):
            return ctx.enter_context(nc.sbuf_tensor(name, shape, dtype))

        g.resid = sb("resid", [P, TOKENS])
        g.normed = sb("normed", [P, TOKENS])
        g.mark = sb("mark", [P, 1])[:, :]
        g.mark2 = sb("mark2", [P, 2])
        psum = ctx.enter_context(nc.psum_tensor("psum", [P, 8, CHUNK], F32))
        g.bank = [psum[:, i, :] for i in range(8)]
        g.banks = Banks(psum)
        g.loaded, g.w = {}, {}
        widths = {k: sum(c for _, _, c in v.values()) for k, v in places.items()}
        def place_weights(blocks, sb):
            for k in blocks:
                tensors[k] = sb(f"w_{k}", [P, widths[k]])[:, :]
                g.w[k] = {name: tensors[k][0:r, o:o + c] for name, (r, o, c) in places[k].items()}
                g.loaded[k] = nc.alloc_semaphore(f"loaded_{k}")

        tensors = {}
        place_weights(("c32", "l2a", "l3a"), sb)
        bf = sb("c_bf", [P, widths["cbf"]], BF16)
        cbf = {name: bf[0:r, o:o + c] for name, (r, o, c) in places["cbf"].items()}
        c32 = g.w["c32"]
        g.ident_bf, g.mask_qk, g.mask_kq, g.ones3 = (cbf[n] for n in ("ident", "mask_qk", "mask_kq", "ones3"))
        g.pick_b, g.pick_c, g.route0, g.route1 = (cbf[n].rearrange("p (n m) -> p n m", m=P)
                                                  for n in ("pick_b", "pick_c", "route0", "route1"))
        (g.mean_of, g.ident, g.ones, g.causal, g.same8, g.same64, g.mod32, g.pair_of, g.iota, g.eps5, g.eps4, g.minus,
         g.one, g.eps6, g.is_rest, g.own_row, g.centre) = (
            c32[n] for n in ("mean_of", "ident", "ones", "causal", "same8", "same64", "mod32", "pair_of", "iota", "eps5",
                             "eps4", "minus", "one", "eps6", "is_rest", "own_row", "centre"))
        g.ones_row = g.ones[0:1, :]
        x_loaded = nc.alloc_semaphore("x_loaded")

        with stage(g, "table_loaded table_cast") as (sbs, (table_loaded, table_cast)):
            wide = sbs("c_wide", [P, widths["cbf"]])
            with nc.Block() as block:
                @block.sync
                def _(sp):
                    sp.dma_start(g.resid[:, :], args["x"]).then_inc(x_loaded, 16)
                    sp.dma_start(tensors["c32"], args["c32"]).then_inc(g.loaded["c32"], 16)
                    sp.dma_start(wide[:, :], args["cbf"]).then_inc(table_loaded, 16)
                    sp.wait_ge(x_loaded, 16)
                    sp.wait_ge(g.loaded["c32"], 16)

                @block.vector
                def _(dve):
                    dve.wait_ge(table_loaded, 16)
                    nc.vector.tensor_copy(bf[:, :], wide[:, :]).then_inc(table_cast, 1)

        def load(blocks):
            with nc.Block() as block:
                @block.sync
                def _(sp):
                    for k in blocks:
                        sp.dma_start(tensors[k], args[k]).then_inc(g.loaded[k], 16)

        def loaded(blocks):
            with nc.Block() as block:
                @block.sync
                def _(sp):
                    for k in blocks:
                        sp.wait_ge(g.loaded[k], 16)

        layers = [latent_attention, top_two_experts, plain_attention, top_two_experts, recurrent_heads, grouped_experts,
                  cumulative_attention, grouped_experts, selective_scan_one, dense_ffn, selective_scan_two, dense_ffn,
                  unit_attention, soft_experts, decayed_sum, soft_experts]
        for part, blocks in ((slice(0, 1), ("l0a", "l2a", "l3a")), (slice(1, 4), ("l0f", "l0b")),
                             (slice(4, 8), ("l1a", "l1f", "l1b")),
                             (slice(8, 12), ("l2f", "l2b")), (slice(12, 16), ("l3f", "l3b"))):
            with ExitStack() as turn:
                place_weights([k for k in blocks if k not in tensors],
                              lambda name, shape: turn.enter_context(nc.sbuf_tensor(name, shape, F32)))
                load(blocks)
                for i, layer in list(enumerate(layers))[part]:
                    if first <= i < last:
                        layernorm(g)
                        layer(g)
                loaded(blocks)
                nc.all_engine_barrier()
        out_stored = nc.alloc_semaphore("out_stored")
        with nc.Block() as block:
            @block.sync
            def _(sp):
                sp.dma_start(args["out"], g.resid[:, :]).then_inc(out_stored, 16)
                sp.wait_ge(out_stored, 16)


class Banks:

    def __init__(self, psum):
        self.psum = psum

    def __getitem__(self, at):
        return self.psum[:, at[0], at[1]]


def packed(inputs):
    cbf, c32 = constants()
    every = {"c32": c32, "cbf": cbf} | weight_parts(inputs)
    arrays, places = {}, {}
    for k, parts in every.items():
        rows, o, places[k] = [], 0, {}
        for name, m in parts:
            places[k][name] = (m.shape[0], o, m.shape[1])
            o += m.shape[1]
            rows.append(blocks((P, m.shape[1]), [(0, 0, m)]))
        arrays[k] = np.concatenate(rows, axis=1)
    return arrays, places


def kernel(**inputs):
    import numpy as _np
    import concourse.bacc as _bacc
    from concourse import mybir as _mybir
    from concourse.bass_utils import run_bass_kernel_spmd as _run

    inputs = {k: _np.asarray(v) for k, v in inputs.items()}
    arrays, places = packed(inputs)
    arrays["x"] = _np.ascontiguousarray(inputs["L0_attn_a_x"].reshape(TOKENS, P).T)
    nc = _bacc.Bacc("TRN2", target_bir_lowering=False, num_devices=1)
    args, sent = {}, {}
    for k, v in arrays.items():
        sent[f"in_{k}"] = v
        args[k] = nc.dram_tensor(f"in_{k}", v.shape, _mybir.dt.float32, kind="ExternalInput").ap()
    args["out"] = nc.dram_tensor("out_0", (P, TOKENS), _mybir.dt.float32, kind="ExternalOutput").ap()
    build(nc, args, places)
    r = _run(nc, [sent], core_ids=[0])
    out = r.results[0]["out_0"]
    return _np.ascontiguousarray(out.T).reshape(BATCH, TIME, P)
```
